# Optimizing a Trainium2 kernel written in Bass

```python
import numpy as np
import jax
import jax.numpy as jnp

def _softmax(x, axis=-1):
    return jax.nn.softmax(x, axis=axis)

def _gelu(x):
    return jax.nn.gelu(x, approximate=True)

def _silu(x):
    return jax.nn.silu(x)

def _sigmoid(x):
    return jax.nn.sigmoid(x)

def _layernorm(x, axis=-1, eps=1e-05):
    m = jnp.mean(x, axis=axis, keepdims=True)
    v = jnp.var(x, axis=axis, keepdims=True)
    return (x - m) / jnp.sqrt(v + eps)

def _scatter_add(tgt, idx, src, axis=0):
    return tgt.at[idx].add(src)

def _segment_sum(src, seg, n):
    return jax.ops.segment_sum(src, seg, n)
kernel_name = 'mk_gps_d2_gnn_r8_b2960b'

def setup_inputs(seed: int=0):
    np.random.seed(seed)
    _w = jnp.asarray

    def _rec_inputs():
        import jax
        import jax.numpy as jnp
        _gk = jax.random.key(seed)
        x = -0.0006008 + 1.001 * jax.random.normal(jax.random.fold_in(_gk, 1), (6250, 256), jnp.float32)
        _s = jax.random.randint(jax.random.fold_in(_gk, 2), (50000,), 0, 6250, jnp.int32)
        _d = jax.random.randint(jax.random.fold_in(_gk, 3), (50000,), 0, 6250, jnp.int32)
        _loop = jnp.arange(6250, dtype=jnp.int32)
        src = jnp.concatenate([_s, _d, _loop])
        dst = jnp.concatenate([_d, _s, _loop])
        _o = jnp.argsort(dst, stable=True)
        src = src[_o]
        dst = dst[_o]
        return (x, src, dst)
    x, src, dst = _rec_inputs()

    def _L0_gnn_setup():
        import jax, jax.numpy as jnp
        import numpy as np
        N_NODES = 1250
        N_EDGES = 40000
        C = 256

        def gcn_conv(x, edge_index, W, b, num_nodes):
            src = edge_index[0]
            dst = edge_index[1]
            loop = jnp.arange(num_nodes, dtype=edge_index.dtype)
            src = jnp.concatenate([src, loop])
            dst = jnp.concatenate([dst, loop])
            ones = jnp.ones(src.shape[0], dtype=x.dtype)
            deg = jax.ops.segment_sum(ones, dst, num_segments=num_nodes)
            dinv = jnp.where(deg > 0, jax.lax.rsqrt(deg), 0.0)
            norm = dinv[src] * dinv[dst]
            h = x @ W
            msg = h[src] * norm[:, None]
            out = jax.ops.segment_sum(msg, dst, num_segments=num_nodes)
            return out + b

        def gcn_block(x, edge_index, W, b, num_nodes):
            z = gcn_conv(x, edge_index, W, b, num_nodes)
            z = jax.nn.relu(z)
            return x + z
        key = jax.random.key(seed)
        k1, k2, k3, k4 = jax.random.split(key, 4)
        x = jax.random.normal(k1, (N_NODES, C), dtype=jnp.float32)
        edge_index = jax.random.randint(k2, (2, N_EDGES), 0, N_NODES, dtype=jnp.int64)
        s = 1.0 / np.sqrt(C)
        W1 = jax.random.uniform(k3, (C, C), jnp.float32, -s, s)
        b1 = jnp.zeros((C,), jnp.float32)
        W2 = jax.random.uniform(k4, (C, C), jnp.float32, -s, s)
        b2 = jnp.zeros((C,), jnp.float32)
        return {'x': x, 'edge_index': edge_index, 'W1': W1, 'b1': b1, 'W2': W2, 'b2': b2}
    _L0_gnn_all = _L0_gnn_setup()
    _L0_gnn_in = {k: v for k, v in _L0_gnn_all.items() if k in ('W1', 'b1', 'W2', 'b2')}
    del _L0_gnn_all

    def _L0_mix_setup():
        import jax, jax.numpy as jnp
        import numpy as np
        HEADS = 4
        DIM_HEAD = 32
        key = jax.random.key(seed)
        k1, k2, k3 = jax.random.split(key, 3)
        B, L, D = (16, 1024, 256)
        hidden = HEADS * DIM_HEAD
        x = jax.random.normal(k1, (B, L, D), dtype=jnp.float32)
        W_qkv = jax.random.normal(k2, (D, 3 * hidden), dtype=jnp.float32) * D ** (-0.5)
        W_out = jax.random.normal(k3, (hidden, D), dtype=jnp.float32) * hidden ** (-0.5)
        b_out = jnp.zeros((D,), dtype=jnp.float32)
        return {'x': x, 'W_qkv': W_qkv, 'W_out': W_out, 'b_out': b_out}
    _L0_mix_all = _L0_mix_setup()
    _L0_mix_in = {k: v for k, v in _L0_mix_all.items() if k in ('W_qkv', 'W_out', 'b_out')}
    del _L0_mix_all

    def _L0_ffn_setup():
        import jax, jax.numpy as jnp
        import numpy as np
        C = 256
        HID = 1024
        E = 8
        TEMP = 1.0
        key = jax.random.key(seed)
        ks = jax.random.split(key, 7)
        x = jax.random.normal(ks[0], (8, 2048, C), dtype=jnp.float32)
        W1 = jax.random.normal(ks[1], (C, HID), dtype=jnp.float32) * 0.02
        b1 = jnp.zeros((HID,), dtype=jnp.float32)
        Wg = jax.random.normal(ks[2], (HID, E), dtype=jnp.float32) * 0.02
        bg = jnp.zeros((E,), dtype=jnp.float32)
        Wd = jax.random.normal(ks[3], (E, HID, C), dtype=jnp.float32) * 0.02
        bd = jnp.zeros((E, C), dtype=jnp.float32)
        return {'x': x, 'W1': W1, 'b1': b1, 'Wg': Wg, 'bg': bg, 'Wd': Wd, 'bd': bd}
    _L0_ffn_all = _L0_ffn_setup()
    _L0_ffn_in = {k: v for k, v in _L0_ffn_all.items() if k in ('W1', 'b1', 'Wg', 'bg', 'Wd', 'bd')}
    del _L0_ffn_all

    def _L1_gnn_setup():
        import jax, jax.numpy as jnp
        import numpy as np
        N_NODES = 6250
        N_EDGES = 100000
        D_IN = 256
        D_OUT = 256
        key = jax.random.key(seed)
        k_feat, k_src, k_dst, k_ws, k_wn, k_b = jax.random.split(key, 6)
        feat = jax.random.normal(k_feat, (N_NODES, D_IN), dtype=jnp.float32)
        src = jax.random.randint(k_src, (N_EDGES,), 0, N_NODES)
        dst = jax.random.randint(k_dst, (N_EDGES,), 0, N_NODES)
        scale = 1.0 / np.sqrt(D_IN)
        W_self = jax.random.normal(k_ws, (D_IN, D_OUT), dtype=jnp.float32) * scale
        W_neigh = jax.random.normal(k_wn, (D_IN, D_OUT), dtype=jnp.float32) * scale
        b = jnp.zeros((D_OUT,), dtype=jnp.float32)
        return {'feat': feat, 'W_self': W_self, 'W_neigh': W_neigh, 'b': b, 'src': src, 'dst': dst}
    _L1_gnn_all = _L1_gnn_setup()
    _L1_gnn_in = {k: v for k, v in _L1_gnn_all.items() if k in ('W_self', 'W_neigh', 'b')}
    del _L1_gnn_all

    def _L1_mix_setup():
        import jax, jax.numpy as jnp
        import numpy as np
        DIM = 256
        HEADS = 4
        HEAD_DIM = DIM // HEADS
        MLP_HIDDEN = DIM * 3
        B, N = (8, 512)
        EPS = 1e-05

        def _layernorm(x, g, b):
            mu = jnp.mean(x, axis=-1, keepdims=True)
            var = jnp.mean(jnp.square(x - mu), axis=-1, keepdims=True)
            return (x - mu) * jax.lax.rsqrt(var + EPS) * g + b
        key = jax.random.key(seed)
        ks = jax.random.split(key, 8)
        s = 0.02
        return {'x': jax.random.normal(ks[0], (B, N, DIM), dtype=jnp.float32), 'w_qkv': jax.random.normal(ks[1], (DIM, 3 * DIM), dtype=jnp.float32) * s, 'b_qkv': jnp.zeros((3 * DIM,), dtype=jnp.float32), 'norm_g': jnp.ones((DIM,), dtype=jnp.float32), 'norm_b': jnp.zeros((DIM,), dtype=jnp.float32), 'w_fc1': jax.random.normal(ks[2], (DIM, MLP_HIDDEN), dtype=jnp.float32) * s, 'b_fc1': jnp.zeros((MLP_HIDDEN,), dtype=jnp.float32), 'w_fc2': jax.random.normal(ks[3], (MLP_HIDDEN, DIM), dtype=jnp.float32) * s, 'b_fc2': jnp.zeros((DIM,), dtype=jnp.float32)}
    _L1_mix_all = _L1_mix_setup()
    _L1_mix_in = {k: v for k, v in _L1_mix_all.items() if k in ('w_qkv', 'b_qkv', 'norm_g', 'norm_b', 'w_fc1', 'b_fc1', 'w_fc2', 'b_fc2')}
    del _L1_mix_all

    def _L1_ffn_setup():
        import jax, jax.numpy as jnp
        import numpy as np
        B, A = (512, 8)
        IN, OUT = (256, 256)
        SH1, SH2 = (256, 128)
        EH1, EH2 = (128, 64)
        E, TOPK = (4, 2)

        def _shared_mlp(x, W1, b1, W2, b2, W3, b3):
            h = jax.nn.relu(x @ W1 + b1)
            h = jax.nn.relu(h @ W2 + b2)
            return h @ W3 + b3

        def _experts_mlp(x, eW1, eb1, eW2, eb2, eW3, eb3):
            h = jax.nn.relu(jnp.einsum('baf,efh->ebah', x, eW1) + eb1[:, None, None, :])
            h = jax.nn.relu(jnp.einsum('ebah,ehg->ebag', h, eW2) + eb2[:, None, None, :])
            o = jnp.einsum('ebag,ego->ebao', h, eW3) + eb3[:, None, None, :]
            return jnp.moveaxis(o, 0, -1)
        key = jax.random.key(seed)
        ks = jax.random.split(key, 16)
        s = 0.05
        return {'x': jax.random.normal(ks[0], (B, A, IN), jnp.float32), 'sW1': jax.random.normal(ks[1], (IN, SH1), jnp.float32) * s, 'sb1': jnp.zeros((SH1,), jnp.float32), 'sW2': jax.random.normal(ks[2], (SH1, SH2), jnp.float32) * s, 'sb2': jnp.zeros((SH2,), jnp.float32), 'sW3': jax.random.normal(ks[3], (SH2, OUT), jnp.float32) * s, 'sb3': jnp.zeros((OUT,), jnp.float32), 'eW1': jax.random.normal(ks[4], (E, IN, EH1), jnp.float32) * s, 'eb1': jnp.zeros((E, EH1), jnp.float32), 'eW2': jax.random.normal(ks[5], (E, EH1, EH2), jnp.float32) * s, 'eb2': jnp.zeros((E, EH2), jnp.float32), 'eW3': jax.random.normal(ks[6], (E, EH2, OUT), jnp.float32) * s, 'eb3': jnp.zeros((E, OUT), jnp.float32), 'gW': jax.random.normal(ks[7], (IN, E), jnp.float32) * s, 'gb': jnp.zeros((E,), jnp.float32)}
    _L1_ffn_all = _L1_ffn_setup()
    _L1_ffn_in = {k: v for k, v in _L1_ffn_all.items() if k in ('sW1', 'sb1', 'sW2', 'sb2', 'sW3', 'sb3', 'eW1', 'eb1', 'eW2', 'eb2', 'eW3', 'eb3', 'gW', 'gb')}
    del _L1_ffn_all
    return {'x': x, 'src': src, 'dst': dst, 'L0_gnn_W1': _L0_gnn_in['W1'], 'L0_gnn_b1': _L0_gnn_in['b1'], 'L0_gnn_W2': _L0_gnn_in['W2'], 'L0_gnn_b2': _L0_gnn_in['b2'], 'L0_mix_W_qkv': _L0_mix_in['W_qkv'], 'L0_mix_W_out': _L0_mix_in['W_out'], 'L0_mix_b_out': _L0_mix_in['b_out'], 'L0_ffn_W1': _L0_ffn_in['W1'], 'L0_ffn_b1': _L0_ffn_in['b1'], 'L0_ffn_Wg': _L0_ffn_in['Wg'], 'L0_ffn_bg': _L0_ffn_in['bg'], 'L0_ffn_Wd': _L0_ffn_in['Wd'], 'L0_ffn_bd': _L0_ffn_in['bd'], 'L1_gnn_W_self': _L1_gnn_in['W_self'], 'L1_gnn_W_neigh': _L1_gnn_in['W_neigh'], 'L1_gnn_b': _L1_gnn_in['b'], 'L1_mix_w_qkv': _L1_mix_in['w_qkv'], 'L1_mix_b_qkv': _L1_mix_in['b_qkv'], 'L1_mix_norm_g': _L1_mix_in['norm_g'], 'L1_mix_norm_b': _L1_mix_in['norm_b'], 'L1_mix_w_fc1': _L1_mix_in['w_fc1'], 'L1_mix_b_fc1': _L1_mix_in['b_fc1'], 'L1_mix_w_fc2': _L1_mix_in['w_fc2'], 'L1_mix_b_fc2': _L1_mix_in['b_fc2'], 'L1_ffn_sW1': _L1_ffn_in['sW1'], 'L1_ffn_sb1': _L1_ffn_in['sb1'], 'L1_ffn_sW2': _L1_ffn_in['sW2'], 'L1_ffn_sb2': _L1_ffn_in['sb2'], 'L1_ffn_sW3': _L1_ffn_in['sW3'], 'L1_ffn_sb3': _L1_ffn_in['sb3'], 'L1_ffn_eW1': _L1_ffn_in['eW1'], 'L1_ffn_eb1': _L1_ffn_in['eb1'], 'L1_ffn_eW2': _L1_ffn_in['eW2'], 'L1_ffn_eb2': _L1_ffn_in['eb2'], 'L1_ffn_eW3': _L1_ffn_in['eW3'], 'L1_ffn_eb3': _L1_ffn_in['eb3'], 'L1_ffn_gW': _L1_ffn_in['gW'], 'L1_ffn_gb': _L1_ffn_in['gb']}

def reference(x, src, dst, L0_gnn_W1, L0_gnn_b1, L0_gnn_W2, L0_gnn_b2, L0_mix_W_qkv, L0_mix_W_out, L0_mix_b_out, L0_ffn_W1, L0_ffn_b1, L0_ffn_Wg, L0_ffn_bg, L0_ffn_Wd, L0_ffn_bd, L1_gnn_W_self, L1_gnn_W_neigh, L1_gnn_b, L1_mix_w_qkv, L1_mix_b_qkv, L1_mix_norm_g, L1_mix_norm_b, L1_mix_w_fc1, L1_mix_b_fc1, L1_mix_w_fc2, L1_mix_b_fc2, L1_ffn_sW1, L1_ffn_sb1, L1_ffn_sW2, L1_ffn_sb2, L1_ffn_sW3, L1_ffn_sb3, L1_ffn_eW1, L1_ffn_eb1, L1_ffn_eW2, L1_ffn_eb2, L1_ffn_eW3, L1_ffn_eb3, L1_ffn_gW, L1_ffn_gb):
    import jax
    import jax.numpy as jnp

    def _L0_gnn_ref(x, edge_index, W1, b1, W2, b2):
        import jax, jax.numpy as jnp
        import numpy as np
        N_NODES = 1250
        N_EDGES = 40000
        C = 256

        def gcn_conv(x, edge_index, W, b, num_nodes):
            src = edge_index[0]
            dst = edge_index[1]
            loop = jnp.arange(num_nodes, dtype=edge_index.dtype)
            src = jnp.concatenate([src, loop])
            dst = jnp.concatenate([dst, loop])
            ones = jnp.ones(src.shape[0], dtype=x.dtype)
            deg = jax.ops.segment_sum(ones, dst, num_segments=num_nodes)
            dinv = jnp.where(deg > 0, jax.lax.rsqrt(deg), 0.0)
            norm = dinv[src] * dinv[dst]
            h = x @ W
            msg = h[src] * norm[:, None]
            out = jax.ops.segment_sum(msg, dst, num_segments=num_nodes)
            return out + b

        def gcn_block(x, edge_index, W, b, num_nodes):
            z = gcn_conv(x, edge_index, W, b, num_nodes)
            z = jax.nn.relu(z)
            return x + z
        n = x.shape[0]
        x = gcn_block(x, edge_index, W1, b1, n)
        x = gcn_block(x, edge_index, W2, b2, n)
        return x

    def _L0_mix_ref(x, W_qkv, W_out, b_out):
        import jax, jax.numpy as jnp
        import numpy as np
        HEADS = 4
        DIM_HEAD = 32
        B, L, D = x.shape
        scale = DIM_HEAD ** (-0.5)
        qkv = jnp.einsum('bld,df->blf', x, W_qkv)
        qkv = qkv.reshape(B, L, 3, HEADS, DIM_HEAD)
        q = jnp.transpose(qkv[:, :, 0], (0, 2, 1, 3)) * scale
        k = jax.nn.softmax(jnp.transpose(qkv[:, :, 1], (0, 2, 1, 3)), axis=2)
        v = jnp.transpose(qkv[:, :, 2], (0, 2, 1, 3))
        context = jnp.einsum('bhld,bhle->bhde', k, v)
        out = jnp.einsum('bhde,bhld->bhle', context, q)
        out = jnp.transpose(out, (0, 2, 1, 3)).reshape(B, L, HEADS * DIM_HEAD)
        return jnp.einsum('blf,fd->bld', out, W_out) + b_out

    def _L0_ffn_ref(x, W1, b1, Wg, bg, Wd, bd):
        import jax, jax.numpy as jnp
        import numpy as np
        C = 256
        HID = 1024
        E = 8
        TEMP = 1.0
        orig_shape = x.shape
        xf = x.reshape(-1, orig_shape[-1])
        H = jax.nn.gelu(xf @ W1 + b1, approximate=False)
        probs = jax.nn.softmax((H @ Wg + bg) / TEMP, axis=-1)
        assign = jnp.argmax(probs, axis=-1)
        out = jnp.zeros_like(xf)
        for e in range(Wd.shape[0]):
            y = H @ Wd[e] + bd[e]
            sel = (assign == e)[:, None]
            out = out + jnp.where(sel, probs[:, e:e + 1] * y, 0.0)
        return out.reshape(orig_shape)

    def _L1_gnn_ref(feat, W_self, W_neigh, b, src, dst):
        import jax, jax.numpy as jnp
        import numpy as np
        N_NODES = 6250
        N_EDGES = 100000
        D_IN = 256
        D_OUT = 256
        n = feat.shape[0]
        msg = feat[src]
        agg = jax.ops.segment_sum(msg, dst, num_segments=n)
        deg = jax.ops.segment_sum(jnp.ones_like(dst, dtype=feat.dtype), dst, num_segments=n)
        h_neigh = agg / jnp.maximum(deg, 1.0)[:, None]
        out = feat @ W_self + h_neigh @ W_neigh + b
        return out

    def _L1_mix_ref(x, w_qkv, b_qkv, norm_g, norm_b, w_fc1, b_fc1, w_fc2, b_fc2):
        import jax, jax.numpy as jnp
        import numpy as np
        DIM = 256
        HEADS = 4
        HEAD_DIM = DIM // HEADS
        MLP_HIDDEN = DIM * 3
        B, N = (8, 512)
        EPS = 1e-05

        def _layernorm(x, g, b):
            mu = jnp.mean(x, axis=-1, keepdims=True)
            var = jnp.mean(jnp.square(x - mu), axis=-1, keepdims=True)
            return (x - mu) * jax.lax.rsqrt(var + EPS) * g + b
        Bx, Nx, C = x.shape
        scale = HEAD_DIM ** (-0.5)
        qkv = (x @ w_qkv + b_qkv).reshape(Bx, Nx, 3, HEADS, HEAD_DIM)
        qkv = jnp.transpose(qkv, (2, 0, 3, 1, 4))
        q, k, v = (qkv[0], qkv[1], qkv[2])
        k = k * scale
        attn = jnp.einsum('bhnd,bhne->bhde', k, v)
        attn = jax.nn.softmax(attn, axis=-1)
        xf = jnp.einsum('bhde,bhne->bhnd', attn, q)
        xf = jnp.transpose(xf, (0, 2, 1, 3)).reshape(Bx, Nx, C)
        x = x + xf
        h = _layernorm(x, norm_g, norm_b)
        h = jax.nn.gelu(h @ w_fc1 + b_fc1, approximate=False) @ w_fc2 + b_fc2
        return x + h

    def _L1_ffn_ref(x, sW1, sb1, sW2, sb2, sW3, sb3, eW1, eb1, eW2, eb2, eW3, eb3, gW, gb):
        import jax, jax.numpy as jnp
        import numpy as np
        B, A = (512, 8)
        IN, OUT = (256, 256)
        SH1, SH2 = (256, 128)
        EH1, EH2 = (128, 64)
        E, TOPK = (4, 2)

        def _shared_mlp(x, W1, b1, W2, b2, W3, b3):
            h = jax.nn.relu(x @ W1 + b1)
            h = jax.nn.relu(h @ W2 + b2)
            return h @ W3 + b3

        def _experts_mlp(x, eW1, eb1, eW2, eb2, eW3, eb3):
            h = jax.nn.relu(jnp.einsum('baf,efh->ebah', x, eW1) + eb1[:, None, None, :])
            h = jax.nn.relu(jnp.einsum('ebah,ehg->ebag', h, eW2) + eb2[:, None, None, :])
            o = jnp.einsum('ebag,ego->ebao', h, eW3) + eb3[:, None, None, :]
            return jnp.moveaxis(o, 0, -1)
        all_out = _experts_mlp(x, eW1, eb1, eW2, eb2, eW3, eb3)
        shared = _shared_mlp(x, sW1, sb1, sW2, sb2, sW3, sb3)
        gates = jax.nn.softmax(x @ gW + gb, axis=-1)
        topv, topi = jax.lax.top_k(gates, TOPK)
        topw = jax.nn.softmax(topv, axis=-1)
        sel = jnp.take_along_axis(all_out, topi[:, :, None, :], axis=-1)
        gated = jnp.sum(sel * topw[:, :, None, :], axis=-1)
        return shared + gated
    edge_index = jnp.stack([src, dst])
    xn = _layernorm(x, axis=-1)
    x = x + _L0_gnn_ref(xn, edge_index, L0_gnn_W1, L0_gnn_b1, L0_gnn_W2, L0_gnn_b2) + _L0_mix_ref(xn[None], L0_mix_W_qkv, L0_mix_W_out, L0_mix_b_out)[0]
    x = x + _L0_ffn_ref(_layernorm(x, axis=-1)[None], L0_ffn_W1, L0_ffn_b1, L0_ffn_Wg, L0_ffn_bg, L0_ffn_Wd, L0_ffn_bd)[0]
    xn = _layernorm(x, axis=-1)
    x = x + _L1_gnn_ref(xn, L1_gnn_W_self, L1_gnn_W_neigh, L1_gnn_b, src, dst) + _L1_mix_ref(xn[None], L1_mix_w_qkv, L1_mix_b_qkv, L1_mix_norm_g, L1_mix_norm_b, L1_mix_w_fc1, L1_mix_b_fc1, L1_mix_w_fc2, L1_mix_b_fc2)[0]
    x = x + _L1_ffn_ref(_layernorm(x, axis=-1)[None], L1_ffn_sW1, L1_ffn_sb1, L1_ffn_sW2, L1_ffn_sb2, L1_ffn_sW3, L1_ffn_sb3, L1_ffn_eW1, L1_ffn_eb1, L1_ffn_eW2, L1_ffn_eb2, L1_ffn_eW3, L1_ffn_eb3, L1_ffn_gW, L1_ffn_gb)[0]
    return x

_drawn_inputs = setup_inputs


def setup_inputs(seed=0):
    import zlib

    import numpy as np

    out = dict(_drawn_inputs(seed))
    spreads = {'L0_gnn_b1': (0.0, 0.1),
     'L0_gnn_b2': (0.0, 0.1),
     'L0_mix_b_out': (0.0, 0.1),
     'L0_ffn_b1': (0.0, 0.8),
     'L0_ffn_bg': (0.0, 0.769),
     'L0_ffn_bd': (0.0, 0.8),
     'L1_gnn_b': (0.0, 0.1),
     'L1_mix_b_qkv': (0.0, 0.1),
     'L1_mix_norm_g': (1.0, 0.6),
     'L1_mix_norm_b': (0.0, 0.8),
     'L1_mix_b_fc1': (0.0, 0.795),
     'L1_mix_b_fc2': (0.0, 0.275),
     'L1_ffn_sb1': (0.0, 2.0),
     'L1_ffn_sb2': (0.0, 0.674),
     'L1_ffn_sb3': (0.0, 0.512),
     'L1_ffn_eb1': (0.0, 0.8),
     'L1_ffn_eb2': (0.0, 0.8),
     'L1_ffn_eb3': (0.0, 0.37),
     'L1_ffn_gb': (0.0, 0.8)}
    factors = {'L0_ffn_W1': 5.24,
     'L0_ffn_Wg': 5.617,
     'L0_ffn_Wd': 6.364,
     'L1_ffn_eW1': 4.067,
     'L1_ffn_eW2': 3.572,
     'L1_ffn_eW3': 2.8}
    for name, (base, spread) in spreads.items():
        noise = np.random.default_rng([zlib.crc32(name.encode()), seed]).standard_normal(out[name].shape)
        drawn = base * np.exp(spread * noise) if base else spread * noise
        out[name] = jnp.asarray(drawn.astype(out[name].dtype))
    for name, factor in factors.items():
        out[name] = (out[name] * factor).astype(out[name].dtype)
    return out
```

```python
from contextlib import ExitStack

import concourse.bass as bass
from concourse import mybir

F32 = mybir.dt.float32
BF16 = mybir.dt.bfloat16
I32 = mybir.dt.int32
ALU = mybir.AluOpType
ACT = mybir.ActivationFunctionType
AX = mybir.AxisListType

P = 128
N = 6250
D = 256
E = 106250
T = -(-N // P)
LAST = N - (T - 1) * P
CH = -(-E // P)
CHR = 896
KC = CHR // P
PAD_DST = 8191
RING = 16
VIS = -(-(CH + T - 1) // RING) * RING
VI = VIS // RING
VC = CHR // P
HID = 1024
NE = 8
HC = HID // P
EPS = 1e-5
MAGIC = 1597463007.0


class Chain:

    def __init__(self, eng, sem, per=0):
        self.eng, self.sem, self.per, self.base, self.k = eng, sem, per, 0, 0

    def tile(self, t):
        assert self.k in (0, self.per)
        self.base, self.k = t * self.per, 0
        return self

    def __call__(self, ins):
        self.k += 1
        ins.then_inc(self.sem, 1)
        self.eng.wait_ge(self.sem, self.base + self.k)


class Step:

    def __init__(self, sem, depth=2):
        self.sem, self.depth = sem, depth

    def after(self, t):
        return self.sem, t + 1 + self.depth

    def room(self, t):
        return self.sem, t + 1


def tiles(eng, *parts):
    def turn(t, parity):
        for part, lag in parts:
            if not isinstance(t, int) or 0 <= t - lag < T:
                part(t - lag, (parity + lag) % 2)

    for t in range(3):
        turn(t, t % 2)
    with eng.Fori(0, (T - 5) // 2) as i:
        turn(2 * i + 3, 1)
        turn(2 * i + 4, 0)
    for t in range(T - 2, T + max(lag for _, lag in parts)):
        turn(t, t % 2)


def build(nc, A, out):
    with ExitStack() as ctx:
        def sb(name, shape, dt=F32):
            return ctx.enter_context(nc.sbuf_tensor(name, shape, dt))

        stage_sems = []

        def sem(name, keep=False):
            s = nc.alloc_semaphore(name=name)
            if not keep:
                stage_sems.append(s)
            return s

        def retire_sems():
            nc.clear_and_free_semaphores(list(stage_sems))
            nc.all_engine_barrier()
            stage_sems.clear()

        def dram(name, shape, dt=F32):
            return nc.dram_tensor(name, shape, dt, kind="Internal").ap()

        XN = sb("XN", [P, T * D])
        AR = sb("AR", [P, T * D + T * (D + 1)])
        ACC = AR[:, 0:T * D]
        KV = AR[:, T * D:T * (2 * D + 1)].rearrange("p (t c) -> p t c", c=D + 1)
        KVf = AR[:, T * D:T * (2 * D + 1)]
        R = AR[:, T * D:2 * T * D]
        WD = AR[:, 0:NE * HC * D]
        rows = sb("rows", [P, RING * D])
        wreg = sb("wreg", [P, 3600])
        work = sb("work", [P, 2048])
        mring = sb("mring", [P, 4 * P])
        idx_stage = sb("idx_stage", [P, RING], I32)
        src_idx = sb("src_idx", [P, CHR], I32)
        dst_rel = sb("dst_rel", [P, CHR])
        acc_at = sb("acc_at", [1, CHR], I32)
        ident = sb("ident", [P, P])
        iota = sb("iota", [P, P])
        bias_rows = sb("bias_rows", [P, 2 * D])
        stats = sb("stats", [P, 6])
        mv = sb("mv", [P, T, 6])
        rstd = sb("rstd", [P, T])
        nmr = sb("nmr", [P, T])
        dinv = sb("dinv", [P, T])
        invdeg = sb("invdeg", [P, T])
        deg = sb("deg", [P, T])
        newton = sb("newton", [P, 2 * T])
        gate = sb("gate", [P, T * NE])
        gtmp = sb("gtmp", [P, T * NE])
        gsml = sb("gsml", [P, 2 * T])
        ps = [ctx.enter_context(nc.psum_tensor(f"ps{b}", [P, 512], F32)) for b in range(8)]
        table = [dram(f"table{n}", [T * P, D]) for n in range(3)]
        src_pad, dst_pad = dram("src_pad", [CHR, P], I32), dram("dst_pad", [CHR, P], I32)
        at_dram = dram("at_dram", [CHR], I32)
        h_spill = dram("h_spill", [T, P, HID])

        s_pool0 = sem("s_pool0", keep=True)
        s_mm = sem("s_mm", keep=True)
        s_ac = sem("s_ac", keep=True)
        s_m = sem("s_m", keep=True)
        s_st = sem("s_st", keep=True)
        s_go = sem("s_go", keep=True)
        s_g = [sem(f"s_g{u}", keep=True) for u in range(RING)]

        def bc(ap, parts=P):
            return ap.partition_broadcast(parts)

        def rsqrt(v, link, x, y, t, n):
            yi, ti = y.bitcast(I32), t.bitcast(I32)
            link(v.tensor_scalar(ti, x.bitcast(I32), 1, None, ALU.logical_shift_right))
            link(v.tensor_scalar(yi, ti, -1.0, MAGIC, ALU.mult, ALU.add))
            for _ in range(4):
                link(v.tensor_tensor(t, y, y, ALU.mult))
                link(v.tensor_tensor(t, t, x, ALU.mult))
                link(v.tensor_scalar(t, t, -0.5, 1.5, ALU.mult, ALU.add))
                link(v.tensor_tensor(y, y, t, ALU.mult))

        def row_stats(v, x, s_chain):
            with v.Fori(0, T) as i:
                v.bn_stats(mv[:, bass.ds(i, 1), :].rearrange("p t c -> p (t c)"), x[:, bass.ds(i * D, D)]).then_inc(s_chain, 1)
            v.wait_ge(s_chain, T)

        def norm_factors(v, link, var=newton[:, T:2 * T], tmp=newton[:, 0:T]):
            mean = nmr[:, :]
            link(v.tensor_tensor(tmp, mv[:, :, 1], mv[:, :, 4], ALU.subtract))
            link(v.tensor_tensor(tmp, tmp, tmp, ALU.mult))
            link(v.tensor_tensor(var, mv[:, :, 2], mv[:, :, 5], ALU.add))
            link(v.tensor_scalar(var, var, 1.0 / D, EPS, ALU.mult, ALU.add))
            link(v.scalar_tensor_tensor(var, tmp, 0.25, var, ALU.mult, ALU.add))
            rsqrt(v, link, var, rstd[:, :], tmp, T)
            link(v.tensor_tensor(mean, mv[:, :, 1], mv[:, :, 4], ALU.add))
            link(v.scalar_tensor_tensor(nmr[:, :], mean, -0.5, rstd[:, :], ALU.mult, ALU.mult))

        e_i = KVf[:, 0:2 * KC * P].bitcast(I32).rearrange("p (a k e) -> p a k e", a=2, k=KC)
        e_f = KVf[:, 2000:2000 + KC * P]
        d_t = KVf[:, 3000:3000 + CHR]
        hi_i = KVf[:, 4000:4000 + CHR].bitcast(I32)
        hi = KVf[:, 5000:5000 + CHR]
        lo = KVf[:, 6000:6000 + CHR]
        ones = KVf[:, 7000:7000 + P]
        iota_b = KVf[:, 7200:7200 + P // 2].bitcast(BF16)
        OH = 8
        oh_lo = [rows[:, b * P // 2:(b + 1) * P // 2].bitcast(BF16) for b in range(OH)]
        oh_hi = [rows[:, 1024 + 32 * b:1024 + 32 * (b + 1)].bitcast(BF16) for b in range(OH)]
        with nc.Block() as block:
            s_x, s_e, s_sp, s_cst, s_iota = (sem(n) for n in ("x_in", "e_in", "e_pad", "consts", "iotas"))
            s_ef, s_et, s_oh, s_hm, s_dg = (sem(n) for n in ("ef", "et", "oh", "hm", "dg"))
            s_ds, s_tot, s_cv, s_vr, s_vf, s_vt = (sem(n) for n in ("ds", "tot", "cv", "vr", "vf", "vt"))
            s_at, s_ad, s_v0, s_lnf, s_xn, s_ve, s_sl = (sem(n) for n in ("at", "ad", "v0", "lnf", "xn0", "ve", "sl"))

            @block.sync
            def _(sp):
                sp.wait_ge(s_pool0, 1)
                for a, name in enumerate(("src", "dst")):
                    full = (CH - 1) // P * P
                    e = A[name]
                    sp.dma_start(e_i[:, a, 0:KC - 1, :], e[0:full * P].rearrange("(k p e) -> p k e", p=P, e=P)).then_inc(s_e, 16)
                    sp.dma_start(e_i[0:CH - 1 - full, a, KC - 1, :],
                                 e[full * P:(CH - 1) * P].rearrange("(p e) -> p e", e=P)).then_inc(s_e, 16)
                    sp.dma_start(e_i[CH - 1 - full:CH - full, a, KC - 1, 0:E - (CH - 1) * P],
                                 e[(CH - 1) * P:E].rearrange("(p e) -> p e", p=1)).then_inc(s_e, 16)
                xv = XN[:, :].rearrange("p (t d) -> p t d", d=D)
                for q in range(4):
                    sp.dma_start(xv[:, 12 * q:12 * q + 12, :],
                                 A["x"][12 * q * P:12 * (q + 1) * P, :].rearrange("(t p) d -> p t d", p=P)).then_inc(s_x, 16)
                sp.dma_start(xv[0:LAST, T - 1, :], A["x"][(T - 1) * P:N, :]).then_inc(s_x, 16)
                sp.wait_ge(s_e, 6 * 16)
                sp.dma_start(src_pad.rearrange("(k p) e -> p k e", p=P), e_i[:, 0, :, :]).then_inc(s_sp, 16)
                sp.dma_start(dst_pad.rearrange("(k p) e -> p k e", p=P), e_i[:, 1, :, :]).then_inc(s_sp, 16)
                sp.wait_ge(s_at, 1)
                sp.dma_start(at_dram.rearrange("(k p) -> p k", p=P), gtmp[:, 0:VC].bitcast(I32), allow_slow_non_contiguous=True).then_inc(s_ad, 16)
                sp.wait_ge(s_ad, 16)
                sp.dma_start(acc_at[0:1, :], at_dram.rearrange("(a n) -> a n", a=1)).then_inc(s_ad, 16)
                sp.wait_ge(s_ad, 32)

            @block.gpsimd
            def _(g):
                g.memset(e_i[:, 0, :, :], 0).then_inc(s_cst, 1)
                g.memset(e_i[:, 1, :, :], PAD_DST).then_inc(s_cst, 1)
                g.memset(XN[:, (T - 1) * D:T * D], 0.0).then_inc(s_cst, 1)
                g.wait_ge(s_cst, 3)
                g.sem_inc(s_pool0, 1)
                g.memset(ident[:, :], 0.0).then_inc(s_cst, 1)
                g.memset(ones[:, :], 1.0).then_inc(s_cst, 1)
                g.wait_ge(s_cst, 5)
                g.affine_select(out=ident[:, :], in_=ident[:, :], compare_op=ALU.not_equal, fill=1.0, base=0,
                                pattern=[[-1, P]], channel_multiplier=1).then_inc(s_cst, 1)
                iv = idx_stage[:, 0:VC]
                g.iota(hi_i[:, 0:P], pattern=[[1, P]], base=0, channel_multiplier=0).then_inc(s_iota, 1)
                g.iota(iv, pattern=[[P, VC]], base=0, channel_multiplier=1).then_inc(s_iota, 1)
                g.wait_ge(s_sp, 32)
                g.wait_ge(s_cv, 1)
                for k in range(VC):
                    for a, pad in enumerate((src_pad, dst_pad)):
                        g.indirect_dma_start(out=e_i[:, a, k, :], out_offset=None, in_=pad,
                                             in_offset=bass.IndirectOffsetOnAxis(ap=newton[:, k:k + 1].bitcast(I32), axis=0)
                                             ).then_inc(s_vr, 16)

            @block.scalar
            def _(a):
                a.wait_ge(s_lnf, 1)
                with a.Fori(0, T) as i:
                    x = XN[:, bass.ds(i * D, D)]
                    a.activation(x, x, ACT.Identity, bias=nmr[:, bass.ds(i, 1)], scale=rstd[:, bass.ds(i, 1)]).then_inc(s_xn, 1)

            @block.tensor
            def _(pe):
                pe.sem_inc(s_mm, RING)
                pe.wait_ge(s_cst, 6)
                pe.wait_ge(s_ef, 1)
                for k in range(KC):
                    pe.transpose(ps[k // 4][:, k % 4 * P:k % 4 * P + P], e_f[:, k * P:(k + 1) * P], ident[:, :]).then_inc(s_et, 1)
                pe.sem_inc(s_hm, OH)
                for u in range(OH):
                    pe.wait_ge(s_oh, 2 * u + 2)
                    pe.matmul(ps[2][:, 0:T], oh_lo[u][:, :], oh_hi[u][:, 0:T], start=(u == 0), stop=False, skip_group_check=True).then_inc(s_hm, 1)
                with pe.Fori(1, CHR // OH - 8) as i:
                    for u in range(OH):
                        pe.wait_ge(s_oh, 2 * OH * i + 2 * u + 2)
                        pe.matmul(ps[2][:, 0:T], oh_lo[u][:, :], oh_hi[u][:, 0:T], start=False, stop=False, skip_group_check=True).then_inc(s_hm, 1)
                pe.wait_ge(s_ds, 1)
                pe.matmul(ps[3][:, 0:T], ones[:, :], deg[:, :], start=True, stop=True).then_inc(s_tot, 1)
                for k in range(VC):
                    pe.wait_ge(s_vf, 2 * k + 2)
                    if k >= 2:
                        pe.wait_ge(s_ve, 2 * k - 2)
                    for a in range(2):
                        pe.transpose(ps[4 + k % 2][:, a * P:a * P + P], work[:, (2 * (k % 2) + a) * P:(2 * (k % 2) + a + 1) * P],
                                     ident[:, :]).then_inc(s_vt, 1)

            @block.vector
            def _(v):
                link = Chain(v, s_v0)
                v.sem_inc(s_ac, 4)
                v.wait_ge(s_iota, 2)
                link(v.tensor_copy(iota[:, :], hi_i[:, 0:P]))
                link(v.tensor_copy(iota_b[:, :], iota[:, :]))
                vf = gtmp[:, 8:8 + VC]
                link(v.tensor_copy(vf, idx_stage[:, 0:VC]))
                v.wait_ge(s_e, 6 * 16)
                v.tensor_copy(e_f, e_i[:, 1, :, :].rearrange("p k e -> p (k e)")).then_inc(s_ef, 1)
                v.wait_ge(s_et, KC)
                d_i = e_f.bitcast(I32)
                for h in range(2):
                    n = min(512, CHR - 512 * h)
                    link(v.tensor_copy(d_t[:, 512 * h:512 * h + n], ps[h][:, 0:n]))
                    link(v.tensor_copy(d_i[:, 512 * h:512 * h + n], ps[h][:, 0:n]))
                link(v.tensor_scalar(hi_i, d_i, 7, None, ALU.arith_shift_right))
                link(v.tensor_copy(hi, hi_i))
                link(v.scalar_tensor_tensor(lo, hi, -float(P), d_t, ALU.mult, ALU.add))
                with v.Fori(0, CHR // OH - 8) as i:
                    for u in range(OH):
                        v.wait_ge(s_hm, OH * i + u + 1)
                        c = OH * i + u
                        v.tensor_scalar(oh_lo[u][:, :], iota_b[:, :], lo[:, bass.ds(c, 1)], None, ALU.is_equal).then_inc(s_oh, 1)
                        v.tensor_scalar(oh_hi[u][:, 0:T], iota_b[:, 0:T], hi[:, bass.ds(c, 1)], None, ALU.is_equal).then_inc(s_oh, 1)
                v.wait_ge(s_hm, CHR - 8 * OH + OH)
                link(v.tensor_copy(deg[:, :], ps[2][:, 0:T]))
                v.sem_inc(s_ds, 1)
                t49 = newton[:, T:2 * T]
                link(v.tensor_scalar(t49, deg[:, :], 1.0, None, ALU.add))
                rsqrt(v, link, t49, dinv[:, :], newton[:, 0:T], T)
                link(v.tensor_scalar(t49, deg[:, :], 1.0, None, ALU.max))
                link(v.reciprocal(invdeg[:, :], t49))
                v.wait_ge(s_tot, 1)
                c = [work[:, 1024 + 64 * n:1024 + 64 * n + T] for n in range(8)]
                tot, end, first, last, cnt, vend, dlt, junk = c
                link(v.tensor_copy(tot, ps[3][:, 0:T]))
                link(v.tensor_tensor_scan(end, ones[:, 0:T], tot, 0.0, ALU.mult, ALU.add))
                ji, fi, li = junk.bitcast(I32), first.bitcast(I32), last.bitcast(I32)
                link(v.tensor_tensor(junk, end, tot, ALU.subtract))
                link(v.tensor_copy(fi, junk))
                link(v.tensor_scalar(fi, fi, 7, None, ALU.arith_shift_right))
                link(v.tensor_scalar(li, end, -1.0, None, ALU.add))
                link(v.tensor_scalar(li, li, 7, None, ALU.arith_shift_right))
                link(v.tensor_copy(junk, fi))
                link(v.tensor_copy(cnt, li))
                link(v.tensor_tensor(cnt, cnt, junk, ALU.subtract))
                link(v.tensor_scalar(cnt, cnt, 1.0, None, ALU.add))
                link(v.scalar_tensor_tensor(cnt, tot, 0.0, cnt, ALU.is_gt, ALU.mult))
                link(v.tensor_tensor_scan(vend, ones[:, 0:T], cnt, 0.0, ALU.mult, ALU.add))
                link(v.tensor_tensor(dlt, junk, vend, ALU.subtract))
                link(v.tensor_tensor(dlt, dlt, cnt, ALU.add))
                tv, cd = gtmp[:, 16:16 + VC], gtmp[:, 24:24 + VC]
                for k in range(VC):
                    link(v.tensor_scalar(junk, vend, vf[:, k:k + 1], 0.0, ALU.is_le, ALU.add, accum_out=tv[:, k:k + 1]))
                    link(v.scalar_tensor_tensor(junk, iota[:, 0:T], tv[:, k:k + 1], dlt, ALU.is_equal, ALU.mult,
                                                accum_out=cd[:, k:k + 1]))
                link(v.tensor_tensor(cd, cd, vf, ALU.add))
                link(v.tensor_scalar(newton[:, 0:VC].bitcast(I32), cd, 0.0, CHR - 1.0, ALU.max, ALU.min))
                v.sem_inc(s_cv, 1)
                link(v.tensor_scalar(cd, tv, T - 1.0, float(D), ALU.min, ALU.mult))
                link(v.tensor_copy(gtmp[:, 0:VC].bitcast(I32), cd))
                v.sem_inc(s_at, 1)
                link(v.tensor_scalar(tv, tv, -float(P), None, ALU.mult))
                v.wait_ge(s_x, 5 * 16)
                row_stats(v, XN, s_sl)
                norm_factors(v, link, gsml[:, 0:T], gsml[:, T:2 * T])
                v.sem_inc(s_lnf, 1)
                v.wait_ge(s_vr, 2 * VC * 16)
                for k in range(VC):
                    if k >= 2:
                        v.wait_ge(s_vt, 2 * k - 2)
                    at = 2 * (k % 2) * P
                    v.tensor_copy(work[:, at:at + P], e_i[:, 0, k, :]).then_inc(s_vf, 1)
                    v.tensor_scalar(work[:, at + P:at + 2 * P], e_i[:, 1, k, :], tv[:, k:k + 1], None, ALU.add).then_inc(s_vf, 1)
                    v.wait_ge(s_vt, 2 * k + 2)
                    v.tensor_copy(src_idx[:, k * P:(k + 1) * P], ps[4 + k % 2][:, 0:P]).then_inc(s_ve, 1)
                    v.tensor_copy(dst_rel[:, k * P:(k + 1) * P], ps[4 + k % 2][:, P:2 * P]).then_inc(s_ve, 1)

        def col(t):
            return bass.ds(t * D, D)

        xrow = [work[:, b * D:(b + 1) * D] for b in range(2)]
        xT = [work[:, (2 + b) * D:(3 + b) * D] for b in range(2)]
        small = work[:, 1024:2048]
        bias_ps = ps[7]

        def load_bias(sp, dst, src, s):
            sp.dma_start(dst, src.partition_broadcast(P)).then_inc(s, 16)

        def start(eng, *steps):
            for step in steps:
                eng.sem_inc(step.sem, step.depth)

        def steps(prefix, names):
            return [Step(sem(prefix + n)) for n in names.split()]

        def to_table(sp, n, h, s_tab):
            with sp.Fori(0, T) as i:
                sp.wait_ge(*h.after(i))
                sp.dma_start(table[n][bass.ds(i * P, P), :], ACC[:, bass.ds(i * D, D)]).then_inc(s_tab, 16)
            sp.wait_ge(s_tab, T * 16)

        w1kv = wreg[:, 0:1024].rearrange("p (c n) -> p c n", c=2)
        kmax = small[:, 0:P]
        with nc.Block() as block:
            row, tp, xt, mm, kv, h, mx = steps("a_", "row tp xt mm kv h mx")
            s_w, s_tab, s_km, s_one = sem("a_w"), sem("a_tab"), sem("a_km"), sem("a_one")

            @block.sync
            def _(sp):
                sp.dma_start(w1kv[:, :, 0:D], A["L0_gnn_W1"].rearrange("(c p) n -> p c n", p=P)).then_inc(s_w, 16)
                sp.dma_start(w1kv[:, :, D:2 * D], A["L0_mix_W_qkv"][:, P:3 * P].rearrange("(c p) n -> p c n", p=P)).then_inc(s_w, 16)
                to_table(sp, 0, h, s_tab)

            @block.gpsimd
            def _(g):
                g.memset(KV[:, :, D:D + 1], 1.0).then_inc(s_one, 1)

            @block.scalar
            def _(a):
                start(a, row, xt)

                def a_row(t, b):
                    a.wait_ge(*tp.room(t))
                    a.copy(xrow[b], XN[:, col(t)]).then_inc(row.sem, 1)

                def a_xt(t, b):
                    a.wait_ge(*tp.after(t))
                    a.wait_ge(*mm.room(t))
                    a.copy(xT[b], ps[b][:, 0:D]).then_inc(xt.sem, 1)
                tiles(a, (a_row, 0), (a_xt, 0))

            @block.tensor
            def _(pe):
                start(pe, tp, mm)
                pe.wait_ge(s_w, 32)

                def p_tp(t, b):
                    pe.wait_ge(*row.after(t))
                    pe.wait_ge(*xt.room(t))
                    pe.transpose(ps[b][:, 0:P], xrow[b][:, 0:P], ident[:, :])
                    pe.transpose(ps[b][:, P:D], xrow[b][:, P:D], ident[:, :]).then_inc(tp.sem, 1)

                def p_mm(t, b):
                    pe.wait_ge(*xt.after(t))
                    for s in (kv, h, mx):
                        pe.wait_ge(*s.room(t))
                    pe.matmul(ps[2 + b][:, :], xT[b][:, 0:P], w1kv[:, 0, :], start=True, stop=False)
                    pe.matmul(ps[2 + b][:, :], xT[b][:, P:D], w1kv[:, 1, :], start=False, stop=True).then_inc(mm.sem, 1)
                tiles(pe, (p_tp, 0), (p_mm, 1))

            @block.vector
            def _(v):
                start(v, h, mx, kv)
                v.memset(kmax, -3.0e38).then_inc(s_km, 1)
                v.wait_ge(s_km, 1)

                def v_h(t, b):
                    v.wait_ge(*mm.after(t))
                    v.tensor_scalar(ACC[:, col(t)], ps[2 + b][:, 0:D], dinv[:, bass.ds(t, 1)], None, ALU.mult).then_inc(h.sem, 1)

                def v_mx(t, b):
                    v.wait_ge(*mx.after(t - 1))
                    n = LAST if isinstance(t, int) and t == T - 1 else P
                    v.tensor_tensor(kmax[0:n], kmax[0:n], ps[2 + b][0:n, D:D + P], ALU.max).then_inc(mx.sem, 1)

                def v_kv(t, b):
                    v.tensor_copy(KV[:, bass.ds(t, 1), 0:D].rearrange("p t c -> p (t c)"), ps[2 + b][:, D:2 * D]).then_inc(kv.sem, 1)
                tiles(v, (v_h, 0), (v_mx, 0), (v_kv, 0))

        erow = [small[:, (1 + b) * P:(2 + b) * P] for b in range(2)]
        nmax, nmat = gsml[:, 0:1], small[:, 3 * P:4 * P]
        wq = wreg[:, 0:D].rearrange("p (c n) -> p c n", c=2)
        wout = wreg[:, D:2 * D]
        g0 = wreg[:, 1024:1536].rearrange("p (c n) -> p c n", c=2)
        w2 = wreg[:, 1536:2048].rearrange("p (c n) -> p c n", c=2)
        wqT, m1 = wreg[:, 2048:2304], wreg[:, 2304:2560]
        cbd, cT = small[:, 4 * P:5 * P], small[:, 5 * P:6 * P]
        with nc.Block() as block:
            sub, ex, cx = steps("c_", "sub ex cx")
            s_w, s_v, s_p, s_a = sem("c_w"), sem("c_v"), sem("c_p"), sem("c_a")

            @block.sync
            def _(sp):
                sp.dma_start(wq, A["L0_mix_W_qkv"][:, 0:P].rearrange("(c p) n -> p c n", p=P)).then_inc(s_w, 16)
                sp.dma_start(wout, A["L0_mix_W_out"]).then_inc(s_w, 16)
                sp.dma_start(w2, A["L0_gnn_W2"].rearrange("(c p) n -> p c n", p=P)).then_inc(s_w, 16)
                sp.wait_ge(s_w, 48)

            @block.scalar
            def _(a):
                start(a, ex)

                def a_ex(t, b):
                    a.wait_ge(*sub.after(t))
                    a.wait_ge(*cx.room(t))
                    a.activation(erow[b], KV[:, bass.ds(t, 1), 0:P].rearrange("p t c -> p (t c)"), ACT.Exp).then_inc(ex.sem, 1)
                tiles(a, (a_ex, 0))

            @block.tensor
            def _(pe):
                start(pe, cx)
                pe.transpose(ps[0][:, 0:P], kmax, ident[:, :]).then_inc(s_p, 1)
                pe.wait_ge(s_v, 2)
                pe.matmul(ps[1][:, 0:P], nmat, ident[:, :], start=True, stop=True).then_inc(s_p, 1)

                def p_cx(t, b):
                    n = LAST if isinstance(t, int) and t == T - 1 else P
                    pe.wait_ge(*ex.after(t))
                    pe.matmul(ps[2][:, 0:P + 1], erow[b][0:n], KV[0:n, bass.ds(t, 1), P:D + 1].rearrange("p t c -> p (t c)"),
                              start=isinstance(t, int) and t == 0, stop=isinstance(t, int) and t == T - 1,
                              skip_group_check=True).then_inc(cx.sem, 1)
                tiles(pe, (p_cx, 0))
                pe.wait_ge(s_w, 48)
                for c in range(2):
                    pe.transpose(ps[3][:, c * P:(c + 1) * P], wq[:, c, :], ident[:, :]).then_inc(s_p, 1)
                pe.wait_ge(s_v, 9)
                pe.transpose(ps[4][:, 0:P], cbd, ident[:, :]).then_inc(s_p, 1)
                pe.wait_ge(s_v, 10)
                pe.matmul(ps[5][:, 0:D], cT, wout, start=True, stop=True).then_inc(s_p, 1)
                pe.wait_ge(s_v, 11)
                for c in range(2):
                    pe.matmul(ps[6][:, c * D:(c + 1) * D], wqT[:, c * P:(c + 1) * P], m1, start=True, stop=True).then_inc(s_p, 1)

            @block.vector
            def _(v):
                link = Chain(v, s_v)
                start(v, sub)
                v.wait_ge(s_p, 1)
                link(v.tensor_reduce(nmax, ps[0][:, 0:P], AX.X, ALU.max, negate=True))
                link(v.tensor_copy(nmat, nmax.broadcast_to([P, P])))
                v.wait_ge(s_p, 2)

                def v_sub(t, b):
                    k = KV[:, bass.ds(t, 1), 0:P].rearrange("p t c -> p (t c)")
                    v.tensor_tensor(k, k, ps[1][:, 0:P], ALU.add).then_inc(sub.sem, 1)
                tiles(v, (v_sub, 0))
                v.wait_ge(*cx.after(T - 1))
                link(v.reciprocal(nmax, ps[2][:, P:P + 1]))
                link(v.memset(cbd, 0.0))
                for q in range(4):
                    r = slice(32 * q, 32 * q + 32)
                    link(v.tensor_scalar(cbd[r, r], ps[2][r, r], nmax[r], 32.0 ** -0.5, ALU.mult, ALU.mult))
                v.wait_ge(s_p, 4)
                link(v.tensor_copy(wqT, ps[3][:, 0:D]))
                v.wait_ge(s_p, 5)
                link(v.tensor_copy(cT, ps[4][:, 0:P]))
                v.wait_ge(s_p, 6)
                link(v.tensor_copy(m1, ps[5][:, 0:D]))
                v.wait_ge(s_p, 8)
                link(v.tensor_copy(wreg[:, 1024:1536], ps[6][:, :]))

        def aggregate(phase, tab, sync=None):
            with nc.Block() as block:
                if sync:
                    block.sync(sync)

                @block.scalar
                def _(a):
                    with a.Fori(0, VI) as i:
                        for q in range(RING // 4):
                            a.wait_ge(s_mm, (i + phase * VI) * RING + 4 * q + 4)
                            a.copy(idx_stage[:, 4 * q:4 * q + 4], src_idx[:, bass.ds(i * RING + 4 * q, 4)]).then_inc(s_st, 1)

                @block.gpsimd
                def _(g):
                    with g.Fori(0, VI) as i:
                        for q in range(RING // 4):
                            g.wait_ge(s_st, (i + phase * VI) * (RING // 4) + q + 1)
                            g.sem_inc(s_go, 1)
                            for u in range(4 * q, 4 * q + 4):
                                g.indirect_dma_start(out=rows[:, u * D:(u + 1) * D], out_offset=None, in_=tab,
                                                     in_offset=bass.IndirectOffsetOnAxis(ap=idx_stage[:, u:u + 1], axis=0)
                                                     ).then_inc(s_g[u], 16)

                @block.tensor
                def _(pe):
                    with pe.Fori(0, VI) as i:
                        turn = i + phase * VI
                        for u in range(RING):
                            pe.wait_ge(s_g[u], turn * 16 + 16)
                            pe.wait_ge(s_m, turn * RING + u + 1)
                            pe.wait_ge(s_ac, turn * RING + u + 1)
                            pe.matmul(ps[u % 4][:, 0:D], mring[:, u % 4 * P:(u % 4 + 1) * P], rows[:, u * D:(u + 1) * D],
                                      start=True, stop=True).then_inc(s_mm, 1)

                @block.vector
                def _(v):
                    def matrix(i, u):
                        v.wait_ge(s_mm, (i + phase * VI) * RING + u + 1 + RING - 4)
                        v.tensor_scalar(mring[:, u % 4 * P:(u % 4 + 1) * P], iota[:, :], dst_rel[:, bass.ds(i * RING + u, 1)], None,
                                        ALU.is_equal).then_inc(s_m, 1)

                    def add(i, u):
                        at = v.value_load(acc_at[0:1, bass.ds(i * RING + u, 1)], min_val=0, max_val=(T - 1) * D)
                        v.wait_ge(s_mm, (i + phase * VI) * RING + u + 1 + RING)
                        v.wait_ge(s_ac, (i + phase * VI) * RING + u + 4)
                        acc = ACC[:, bass.ds(at, D)]
                        v.tensor_tensor(acc, acc, ps[u % 4][:, 0:D], ALU.add).then_inc(s_ac, 1)

                    with v.Fori(0, VI) as i:
                        for u in range(RING + 2):
                            if u < RING:
                                matrix(i, u)
                            if u >= 2:
                                add(i, u - 2)

        b_row, b_row2 = bias_rows[:, 0:D], bias_rows[:, D:2 * D]
        s_r0 = sem("r_in", keep=True)
        Rt = R.rearrange("p (t d) -> p t d", d=D)

        def fetch_x(sp):
            sp.wait_ge(s_z, 1)
            for q in range(4):
                sp.dma_start(Rt[:, 12 * q:12 * q + 12, :],
                             A["x"][12 * q * P:12 * (q + 1) * P, :].rearrange("(t p) d -> p t d", p=P)).then_inc(s_r0, 16)
            sp.dma_start(Rt[0:LAST, T - 1, :], A["x"][(T - 1) * P:N, :]).then_inc(s_r0, 16)
            load_bias(sp, b_row, A["L0_gnn_b1"], s_r0)
            load_bias(sp, b_row2, A["L0_mix_b_out"], s_r0)
            sp.wait_ge(s_r0, 7 * 16)

        s_z = sem("r_zero")
        with nc.Block() as block:
            @block.gpsimd
            def _(g):
                g.memset(R[:, (T - 1) * D:T * D], 0.0).then_inc(s_z, 1)
        aggregate(0, table[0], fetch_x)

        x1 = [small[:, b * D:(b + 1) * D] for b in range(2)]
        zt = [small[:, (2 + b) * D:(3 + b) * D] for b in range(2)]
        xT2 = [rows[:, b * 512:(b + 1) * 512] for b in range(2)]
        with nc.Block() as block:
            row, tp, xt, mm, z, w1, r, h, rb, wr = steps("b_", "row tp xt mm z x1 r h rb wr")
            s_tab, s_b = sem("b_tab"), sem("b_bias")

            @block.sync
            def _(sp):
                to_table(sp, 1, h, s_tab)

            @block.gpsimd
            def _(g):
                start(g, rb, wr)

                def g_rb(t, b):
                    g.tensor_tensor(R[:, col(t)], R[:, col(t)], b_row2, ALU.add).then_inc(rb.sem, 1)

                def g_wr(t, b):
                    g.wait_ge(*row.after(t))
                    g.wait_ge(*w1.after(t))
                    g.tensor_copy(XN[:, col(t)], x1[b]).then_inc(wr.sem, 1)
                tiles(g, (g_rb, 0), (g_wr, 1))

            @block.scalar
            def _(a):
                start(a, row, xt)

                def a_row(t, b):
                    a.wait_ge(*tp.room(t))
                    a.copy(xrow[b], XN[:, col(t)]).then_inc(row.sem, 1)

                def a_xt(t, b):
                    a.wait_ge(*tp.after(t))
                    a.wait_ge(*mm.room(t))
                    a.copy(xT2[b], ps[b][:, :]).then_inc(xt.sem, 1)
                tiles(a, (a_row, 0), (a_xt, 0))

            @block.tensor
            def _(pe):
                start(pe, tp, mm)

                def p_tp(t, b):
                    pe.wait_ge(*row.after(t))
                    pe.wait_ge(*w1.after(t))
                    pe.wait_ge(*xt.room(t))
                    for c in range(2):
                        pe.transpose(ps[b][:, c * P:(c + 1) * P], xrow[b][:, c * P:(c + 1) * P], ident[:, :])
                    pe.transpose(ps[b][:, 2 * P:3 * P], x1[b][:, 0:P], ident[:, :])
                    pe.transpose(ps[b][:, 3 * P:4 * P], x1[b][:, P:D], ident[:, :]).then_inc(tp.sem, 1)

                def p_mm(t, b):
                    pe.wait_ge(*xt.after(t))
                    pe.wait_ge(*r.room(t))
                    pe.wait_ge(*h.room(t))
                    for c in range(2):
                        pe.matmul(ps[2 + b][:, 0:D], xT2[b][:, c * P:(c + 1) * P], g0[:, c, :], start=c == 0, stop=c == 1)
                    pe.matmul(ps[2 + b][:, D:2 * D], xT2[b][:, 2 * P:3 * P], w2[:, 0, :], start=True, stop=False)
                    pe.matmul(ps[2 + b][:, D:2 * D], xT2[b][:, 3 * P:4 * P], w2[:, 1, :], start=False, stop=True).then_inc(mm.sem, 1)
                tiles(pe, (p_tp, 0), (p_mm, 1))

            @block.vector
            def _(v):
                start(v, z, w1, r, h)
                v.tensor_copy(bias_ps[:, 0:D], b_row).then_inc(s_b, 1)
                v.wait_ge(s_b, 1)

                def v_z(t, b):
                    v.wait_ge(*w1.room(t))
                    v.scalar_tensor_tensor(ps[4 + b][:, 0:D], ACC[:, col(t)], dinv[:, bass.ds(t, 1)], bias_ps[:, 0:D],
                                           ALU.mult, ALU.add).then_inc(z.sem, 1)

                def v_x1(t, b):
                    v.wait_ge(*z.after(t))
                    v.wait_ge(*tp.room(t))
                    v.wait_ge(*wr.room(t))
                    v.scalar_tensor_tensor(x1[b], ps[4 + b][:, 0:D], 0.0, XN[:, col(t)], ALU.max, ALU.add).then_inc(w1.sem, 1)

                def v_r(t, b):
                    v.wait_ge(*mm.after(t))
                    v.wait_ge(*rb.after(t))
                    v.tensor_tensor(R[:, col(t)], R[:, col(t)], ps[2 + b][:, 0:D], ALU.add).then_inc(r.sem, 1)

                def v_h(t, b):
                    v.wait_ge(*z.after(t))
                    v.tensor_scalar(ACC[:, col(t)], ps[2 + b][:, D:2 * D], dinv[:, bass.ds(t, 1)], None, ALU.mult).then_inc(h.sem, 1)
                tiles(v, (v_z, 0), (v_x1, 0), (v_r, 2), (v_h, 2))

        def fetch_b2(sp):
            load_bias(sp, b_row, A["L0_gnn_b2"], s_r0)
            sp.wait_ge(s_r0, 8 * 16)
        aggregate(1, table[1], fetch_b2)
        STAGE_AGG2_DONE = True

        with nc.Block() as block:
            z, xp, rx = steps("d_", "z xp rx")
            s_b, s_sl, s_n = sem("d_bias"), sem("d_stats"), sem("d_norm")

            @block.gpsimd
            def _(g):
                start(g, rx)

                def g_rx(t, b):
                    g.tensor_tensor(R[:, col(t)], R[:, col(t)], XN[:, col(t)], ALU.add).then_inc(rx.sem, 1)
                tiles(g, (g_rx, 0))

            @block.vector
            def _(v):
                start(v, z, xp)

                def v_z(t, b):
                    v.wait_ge(*xp.room(t))
                    v.scalar_tensor_tensor(ps[4 + b][:, 0:D], ACC[:, col(t)], dinv[:, bass.ds(t, 1)], b_row,
                                           ALU.mult, ALU.add).then_inc(z.sem, 1)

                def v_xp(t, b):
                    v.wait_ge(*z.after(t))
                    v.wait_ge(*rx.after(t))
                    v.scalar_tensor_tensor(XN[:, col(t)], ps[4 + b][:, 0:D], 0.0, R[:, col(t)], ALU.max, ALU.add).then_inc(xp.sem, 1)
                tiles(v, (v_z, 0), (v_xp, 1))
                v.wait_ge(*xp.after(T - 1))
                row_stats(v, XN, s_sl)
                norm_factors(v, Chain(v, s_n))

        ff1 = wreg[:, 0:2048].rearrange("p (c n) -> p c n", c=2)
        wg = wreg[:, 2048:2048 + HC * NE].rearrange("p (k n) -> p k n", n=NE)
        hb = wreg[:, 2112:2112 + HC]
        bgr = wreg[:, 2120:2120 + NE]
        i8 = wreg[:, 2128:2128 + NE]
        bd = wreg[0:NE, 2304:2304 + D]
        hT = [rows[:, b * HID:(b + 1) * HID] for b in range(2)]
        hL = [rows[:, (2 + b) * HID:(3 + b) * HID] for b in range(2)]
        s_wd = sem("s_wd")
        gate3 = gate[:, :].rearrange("p (t e) -> p t e", e=NE)
        gtmp3 = gtmp[:, :].rearrange("p (t e) -> p t e", e=NE)
        with nc.Block() as block:
            row, tp, xt, mm, gl, lg, lc = steps("f_", "row tp xt mm gl lg lc")
            s_w, s_sp, s_v, s_a = sem("f_w"), [sem("f_sp0"), sem("f_sp1")], sem("f_v"), sem("f_a")

            @block.sync
            def _(sp):
                sp.dma_start(ff1, A["L0_ffn_W1"].rearrange("(c p) n -> p c n", p=P)).then_inc(s_w, 16)
                sp.dma_start(wg, A["L0_ffn_Wg"].rearrange("(k p) n -> p k n", p=P)).then_inc(s_w, 16)
                sp.dma_start(hb, A["L0_ffn_b1"].rearrange("(k p) -> p k", p=P), allow_slow_non_contiguous=True).then_inc(s_w, 16)
                load_bias(sp, bgr, A["L0_ffn_bg"], s_w)
                sp.dma_start(bd, A["L0_ffn_bd"]).then_inc(s_w, 16)
                sp.wait_ge(s_w, 5 * 16)
                for e in range(NE):
                    sp.dma_start(WD[:, e * HC * D:(e + 1) * HC * D].rearrange("p (k n) -> p k n", n=D),
                                 A["L0_ffn_Wd"][e].rearrange("(k p) n -> p k n", p=P)).then_inc(s_wd, 16)

                for b in range(2):
                    sp.sem_inc(s_sp[b], 16)

                def s_h(t, b):
                    sp.wait_ge(*gl.after(t))
                    sp.dma_start(h_spill[bass.ds(t, 1)].rearrange("t p n -> (t p) n"), hT[b]).then_inc(s_sp[b], 16)
                tiles(sp, (s_h, 0))
                sp.wait_ge(s_sp[0], 16 * 26)
                sp.wait_ge(s_sp[1], 16 * 25)

            @block.scalar
            def _(a):
                start(a, row, gl)
                a.wait_ge(s_w, 5 * 16)

                def a_row(t, b):
                    a.wait_ge(*tp.room(t))
                    a.activation(xrow[b], XN[:, col(t)], ACT.Identity, bias=nmr[:, bass.ds(t, 1)],
                                 scale=rstd[:, bass.ds(t, 1)]).then_inc(row.sem, 1)

                def a_gl(t, b):
                    a.wait_ge(*mm.after(t))
                    a.wait_ge(*lg.room(t))
                    a.wait_ge(s_sp[b], 8 * (t - b) + 16)
                    for k in range(HC):
                        ins = a.activation(hT[b][:, k * P:(k + 1) * P], ps[2 + 2 * b + k // 4][:, k % 4 * P:(k % 4 + 1) * P],
                                           ACT.Gelu, bias=hb[:, k:k + 1])
                    ins.then_inc(gl.sem, 1)
                tiles(a, (a_row, 0), (a_gl, 1))

            @block.tensor
            def _(pe):
                start(pe, tp, mm, lg)
                pe.wait_ge(s_w, 5 * 16)

                def p_tp(t, b):
                    pe.wait_ge(*row.after(t))
                    pe.wait_ge(*xt.room(t))
                    pe.transpose(ps[b][:, 0:P], xrow[b][:, 0:P], ident[:, :])
                    pe.transpose(ps[b][:, P:D], xrow[b][:, P:D], ident[:, :]).then_inc(tp.sem, 1)

                def p_mm(t, b):
                    pe.wait_ge(*xt.after(t))
                    pe.wait_ge(*gl.room(t))
                    for k in range(HC):
                        o = ps[2 + 2 * b + k // 4][:, k % 4 * P:(k % 4 + 1) * P]
                        for c in range(2):
                            ins = pe.matmul(o, ff1[:, c, k * P:(k + 1) * P], xT[b][:, c * P:(c + 1) * P], start=c == 0, stop=c == 1)
                    ins.then_inc(mm.sem, 1)

                def p_lg(t, b):
                    pe.wait_ge(*gl.after(t))
                    pe.wait_ge(*lc.room(t))
                    for k in range(HC):
                        ins = pe.matmul(ps[6 + b][:, 0:NE], hT[b][:, k * P:(k + 1) * P], wg[:, k, :], start=k == 0, stop=k == HC - 1)
                    ins.then_inc(lg.sem, 1)
                tiles(pe, (p_tp, 0), (p_mm, 0), (p_lg, 1))

            @block.vector
            def _(v):
                start(v, xt, lc)
                v.wait_ge(s_w, 5 * 16)

                def v_xt(t, b):
                    v.wait_ge(*tp.after(t))
                    v.wait_ge(*mm.room(t))
                    v.tensor_copy(xT[b], ps[b][:, 0:D]).then_inc(xt.sem, 1)

                def v_lc(t, b):
                    v.wait_ge(*lg.after(t))
                    v.tensor_tensor(gate[:, bass.ds(t * NE, NE)], ps[6 + b][:, 0:NE], bgr, ALU.add).then_inc(lc.sem, 1)
                tiles(v, (v_xt, 0), (v_lc, 1))

        def wide(x, n):
            return x.unsqueeze(2).broadcast_to([P, T, n])

        with nc.Block() as block:
            s_v, s_a = sem("g_v"), sem("g_a")
            mxg, sm = gsml[:, 0:T], gsml[:, T:2 * T]

            @block.scalar
            def _(a):
                a.wait_ge(s_v, 3)
                a.activation(gate[:, :], gate[:, :], ACT.Exp).then_inc(s_a, 1)

            @block.vector
            def _(v):
                link = Chain(v, s_v)
                link(v.tensor_scalar(i8, iota[:, 0:NE], -1.0, float(NE), ALU.mult, ALU.add))
                link(v.tensor_reduce(mxg, gate3, AX.X, ALU.max))
                link(v.tensor_tensor(gate3, gate3, wide(mxg, NE), ALU.subtract))
                v.wait_ge(s_a, 1)
                link(v.tensor_reduce(sm, gate3, AX.X, ALU.add))
                link(v.reciprocal(sm, sm))
                link(v.tensor_tensor(gate3, gate3, wide(sm, NE), ALU.mult))
                link(v.tensor_reduce(mxg, gate3, AX.X, ALU.max))
                link(v.tensor_tensor(gtmp3, gate3, wide(mxg, NE), ALU.is_equal))
                link(v.tensor_tensor(gtmp3, gtmp3, i8.unsqueeze(1).broadcast_to([P, T, NE]), ALU.mult))
                link(v.tensor_reduce(mxg, gtmp3, AX.X, ALU.max))
                link(v.tensor_tensor(gtmp3, gtmp3, wide(mxg, NE), ALU.is_equal))
                link(v.tensor_tensor(gate3, gate3, gtmp3, ALU.mult))

        wst = [small[:, b * NE:(b + 1) * NE] for b in range(2)]
        wT = [small[0:NE, 64 + b * P:64 + (b + 1) * P] for b in range(2)]
        with nc.Block() as block:
            wc, wt, wtc, bm, ax = steps("e_", "wc wt wtc bm ax")
            s_hl = [sem("e_h0"), sem("e_h1")]
            dn, ad = Step(sem("e_down"), 4), Step(sem("e_added"), 4)
            s_c = sem("e_chain")

            @block.sync
            def _(sp):
                def s_h(t, b):
                    sp.wait_ge(*bm.room(t))
                    sp.dma_start(hL[b], h_spill[bass.ds(t, 1)].rearrange("t p n -> (t p) n")).then_inc(s_hl[b], 16)
                tiles(sp, (s_h, 0))

            @block.tensor
            def _(pe):
                start(pe, wt, bm, dn)
                pe.wait_ge(s_wd, NE * 16)

                def p_w(t, b):
                    pe.wait_ge(*wc.after(t))
                    pe.wait_ge(*wtc.room(t))
                    pe.transpose(ps[4 + b][0:NE, 0:P], wst[b], ident[:, :]).then_inc(wt.sem, 1)

                def p_e(t, b):
                    pe.wait_ge(s_hl[b], 8 * (t - b) + 16)
                    for q in range(NE // 2):
                        pe.wait_ge(*ad.room(4 * t + q))
                        for e in (2 * q, 2 * q + 1):
                            for k in range(HC):
                                ins = pe.matmul(ps[q][:, e % 2 * D:(e % 2 + 1) * D], hL[b][:, k * P:(k + 1) * P],
                                                WD[:, (e * HC + k) * D:(e * HC + k + 1) * D], start=k == 0, stop=k == HC - 1)
                        ins.then_inc(dn.sem, 1)
                    pe.wait_ge(*wtc.after(t))
                    pe.wait_ge(*ax.room(t))
                    pe.matmul(ps[6 + b][:, 0:D], wT[b], bd, start=True, stop=True).then_inc(bm.sem, 1)
                tiles(pe, (p_w, 0), (p_e, 0))

            @block.vector
            def _(v):
                start(v, wc, wtc, ad, ax)
                chain = Chain(v, s_c, NE + 1)

                def v_wc(t, b):
                    v.wait_ge(*wt.room(t))
                    v.tensor_copy(wst[b], gate[:, bass.ds(t * NE, NE)]).then_inc(wc.sem, 1)

                def v_wtc(t, b):
                    v.wait_ge(*wt.after(t))
                    v.wait_ge(*bm.room(t))
                    v.tensor_copy(wT[b], ps[4 + b][0:NE, 0:P]).then_inc(wtc.sem, 1)

                def v_add(t, b):
                    chain.tile(t)
                    x = XN[:, col(t)]
                    for q in range(NE // 2):
                        v.wait_ge(*dn.after(4 * t + q))
                        for e in (2 * q, 2 * q + 1):
                            chain(v.scalar_tensor_tensor(x, ps[q][:, e % 2 * D:(e % 2 + 1) * D], gate[:, bass.ds(t * NE + e, 1)], x,
                                                         ALU.mult, ALU.add))
                        v.sem_inc(ad.sem, 1)
                    v.wait_ge(*bm.after(t))
                    chain(v.tensor_tensor(x, x, ps[6 + b][:, 0:D], ALU.add))
                    v.sem_inc(ax.sem, 1)
                tiles(v, (v_wc, 0), (v_wtc, 0), (v_add, 0))

        retire_sems()

        wns = wreg[:, 0:1024].rearrange("p (c n) -> p c n", c=2)
        x3 = [work[:, b * (D + 1):(b + 1) * (D + 1)] for b in range(2)]
        xT3 = [small[:, b * D:(b + 1) * D] for b in range(2)]
        with nc.Block() as block:
            row, tp, xt, mm, tb, r, rb, wr = steps("h_", "row tp xt mm tb r rb wr")
            s_w, s_sl, s_n, s_nf, s_one, s_tab, s_bs = (sem("h_" + n) for n in "w sl n nf one tab bs".split())

            @block.sync
            def _(sp):
                sp.dma_start(wns[:, :, 0:D], A["L1_gnn_W_neigh"].rearrange("(c p) n -> p c n", p=P)).then_inc(s_w, 16)
                sp.dma_start(wns[:, :, D:2 * D], A["L1_gnn_W_self"].rearrange("(c p) n -> p c n", p=P)).then_inc(s_w, 16)
                load_bias(sp, b_row, A["L1_gnn_b"], s_w)
                load_bias(sp, b_row2, A["L1_mix_b_fc2"], s_w)
                to_table(sp, 2, tb, s_tab)

            @block.gpsimd
            def _(g):
                start(g, rb, wr)
                for b in range(2):
                    g.memset(x3[b][:, D:D + 1], 1.0).then_inc(s_one, 1)
                g.wait_ge(s_w, 4 * 16)
                g.tensor_tensor(b_row, b_row, b_row2, ALU.add).then_inc(s_bs, 1)
                g.wait_ge(s_bs, 1)

                def g_rb(t, b):
                    g.wait_ge(*r.after(t))
                    g.tensor_tensor(R[:, col(t)], R[:, col(t)], b_row, ALU.add).then_inc(rb.sem, 1)

                def g_wr(t, b):
                    g.tensor_copy(XN[:, col(t)], x3[b][:, 0:D]).then_inc(wr.sem, 1)
                tiles(g, (g_rb, 0), (g_wr, 0))

            @block.scalar
            def _(a):
                start(a, row)
                a.wait_ge(s_nf, 1)

                def a_row(t, b):
                    a.wait_ge(*mm.room(t))
                    a.wait_ge(*wr.room(t))
                    a.activation(x3[b][:, 0:D], XN[:, col(t)], ACT.Identity, bias=nmr[:, bass.ds(t, 1)],
                                 scale=rstd[:, bass.ds(t, 1)]).then_inc(row.sem, 1)
                tiles(a, (a_row, 0))

            @block.tensor
            def _(pe):
                start(pe, tp, mm)
                pe.wait_ge(s_w, 4 * 16)
                pe.wait_ge(s_one, 2)

                def p_tp(t, b):
                    pe.wait_ge(*row.after(t))
                    pe.wait_ge(*xt.room(t))
                    pe.transpose(ps[b][:, 0:P], x3[b][:, 0:P], ident[:, :])
                    pe.transpose(ps[b][:, P:D], x3[b][:, P:D], ident[:, :]).then_inc(tp.sem, 1)

                def p_mm(t, b):
                    first, last = (isinstance(t, int) and t == q for q in (0, T - 1))
                    n = LAST if last else P
                    for c in range(2):
                        pe.matmul(ps[5 + c][:, 0:D + 1], x3[b][0:n, c * P:(c + 1) * P], x3[b][0:n, :], start=first, stop=last,
                                  skip_group_check=True)
                    pe.wait_ge(*xt.after(t))
                    pe.wait_ge(*tb.room(t))
                    pe.wait_ge(*r.room(t))
                    pe.matmul(ps[2 + b][:, :], xT3[b][:, 0:P], wns[:, 0, :], start=True, stop=False)
                    pe.matmul(ps[2 + b][:, :], xT3[b][:, P:D], wns[:, 1, :], start=False, stop=True).then_inc(mm.sem, 1)
                tiles(pe, (p_tp, 0), (p_mm, 0))

            @block.vector
            def _(v):
                start(v, xt, r, tb)
                row_stats(v, XN, s_sl)
                norm_factors(v, Chain(v, s_n))
                v.sem_inc(s_nf, 1)

                def v_xt(t, b):
                    v.wait_ge(*tp.after(t))
                    v.wait_ge(*mm.room(t))
                    v.tensor_copy(xT3[b], ps[b][:, 0:D]).then_inc(xt.sem, 1)

                def v_r(t, b):
                    v.wait_ge(*mm.after(t))
                    v.tensor_tensor(R[:, col(t)], XN[:, col(t)], ps[2 + b][:, D:2 * D], ALU.add).then_inc(r.sem, 1)

                def v_tb(t, b):
                    v.tensor_copy(ACC[:, col(t)], ps[2 + b][:, 0:D]).then_inc(tb.sem, 1)
                tiles(v, (v_xt, 0), (v_r, 0), (v_tb, 0))

        wqkv = rows[:, 0:1536].rearrange("p (c n) -> p c n", c=2)
        gram = rows[:, 1536:2048].rearrange("p (c n) -> p c n", c=2)
        t1 = rows[:, 2048:2560].rearrange("p (c n) -> p c n", c=2)
        wq1T = rows[:, 2560:3072].rearrange("p (c n) -> p c n", c=2)
        abd = rows[:, 3072:3328].rearrange("p (c n) -> p c n", c=2)
        abT = rows[:, 3328:3584].rearrange("p (c n) -> p c n", c=2)
        bqc = rows[:, 3584:3586]
        bqm = rows[:, 3600:3728]
        csum, nmx = rows[:, 3586:3588], rows[:, 3588:3590]
        rsm = rows[:, 3590:3592]
        nval = rows[0:1, 3592:3593]
        att = rows[:, 3728:3856].rearrange("p (c n) -> p c n", c=2)
        bqkv = work[0:1, 0:768]
        crow = work[0:1, 768:1024]
        t2row = work[0:1, 1024:1280]
        g1 = wreg[:, 0:512].rearrange("p (c n) -> p c n", c=2)
        c1row = bias_rows[:, D:2 * D]
        fc1 = wreg[:, 512:2048].rearrange("p (c n) -> p c n", c=2)
        fc2 = wreg[:, 2048:3584].rearrange("p (k n) -> p k n", n=D)
        lng, lnb, fb1 = wreg[:, 3584:3586], wreg[:, 3586:3588], wreg[:, 3588:3594]
        with nc.Block() as block:
            s_w, s_v, s_p, s_a, s_z3 = (sem("i_" + n) for n in "w v p a z".split())

            @block.sync
            def _(sp):
                sp.dma_start(wqkv, A["L1_mix_w_qkv"].rearrange("(c p) n -> p c n", p=P)).then_inc(s_w, 16)
                sp.dma_start(bqkv, A["L1_mix_b_qkv"].rearrange("(a n) -> a n", a=1)).then_inc(s_w, 16)
                sp.dma_start(bqc, A["L1_mix_b_qkv"][0:D].rearrange("(c p) -> p c", p=P), allow_slow_non_contiguous=True).then_inc(s_w, 16)
                sp.dma_start(fc1, A["L1_mix_w_fc1"].rearrange("(c p) n -> p c n", p=P)).then_inc(s_w, 16)
                sp.dma_start(fc2, A["L1_mix_w_fc2"].rearrange("(k p) n -> p k n", p=P)).then_inc(s_w, 16)
                sp.dma_start(lng, A["L1_mix_norm_g"].rearrange("(c p) -> p c", p=P), allow_slow_non_contiguous=True).then_inc(s_w, 16)
                sp.dma_start(lnb, A["L1_mix_norm_b"].rearrange("(c p) -> p c", p=P), allow_slow_non_contiguous=True).then_inc(s_w, 16)
                sp.dma_start(fb1, A["L1_mix_b_fc1"].rearrange("(k p) -> p k", p=P), allow_slow_non_contiguous=True).then_inc(s_w, 16)
                sp.wait_ge(s_w, 8 * 16)

            @block.gpsimd
            def _(g):
                g.memset(ACC, 0.0).then_inc(s_z3, 1)
                g.memset(rows[:, 3072:3328], 0.0).then_inc(s_z3, 1)
                g.memset(nval, float(N)).then_inc(s_z3, 1)

            @block.scalar
            def _(a):
                a.wait_ge(s_v, 13)
                for c in range(2):
                    a.activation(att[:, c, :], att[:, c, :], ACT.Exp, bias=nmx[:, c:c + 1], scale=64.0 ** -0.5).then_inc(s_a, 1)

            @block.tensor
            def _(pe):
                pe.wait_ge(s_w, 8 * 16)
                pe.wait_ge(s_z3, 3)
                pe.wait_ge(s_v, 4)
                for c in range(2):
                    pe.matmul(ps[0][0:1, c * P:(c + 1) * P], csum[:, c:c + 1], ident[:, :], start=True, stop=True).then_inc(s_p, 1)
                pe.wait_ge(s_v, 5)
                for m in range(2):
                    for c in range(2):
                        pe.matmul(ps[1][:, m * D:(m + 1) * D], gram[:, c, m * P:(m + 1) * P], wqkv[:, c, 2 * D:3 * D], start=c == 0, stop=False)
                    pe.matmul(ps[1][:, m * D:(m + 1) * D], crow[:, m * P:(m + 1) * P], bqkv[:, 2 * D:3 * D], start=False, stop=True).then_inc(s_p, 1)
                for c in range(2):
                    pe.matmul(ps[2][0:1, 0:D], csum[:, c:c + 1], wqkv[:, c, 2 * D:3 * D], start=c == 0, stop=False)
                pe.matmul(ps[2][0:1, 0:D], nval, bqkv[:, 2 * D:3 * D], start=False, stop=True).then_inc(s_p, 1)
                pe.wait_ge(s_v, 7)
                for m in range(2):
                    for c in range(2):
                        pe.matmul(ps[3][:, m * D:(m + 1) * D], wqkv[:, c, D + m * P:D + (m + 1) * P], t1[:, c, :], start=c == 0, stop=False)
                    pe.matmul(ps[3][:, m * D:(m + 1) * D], bqkv[:, D + m * P:D + (m + 1) * P], t2row, start=False, stop=True).then_inc(s_p, 1)
                for m in range(2):
                    for c in range(2):
                        ins = pe.transpose(ps[4][:, m * D + c * P:m * D + (c + 1) * P], wqkv[:, c, m * P:(m + 1) * P], ident[:, :])
                ins.then_inc(s_p, 1)
                pe.wait_ge(s_v, 21)
                for m in range(2):
                    pe.transpose(ps[5][:, m * P:(m + 1) * P], abd[:, m, :], ident[:, :]).then_inc(s_p, 1)
                pe.wait_ge(s_v, 22)
                for rr in range(2):
                    for m in range(2):
                        pe.matmul(ps[6][:, rr * D + m * P:rr * D + (m + 1) * P], wq1T[:, m, rr * P:(rr + 1) * P], abT[:, m, :],
                                  start=True, stop=True).then_inc(s_p, 1)
                for m in range(2):
                    pe.wait_ge(s_v, 23 + 2 * m)
                    pe.matmul(ps[2][:, m * P:(m + 1) * P], bqm, abT[:, m, :], start=True, stop=True).then_inc(s_p, 1)

            @block.vector
            def _(v):
                link = Chain(v, s_v)
                for c in range(2):
                    link(v.tensor_copy(gram[:, c, :], ps[5 + c][:, 0:D]))
                    link(v.tensor_copy(csum[:, c:c + 1], ps[5 + c][:, D:D + 1]))
                v.wait_ge(s_p, 2)
                link(v.tensor_copy(crow, ps[0][0:1, 0:D]))
                v.wait_ge(s_p, 5)
                link(v.tensor_copy(rows[:, 2048:2560], ps[1][:, :]))
                link(v.tensor_copy(t2row, ps[2][0:1, 0:D]))
                v.wait_ge(s_p, 7)
                for m in range(2):
                    link(v.tensor_copy(att[0:64, m, :], ps[3][0:64, m * D + 2 * m * 64:m * D + (2 * m + 1) * 64]))
                    link(v.tensor_copy(att[64:128, m, :], ps[3][64:128, m * D + (2 * m + 1) * 64:m * D + (2 * m + 2) * 64]))
                link(v.tensor_reduce(nmx, att, AX.X, ALU.max, negate=True))
                link(v.tensor_scalar(nmx, nmx, 64.0 ** -0.5, None, ALU.mult))
                v.wait_ge(s_p, 8)
                link(v.tensor_copy(rows[:, 2560:3072], ps[4][:, :]))
                v.wait_ge(s_a, 2)
                link(v.tensor_reduce(rsm, att, AX.X, ALU.add))
                link(v.reciprocal(rsm, rsm))
                v.wait_ge(s_z3, 3)
                link(v.tensor_scalar(bqm, bqc[:, 0:1].broadcast_to([P, P]), 1.0, None, ALU.mult))
                for m in range(2):
                    for q in range(2):
                        rr = slice(64 * q, 64 * q + 64)
                        link(v.tensor_scalar(abd[rr, m, rr], att[rr, m, :], rsm[rr, m:m + 1], None, ALU.mult))
                v.wait_ge(s_p, 10)
                link(v.tensor_copy(rows[:, 3328:3584], ps[5][:, 0:D]))
                v.wait_ge(s_p, 14)
                link(v.tensor_copy(wreg[:, 0:512], ps[6][:, :]))
                v.wait_ge(s_p, 15)
                link(v.tensor_scalar(bqm, bqc[:, 1:2].broadcast_to([P, P]), 1.0, None, ALU.mult))
                link(v.tensor_copy(c1row[:, 0:P], ps[2][:, 0:P]))
                v.wait_ge(s_p, 16)
                link(v.tensor_copy(c1row[:, P:D], ps[2][:, P:D]))

        aggregate(2, table[2])

        yt = [work[:, 1024 + b * D:1024 + (b + 1) * D] for b in range(2)]
        ht = [work[:, 1536 + b * D:1536 + (b + 1) * D] for b in range(2)]
        hT1 = [rows[:, b * D:(b + 1) * D] for b in range(2)]
        uT = [rows[:, 512 + b * 768:512 + (b + 1) * 768] for b in range(2)]
        mw = [newton[:, 8 * b:8 * b + 8] for b in range(2)]
        with nc.Block() as block:
            row, xc, tp, xt, gm, y, ln, t2, hx, f1, gl, f2, o, ry = steps("j_", "row xc tp xt gm y ln t2 hx f1 gl f2 o ry")
            s_c = sem("j_chain")

            @block.gpsimd
            def _(g):
                start(g, xc, ry)

                def g_xc(t, b):
                    g.wait_ge(*row.after(t))
                    g.tensor_tensor(XN[:, col(t)], XN[:, col(t)], c1row, ALU.add).then_inc(xc.sem, 1)

                def g_ry(t, b):
                    g.wait_ge(*y.after(t))
                    g.tensor_tensor(R[:, col(t)], R[:, col(t)], yt[b], ALU.add).then_inc(ry.sem, 1)
                tiles(g, (g_xc, 0), (g_ry, 0))

            @block.scalar
            def _(a):
                start(a, row, hx, gl)

                def a_row(t, b):
                    a.wait_ge(*tp.room(t))
                    a.copy(xrow[b], XN[:, col(t)]).then_inc(row.sem, 1)

                def a_hx(t, b):
                    a.wait_ge(*t2.after(t))
                    a.wait_ge(*f1.room(t))
                    for c in range(2):
                        ins = a.activation(hT1[b][:, c * P:(c + 1) * P], ps[1][:, c * P:(c + 1) * P], ACT.Identity,
                                           bias=lnb[:, c:c + 1], scale=lng[:, c:c + 1])
                    ins.then_inc(hx.sem, 1)

                def a_gl(t, b):
                    a.wait_ge(*f1.after(t))
                    a.wait_ge(*f2.room(t))
                    for k in range(6):
                        ins = a.activation(uT[b][:, k * P:(k + 1) * P], ps[4 + 2 * b + k // 4][:, k % 4 * P:(k % 4 + 1) * P], ACT.Gelu,
                                           bias=fb1[:, k:k + 1])
                    ins.then_inc(gl.sem, 1)
                tiles(a, (a_row, 0), (a_gl, 2), (a_hx, 1))

            @block.tensor
            def _(pe):
                start(pe, tp, gm, t2, f1, f2)

                def p_tp(t, b):
                    pe.wait_ge(*row.after(t))
                    pe.wait_ge(*xt.after(t - 1))
                    pe.transpose(ps[0][:, 0:P], xrow[b][:, 0:P], ident[:, :])
                    pe.transpose(ps[0][:, P:D], xrow[b][:, P:D], ident[:, :]).then_inc(tp.sem, 1)

                def p_gm(t, b):
                    pe.wait_ge(*xt.after(t))
                    pe.wait_ge(*y.after(t - 1))
                    for c in range(2):
                        ins = pe.matmul(ps[2][:, 0:D], xT[b][:, c * P:(c + 1) * P], g1[:, c, :], start=c == 0, stop=c == 1)
                    ins.then_inc(gm.sem, 1)

                def p_t2(t, b):
                    pe.wait_ge(*ln.after(t))
                    pe.wait_ge(*hx.after(t - 1))
                    pe.transpose(ps[1][:, 0:P], ht[b][:, 0:P], ident[:, :])
                    pe.transpose(ps[1][:, P:D], ht[b][:, P:D], ident[:, :]).then_inc(t2.sem, 1)

                def p_f1(t, b):
                    pe.wait_ge(*hx.after(t))
                    pe.wait_ge(*gl.room(t))
                    for k in range(6):
                        for c in range(2):
                            ins = pe.matmul(ps[4 + 2 * b + k // 4][:, k % 4 * P:(k % 4 + 1) * P], fc1[:, c, k * P:(k + 1) * P],
                                            hT1[b][:, c * P:(c + 1) * P], start=c == 0, stop=c == 1)
                    ins.then_inc(f1.sem, 1)

                def p_f2(t, b):
                    pe.wait_ge(*gl.after(t))
                    pe.wait_ge(*o.after(t - 1))
                    for k in range(6):
                        ins = pe.matmul(ps[3][:, 0:D], uT[b][:, k * P:(k + 1) * P], fc2[:, k, :], start=k == 0, stop=k == 5)
                    ins.then_inc(f2.sem, 1)
                tiles(pe, (p_tp, 0), (p_t2, 1), (p_gm, 0), (p_f2, 2), (p_f1, 1))

            @block.vector
            def _(v):
                start(v, xt, y, ln, o)
                chain = Chain(v, s_c, 24)

                def v_xt(t, b):
                    v.wait_ge(*tp.after(t))
                    v.wait_ge(*gm.room(t))
                    v.tensor_copy(xT[b], ps[0][:, 0:D]).then_inc(xt.sem, 1)

                def v_y(t, b):
                    v.wait_ge(*gm.after(t))
                    v.wait_ge(*xc.after(t))
                    v.wait_ge(*ry.room(t))
                    v.tensor_tensor(yt[b], XN[:, col(t)], ps[2][:, 0:D], ALU.add).then_inc(y.sem, 1)

                def v_ln(t, b):
                    chain.tile(t)
                    m = mw[b]
                    v.wait_ge(*y.after(t))
                    chain(v.bn_stats(stats[:, :], yt[b]))
                    chain(v.tensor_scalar(m[:, 0:1], stats[:, 1:2], stats[:, 4:5], 0.5, ALU.add, ALU.mult))
                    chain(v.tensor_scalar(m[:, 1:2], stats[:, 1:2], stats[:, 4:5], 0.5, ALU.subtract, ALU.mult))
                    chain(v.tensor_scalar(m[:, 2:3], stats[:, 2:3], stats[:, 5:6], 1.0 / D, ALU.add, ALU.mult))
                    chain(v.scalar_tensor_tensor(m[:, 2:3], m[:, 1:2], m[:, 1:2], m[:, 2:3], ALU.mult, ALU.add))
                    chain(v.tensor_scalar(m[:, 2:3], m[:, 2:3], EPS, None, ALU.add))
                    rsqrt(v, chain, m[:, 2:3], m[:, 3:4], m[:, 4:5], 1)
                    v.wait_ge(*t2.room(t))
                    v.tensor_scalar(ht[b], yt[b], m[:, 0:1], m[:, 3:4], ALU.subtract, ALU.mult).then_inc(ln.sem, 1)

                def v_o(t, b):
                    v.wait_ge(*f2.after(t))
                    v.wait_ge(*ry.after(t))
                    v.tensor_tensor(R[:, col(t)], R[:, col(t)], ps[3][:, 0:D], ALU.add).then_inc(o.sem, 1)
                tiles(v, (v_xt, 0), (v_y, 0), (v_o, 2), (v_ln, 0))

        gw = wreg[:, 0:8].rearrange("p (c n) -> p c n", c=2)
        gbr = wreg[:, 8:12]
        with nc.Block() as block:
            s_r, s_sl, s_n, s_w9 = sem("k_r"), sem("k_sl"), sem("k_n"), sem("k_w")

            @block.sync
            def _(sp):
                sp.dma_start(gw, A["L1_ffn_gW"].rearrange("(c p) n -> p c n", p=P)).then_inc(s_w9, 16)
                load_bias(sp, gbr, A["L1_ffn_gb"], s_w9)
                sp.wait_ge(s_w9, 32)

            @block.vector
            def _(v):
                with v.Fori(0, T) as i:
                    v.scalar_tensor_tensor(R[:, col(i)], ACC[:, col(i)], invdeg[:, bass.ds(i, 1)], R[:, col(i)], ALU.mult,
                                           ALU.add).then_inc(s_r, 1)
                v.wait_ge(s_r, T)
                row_stats(v, R, s_sl)
                norm_factors(v, Chain(v, s_n))

        NG = 4
        lgt = gate[:, 0:T * NG].rearrange("p (t e) -> p t e", e=NG)
        with nc.Block() as block:
            row, tp, xt, gt, gc, wr = steps("l_", "row tp xt gt gc wr")

            @block.gpsimd
            def _(g):
                start(g, wr)

                def g_wr(t, b):
                    g.wait_ge(*xt.after(t))
                    g.tensor_copy(XN[:, col(t)], xT[b]).then_inc(wr.sem, 1)
                tiles(g, (g_wr, 0))

            @block.scalar
            def _(a):
                start(a, row)

                def a_row(t, b):
                    a.wait_ge(*tp.room(t))
                    a.activation(xrow[b], R[:, col(t)], ACT.Identity, bias=nmr[:, bass.ds(t, 1)],
                                 scale=rstd[:, bass.ds(t, 1)]).then_inc(row.sem, 1)
                tiles(a, (a_row, 0))

            @block.tensor
            def _(pe):
                start(pe, tp, gt)

                def p_tp(t, b):
                    pe.wait_ge(*row.after(t))
                    pe.wait_ge(*xt.room(t))
                    pe.transpose(ps[b][:, 0:P], xrow[b][:, 0:P], ident[:, :])
                    pe.transpose(ps[b][:, P:D], xrow[b][:, P:D], ident[:, :]).then_inc(tp.sem, 1)

                def p_gt(t, b):
                    pe.wait_ge(*xt.after(t))
                    pe.wait_ge(*gc.room(t))
                    for c in range(2):
                        ins = pe.matmul(ps[2 + b][:, 0:NG], xT[b][:, c * P:(c + 1) * P], gw[:, c, :], start=c == 0, stop=c == 1)
                    ins.then_inc(gt.sem, 1)
                tiles(pe, (p_tp, 0), (p_gt, 1))

            @block.vector
            def _(v):
                start(v, xt, gc)

                def v_xt(t, b):
                    v.wait_ge(*tp.after(t))
                    v.wait_ge(*gt.room(t))
                    v.wait_ge(*wr.room(t))
                    v.tensor_copy(xT[b], ps[b][:, 0:D]).then_inc(xt.sem, 1)

                def v_gc(t, b):
                    v.wait_ge(*gt.after(t))
                    v.tensor_tensor(gate[:, bass.ds(t * NG, NG)], ps[2 + b][:, 0:NG], gbr, ALU.add).then_inc(gc.sem, 1)
                tiles(v, (v_xt, 0), (v_gc, 1))

        sw1 = wreg[:, 0:512].rearrange("p (c n) -> p c n", c=2)
        sw2 = wreg[:, 512:768].rearrange("p (c n) -> p c n", c=2)
        sw3 = wreg[:, 768:1024]
        ew1 = wreg[:, 1024:2048].rearrange("p (e c n) -> p e c n", e=NG, c=2)
        ew2 = wreg[:, 2048:2560].rearrange("p (e n) -> p e n", n=P)
        ew3 = wreg[:, 2560:3072].rearrange("p (q n) -> p q n", n=D)
        sb1c, eb1c, sb2c, eb2c = wreg[:, 3072:3074], wreg[:, 3074:3078], wreg[:, 3078:3079], wreg[:, 3079:3081]
        bend = wreg[0:NG + 1, 3328:3584]
        with nc.Block() as block:
            s_v, s_a, s_w, s_z5 = sem("m_v"), sem("m_a"), sem("m_w"), sem("m_z")
            mxg, sm, rk, t_a, t_b = gsml[:, 0:T], gsml[:, T:2 * T], newton[:, 0:T], gtmp[:, 200:200 + T], gtmp[:, 250:250 + T]
            rank = gtmp[:, 0:T * NG].rearrange("p (t e) -> p t e", e=NG)

            @block.gpsimd
            def _(g):
                g.memset(wreg[:, 2048:2560], 0.0).then_inc(s_z5, 1)

            @block.sync
            def _(sp):
                def ld(dst, src, slow=False):
                    sp.dma_start(dst, src, allow_slow_non_contiguous=slow).then_inc(s_w, 16)
                ld(sw1, A["L1_ffn_sW1"].rearrange("(c p) n -> p c n", p=P))
                ld(sw2, A["L1_ffn_sW2"].rearrange("(c p) n -> p c n", p=P))
                ld(sw3, A["L1_ffn_sW3"])
                for e in range(NG):
                    ld(ew1[:, e, :, :], A["L1_ffn_eW1"][e].rearrange("(c p) n -> p c n", p=P))
                    ld(ew3[64 * (e % 2):64 * (e % 2) + 64, e // 2, :], A["L1_ffn_eW3"][e])
                    ld(eb2c[64 * (e % 2):64 * (e % 2) + 64, e // 2:e // 2 + 1], A["L1_ffn_eb2"][e].rearrange("(p a) -> p a", a=1), slow=True)
                sp.wait_ge(s_z5, 1)
                for e in range(NG):
                    ld(ew2[:, e, 64 * (e % 2):64 * (e % 2) + 64], A["L1_ffn_eW2"][e])
                ld(sb1c, A["L1_ffn_sb1"].rearrange("(c p) -> p c", p=P), slow=True)
                ld(eb1c, A["L1_ffn_eb1"].rearrange("e p -> p e"), slow=True)
                ld(sb2c, A["L1_ffn_sb2"].rearrange("(p a) -> p a", a=1), slow=True)
                ld(bend[0:NG], A["L1_ffn_eb3"])
                ld(bend[NG:NG + 1], A["L1_ffn_sb3"].rearrange("(a n) -> a n", a=1))
                sp.wait_ge(s_w, (3 + 3 * NG + NG + 5) * 16)

            @block.scalar
            def _(a):
                a.wait_ge(s_v, 2)
                a.activation(lgt, lgt, ACT.Exp).then_inc(s_a, 1)
                a.wait_ge(s_v, 42)
                a.activation(rank, rank, ACT.Exp).then_inc(s_a, 1)

            @block.vector
            def _(v):
                link = Chain(v, s_v)
                link(v.tensor_reduce(mxg, lgt, AX.X, ALU.max))
                link(v.tensor_tensor(lgt, lgt, wide(mxg, NG), ALU.subtract))
                v.wait_ge(s_a, 1)
                link(v.tensor_reduce(sm, lgt, AX.X, ALU.add))
                link(v.reciprocal(sm, sm))
                link(v.tensor_tensor(lgt, lgt, wide(sm, NG), ALU.mult))
                for e in range(NG):
                    first = True
                    for j in range(NG):
                        if j == e:
                            continue
                        dst = rank[:, :, e] if first else t_a
                        link(v.tensor_tensor(dst, lgt[:, :, j], lgt[:, :, e], ALU.is_ge if j < e else ALU.is_gt))
                        if not first:
                            link(v.tensor_tensor(rank[:, :, e], rank[:, :, e], t_a, ALU.add))
                        first = False
                link(v.tensor_reduce(mxg, lgt, AX.X, ALU.max))
                for e in range(NG):
                    link(v.tensor_scalar(rank[:, :, e], rank[:, :, e], 2.0, None, ALU.is_lt))
                    link(v.tensor_tensor(lgt[:, :, e], lgt[:, :, e], mxg, ALU.subtract))
                for e in range(NG):
                    link(v.tensor_copy(gate[:, 200 + e * T:200 + (e + 1) * T] if e < 3 else newton[:, T:2 * T], rank[:, :, e]))
                for e in range(NG):
                    link(v.tensor_copy(rank[:, :, e], lgt[:, :, e]))
                v.wait_ge(s_a, 2)
                for e in range(NG):
                    sel = gate[:, 200 + e * T:200 + (e + 1) * T] if e < 3 else newton[:, T:2 * T]
                    link(v.tensor_tensor(rank[:, :, e], rank[:, :, e], sel, ALU.mult))
                link(v.tensor_reduce(sm, rank, AX.X, ALU.add))
                link(v.reciprocal(sm, sm))
                link(v.tensor_tensor(lgt, rank, wide(sm, NG), ALU.mult))

        wst = [small[:, 8 * b:8 * b + NG + 1] for b in range(2)]
        wT = [small[0:NG + 1, 64 + b * P:64 + (b + 1) * P] for b in range(2)]
        a1 = [rows[:, b * 768:(b + 1) * 768] for b in range(2)]
        a2 = [rows[:, 1536 + b * 384:1536 + (b + 1) * 384] for b in range(2)]
        with nc.Block() as block:
            l1, r1, l2, r2, l3, wc, wt, wtc, ad = steps("n_", "l1 r1 l2 r2 l3 wc wt wtc ad")
            s_o, s_c, s_one = sem("n_out"), sem("n_chain"), sem("n_one")

            @block.sync
            def _(sp):
                with sp.Fori(0, T - 1) as i:
                    sp.wait_ge(*ad.after(i))
                    sp.dma_start(out[bass.ds(i * P, P), :], R[:, bass.ds(i * D, D)]).then_inc(s_o, 16)
                sp.wait_ge(*ad.after(T - 1))
                sp.dma_start(out[(T - 1) * P:N, :], R[0:LAST, (T - 1) * D:T * D]).then_inc(s_o, 16)
                sp.wait_ge(s_o, T * 16)

            @block.scalar
            def _(a):
                start(a, r1, r2)

                def a_r1(t, b):
                    a.wait_ge(*l1.after(t))
                    a.wait_ge(*l2.room(t))
                    for k in range(6):
                        bias = sb1c[:, k:k + 1] if k < 2 else eb1c[:, k - 2:k - 1]
                        ins = a.activation(a1[b][:, k * P:(k + 1) * P], ps[k // 4][:, k % 4 * P:(k % 4 + 1) * P], ACT.Relu, bias=bias)
                    ins.then_inc(r1.sem, 1)

                def a_r2(t, b):
                    a.wait_ge(*l2.after(t))
                    a.wait_ge(*l3.room(t))
                    for k in range(3):
                        bias = sb2c if k < 1 else eb2c[:, k - 1:k]
                        ins = a.activation(a2[b][:, k * P:(k + 1) * P], ps[2][:, k * P:(k + 1) * P], ACT.Relu, bias=bias)
                    ins.then_inc(r2.sem, 1)
                tiles(a, (a_r1, 0), (a_r2, 0))

            @block.tensor
            def _(pe):
                start(pe, l1, l2, l3, wt)

                def p_l1(t, b):
                    pe.wait_ge(*r1.after(t - 1))
                    for k in range(6):
                        for c in range(2):
                            w = sw1[:, c, k * P:(k + 1) * P] if k < 2 else ew1[:, k - 2, c, :]
                            ins = pe.matmul(ps[k // 4][:, k % 4 * P:(k % 4 + 1) * P], w, XN[:, bass.ds(t * D + c * P, P)],
                                            start=c == 0, stop=c == 1)
                    ins.then_inc(l1.sem, 1)

                def p_l2(t, b):
                    pe.wait_ge(*r1.after(t))
                    pe.wait_ge(*r2.after(t - 1))
                    for c in range(2):
                        pe.matmul(ps[2][:, 0:P], sw2[:, c, :], a1[b][:, c * P:(c + 1) * P], start=c == 0, stop=c == 1)
                    for e in range(NG):
                        ins = pe.matmul(ps[2][:, (1 + e // 2) * P:(2 + e // 2) * P], ew2[:, e, :], a1[b][:, (2 + e) * P:(3 + e) * P],
                                        start=e % 2 == 0, stop=e % 2 == 1)
                    ins.then_inc(l2.sem, 1)
                    pe.wait_ge(*wc.after(t))
                    pe.wait_ge(*wtc.room(t))
                    pe.transpose(ps[6 + b][0:NG + 1, 0:P], wst[b], ident[:, :]).then_inc(wt.sem, 1)

                def p_l3(t, b):
                    pe.wait_ge(*r2.after(t))
                    pe.wait_ge(*ad.after(t - 1))
                    for e in range(NG):
                        q = slice(64 * (e % 2), 64 * (e % 2) + 64)
                        pe.matmul(ps[3 + e % 2][:, e // 2 * D:(e // 2 + 1) * D], a2[b][q, (1 + e // 2) * P:(2 + e // 2) * P], ew3[q, e // 2, :],
                                  start=True, stop=True)
                    pe.matmul(ps[5][:, 0:D], a2[b][:, 0:P], sw3, start=True, stop=False)
                    pe.wait_ge(*wtc.after(t))
                    pe.matmul(ps[5][:, 0:D], wT[b], bend, start=False, stop=True).then_inc(l3.sem, 1)
                tiles(pe, (p_l1, 0), (p_l3, 1), (p_l2, 0))

            @block.vector
            def _(v):
                start(v, wc, wtc, ad)
                chain = Chain(v, s_c, NG)
                for b in range(2):
                    v.memset(wst[b][:, NG:NG + 1], 1.0).then_inc(s_one, 1)

                def v_w(t, b):
                    v.wait_ge(*wt.room(t))
                    v.tensor_copy(wst[b][:, 0:NG], gate[:, bass.ds(t * NG, NG)]).then_inc(wc.sem, 1)

                def v_wt(t, b):
                    v.wait_ge(*wt.after(t))
                    v.wait_ge(*l3.room(t))
                    v.tensor_copy(wT[b], ps[6 + b][0:NG + 1, 0:P]).then_inc(wtc.sem, 1)

                def v_ad(t, b):
                    v.wait_ge(*l3.after(t))
                    chain.tile(t)
                    x = R[:, col(t)]
                    chain(v.tensor_tensor(x, x, ps[5][:, 0:D], ALU.add))
                    for e in range(NG):
                        ins = v.scalar_tensor_tensor(x, ps[3 + e % 2][:, e // 2 * D:(e // 2 + 1) * D], gate[:, bass.ds(t * NG + e, 1)], x,
                                                     ALU.mult, ALU.add)
                        if e < NG - 1:
                            chain(ins)
                        else:
                            ins.then_inc(ad.sem, 1)
                tiles(v, (v_w, 0), (v_wt, 0), (v_ad, 1))


_INPUTS = ["x", "src", "dst", "L0_gnn_W1", "L0_gnn_b1", "L0_gnn_W2", "L0_gnn_b2", "L0_mix_W_qkv", "L0_mix_W_out", "L0_mix_b_out",
           "L0_ffn_W1", "L0_ffn_b1", "L0_ffn_Wg", "L0_ffn_bg", "L0_ffn_Wd", "L0_ffn_bd", "L1_gnn_W_self", "L1_gnn_W_neigh", "L1_gnn_b",
           "L1_mix_w_qkv", "L1_mix_b_qkv", "L1_mix_norm_g", "L1_mix_norm_b", "L1_mix_w_fc1", "L1_mix_b_fc1", "L1_mix_w_fc2",
           "L1_mix_b_fc2", "L1_ffn_sW1", "L1_ffn_sb1", "L1_ffn_sW2", "L1_ffn_sb2", "L1_ffn_sW3", "L1_ffn_sb3", "L1_ffn_eW1",
           "L1_ffn_eb1", "L1_ffn_eW2", "L1_ffn_eb2", "L1_ffn_eW3", "L1_ffn_eb3", "L1_ffn_gW", "L1_ffn_gb"]


def kernel(**inputs):
    import numpy as np
    import concourse.bacc as bacc
    from concourse.bass_utils import run_bass_kernel_spmd

    nc = bacc.Bacc("TRN2", target_bir_lowering=False, num_devices=1)
    arrays, aps = {}, {}
    for name in _INPUTS:
        a = np.ascontiguousarray(inputs[name])
        arrays["in_" + name] = a
        aps[name] = nc.dram_tensor("in_" + name, a.shape, mybir.dt.from_np(a.dtype), kind="ExternalInput").ap()
    out = nc.dram_tensor("out_x", (N, D), F32, kind="ExternalOutput").ap()
    build(nc, aps, out)
    return run_bass_kernel_spmd(nc, [arrays], core_ids=[0]).results[0]["out_x"]
```

```python
from contextlib import ExitStack

import concourse.bass as bass
from concourse import mybir

F32 = mybir.dt.float32
BF16 = mybir.dt.bfloat16
I32 = mybir.dt.int32
ALU = mybir.AluOpType
ACT = mybir.ActivationFunctionType
AX = mybir.AxisListType

P = 128
N = 6250
D = 256
E = 106250
T = -(-N // P)
LAST = N - (T - 1) * P
CH = -(-E // P)
CHR = 896
KC = CHR // P
PAD_DST = 8191
RING = 16
VIS = -(-(CH + T - 1) // RING) * RING
VI = VIS // RING
VC = CHR // P
HID = 1024
NE = 8
HC = HID // P
REG = (T + 1) * P
JUNK = NE * REG
ZERO = JUNK + P
BLK = (N + NE * (P - 1)) // P
EPS = 1e-5
MAGIC = 1597463007.0


class Chain:

    def __init__(self, eng, sem, per=0):
        self.eng, self.sem, self.per, self.base, self.k = eng, sem, per, 0, 0

    def tile(self, t):
        assert self.k in (0, self.per)
        self.base, self.k = t * self.per, 0
        return self

    def __call__(self, ins):
        self.k += 1
        ins.then_inc(self.sem, 1)
        self.eng.wait_ge(self.sem, self.base + self.k)


class Step:

    def __init__(self, sem, depth=2):
        self.sem, self.depth = sem, depth

    def after(self, t):
        return self.sem, t + 1 + self.depth

    def room(self, t):
        return self.sem, t + 1


def tiles(eng, *parts, n=T, unroll=2):
    def turn(t, b):
        for part, lag in parts:
            if not isinstance(t, int) or 0 <= t - lag < n:
                part(t - lag, (b - lag) % unroll)

    lags = max(lag for _, lag in parts)
    head = max(3, lags) + (n - 2 - max(3, lags)) % unroll
    for t in range(head):
        turn(t, t % unroll)
    with eng.Fori(0, (n - 2 - head) // unroll) as i:
        for q in range(unroll):
            turn(unroll * i + head + q, (head + q) % unroll)
    for t in range(n - 2, n + lags):
        turn(t, t % unroll)


def build(nc, A, out):
    with ExitStack() as ctx:
        def sb(name, shape, dt=F32):
            return ctx.enter_context(nc.sbuf_tensor(name, shape, dt))

        stage_sems = []

        def sem(name, keep=False):
            s = nc.alloc_semaphore(name=name)
            if not keep:
                stage_sems.append(s)
            return s

        def retire_sems():
            nc.clear_and_free_semaphores(list(stage_sems))
            nc.all_engine_barrier()
            stage_sems.clear()

        def dram(name, shape, dt=F32):
            return nc.dram_tensor(name, shape, dt, kind="Internal").ap()

        XN = sb("XN", [P, T * D])
        AR = sb("AR", [P, T * D + T * (D + 1)])
        ACC = AR[:, 0:T * D]
        KV = AR[:, T * D:T * (2 * D + 1)].rearrange("p (t c) -> p t c", c=D + 1)
        KVf = AR[:, T * D:T * (2 * D + 1)]
        R = AR[:, T * D:2 * T * D]
        WD = AR[:, 0:NE * HC * D]
        rows = sb("rows", [P, RING * D])
        wreg = sb("wreg", [P, 3600])
        work = sb("work", [P, 2048])
        mring = sb("mring", [P, 4 * P])
        idx_stage = sb("idx_stage", [P, RING], I32)
        src_idx = sb("src_idx", [P, CHR], I32)
        dst_rel = sb("dst_rel", [P, CHR])
        acc_at = sb("acc_at", [1, CHR], I32)
        ident = sb("ident", [P, P])
        iota = sb("iota", [P, P])
        bias_rows = sb("bias_rows", [P, 2 * D])
        stats = sb("stats", [P, 6])
        mv = sb("mv", [P, T, 6])
        rstd = sb("rstd", [P, T])
        nmr = sb("nmr", [P, T])
        dinv = sb("dinv", [P, T])
        invdeg = sb("invdeg", [P, T])
        deg = sb("deg", [P, T])
        newton = sb("newton", [P, 2 * T])
        gate = sb("gate", [P, T * NE])
        gtmp = sb("gtmp", [P, T * NE])
        gsml = sb("gsml", [P, 2 * T])
        ps = [ctx.enter_context(nc.psum_tensor(f"ps{b}", [P, 512], F32)) for b in range(8)]
        table = [dram(f"table{n}", [T * P, D]) for n in range(3)]
        src_pad, dst_pad = dram("src_pad", [CHR, P], I32), dram("dst_pad", [CHR, P], I32)
        at_dram = dram("at_dram", [CHR], I32)
        h_sorted = dram("h_sorted", [ZERO + P, HID])
        y_sorted = dram("y_sorted", [BLK * P, D])
        pos_f = sb("pos_f", [P, T])
        pos_all = sb("pos_all", [P, T], I32)
        prob = sb("prob", [P, T])
        pos_stage = sb("pos_stage", [P, 2], I32)

        s_pool0 = sem("s_pool0", keep=True)
        s_mm = sem("s_mm", keep=True)
        s_ac = sem("s_ac", keep=True)
        s_m = sem("s_m", keep=True)
        s_st = sem("s_st", keep=True)
        s_go = sem("s_go", keep=True)
        s_g = [sem(f"s_g{u}", keep=True) for u in range(RING)]

        def bc(ap, parts=P):
            return ap.partition_broadcast(parts)

        def loads(engine, ap, most):
            return nc.values_load_multi_w_load_instructions(ap, engines=(engine,), min_val=0, max_val=most)[1]

        def rsqrt(v, link, x, y, t, n):
            yi, ti = y.bitcast(I32), t.bitcast(I32)
            link(v.tensor_scalar(ti, x.bitcast(I32), 1, None, ALU.logical_shift_right))
            link(v.tensor_scalar(yi, ti, -1.0, MAGIC, ALU.mult, ALU.add))
            for _ in range(4):
                link(v.tensor_tensor(t, y, y, ALU.mult))
                link(v.tensor_tensor(t, t, x, ALU.mult))
                link(v.tensor_scalar(t, t, -0.5, 1.5, ALU.mult, ALU.add))
                link(v.tensor_tensor(y, y, t, ALU.mult))

        def row_stats(v, x, s_chain):
            with v.Fori(0, T) as i:
                v.bn_stats(mv[:, bass.ds(i, 1), :].rearrange("p t c -> p (t c)"), x[:, bass.ds(i * D, D)]).then_inc(s_chain, 1)
            v.wait_ge(s_chain, T)

        def norm_factors(v, link, var=newton[:, T:2 * T], tmp=newton[:, 0:T]):
            mean = nmr[:, :]
            link(v.tensor_tensor(tmp, mv[:, :, 1], mv[:, :, 4], ALU.subtract))
            link(v.tensor_tensor(tmp, tmp, tmp, ALU.mult))
            link(v.tensor_tensor(var, mv[:, :, 2], mv[:, :, 5], ALU.add))
            link(v.tensor_scalar(var, var, 1.0 / D, EPS, ALU.mult, ALU.add))
            link(v.scalar_tensor_tensor(var, tmp, 0.25, var, ALU.mult, ALU.add))
            rsqrt(v, link, var, rstd[:, :], tmp, T)
            link(v.tensor_tensor(mean, mv[:, :, 1], mv[:, :, 4], ALU.add))
            link(v.scalar_tensor_tensor(nmr[:, :], mean, -0.5, rstd[:, :], ALU.mult, ALU.mult))

        e_i = KVf[:, 0:2 * KC * P].bitcast(I32).rearrange("p (a k e) -> p a k e", a=2, k=KC)
        e_f = KVf[:, 2000:2000 + KC * P]
        d_t = KVf[:, 3000:3000 + CHR]
        hi_i = KVf[:, 4000:4000 + CHR].bitcast(I32)
        hi = KVf[:, 5000:5000 + CHR]
        lo = KVf[:, 6000:6000 + CHR]
        ones = KVf[:, 7000:7000 + P]
        iota_b = KVf[:, 7200:7200 + P // 2].bitcast(BF16)
        OH = 8
        oh_lo = [rows[:, b * P // 2:(b + 1) * P // 2].bitcast(BF16) for b in range(OH)]
        oh_hi = [rows[:, 1024 + 32 * b:1024 + 32 * (b + 1)].bitcast(BF16) for b in range(OH)]
        with nc.Block() as block:
            s_x, s_e, s_sp, s_cst, s_iota = (sem(n) for n in ("x_in", "e_in", "e_pad", "consts", "iotas"))
            s_ef, s_et, s_oh, s_hm, s_dg = (sem(n) for n in ("ef", "et", "oh", "hm", "dg"))
            s_ds, s_tot, s_cv, s_vr, s_vf, s_vt = (sem(n) for n in ("ds", "tot", "cv", "vr", "vf", "vt"))
            s_at, s_ad, s_v0, s_lnf, s_xn, s_ve, s_sl = (sem(n) for n in ("at", "ad", "v0", "lnf", "xn0", "ve", "sl"))

            @block.sync
            def _(sp):
                sp.wait_ge(s_pool0, 1)
                for a, name in enumerate(("src", "dst")):
                    full = (CH - 1) // P * P
                    e = A[name]
                    sp.dma_start(e_i[:, a, 0:KC - 1, :], e[0:full * P].rearrange("(k p e) -> p k e", p=P, e=P)).then_inc(s_e, 16)
                    sp.dma_start(e_i[0:CH - 1 - full, a, KC - 1, :],
                                 e[full * P:(CH - 1) * P].rearrange("(p e) -> p e", e=P)).then_inc(s_e, 16)
                    sp.dma_start(e_i[CH - 1 - full:CH - full, a, KC - 1, 0:E - (CH - 1) * P],
                                 e[(CH - 1) * P:E].rearrange("(p e) -> p e", p=1)).then_inc(s_e, 16)
                xv = XN[:, :].rearrange("p (t d) -> p t d", d=D)
                for q in range(4):
                    sp.dma_start(xv[:, 12 * q:12 * q + 12, :],
                                 A["x"][12 * q * P:12 * (q + 1) * P, :].rearrange("(t p) d -> p t d", p=P)).then_inc(s_x, 16)
                sp.dma_start(xv[0:LAST, T - 1, :], A["x"][(T - 1) * P:N, :]).then_inc(s_x, 16)
                sp.wait_ge(s_e, 6 * 16)
                sp.dma_start(src_pad.rearrange("(k p) e -> p k e", p=P), e_i[:, 0, :, :]).then_inc(s_sp, 16)
                sp.dma_start(dst_pad.rearrange("(k p) e -> p k e", p=P), e_i[:, 1, :, :]).then_inc(s_sp, 16)
                sp.wait_ge(s_at, 1)
                sp.dma_start(at_dram.rearrange("(k p) -> p k", p=P), gtmp[:, 0:VC].bitcast(I32), allow_slow_non_contiguous=True).then_inc(s_ad, 16)
                sp.wait_ge(s_ad, 16)
                sp.dma_start(acc_at[0:1, :], at_dram.rearrange("(a n) -> a n", a=1)).then_inc(s_ad, 16)
                sp.wait_ge(s_ad, 32)

            @block.gpsimd
            def _(g):
                g.memset(e_i[:, 0, :, :], 0).then_inc(s_cst, 1)
                g.memset(e_i[:, 1, :, :], PAD_DST).then_inc(s_cst, 1)
                g.memset(XN[:, (T - 1) * D:T * D], 0.0).then_inc(s_cst, 1)
                g.wait_ge(s_cst, 3)
                g.sem_inc(s_pool0, 1)
                g.memset(ident[:, :], 0.0).then_inc(s_cst, 1)
                g.memset(ones[:, :], 1.0).then_inc(s_cst, 1)
                g.wait_ge(s_cst, 5)
                g.affine_select(out=ident[:, :], in_=ident[:, :], compare_op=ALU.not_equal, fill=1.0, base=0,
                                pattern=[[-1, P]], channel_multiplier=1).then_inc(s_cst, 1)
                iv = idx_stage[:, 0:VC]
                g.iota(hi_i[:, 0:P], pattern=[[1, P]], base=0, channel_multiplier=0).then_inc(s_iota, 1)
                g.iota(iv, pattern=[[P, VC]], base=0, channel_multiplier=1).then_inc(s_iota, 1)
                g.wait_ge(s_sp, 32)
                g.wait_ge(s_cv, 1)
                for k in range(VC):
                    for a, pad in enumerate((src_pad, dst_pad)):
                        g.indirect_dma_start(out=e_i[:, a, k, :], out_offset=None, in_=pad,
                                             in_offset=bass.IndirectOffsetOnAxis(ap=newton[:, k:k + 1].bitcast(I32), axis=0)
                                             ).then_inc(s_vr, 16)

            @block.scalar
            def _(a):
                a.wait_ge(s_lnf, 1)
                with a.Fori(0, T) as i:
                    x = XN[:, bass.ds(i * D, D)]
                    a.activation(x, x, ACT.Identity, bias=nmr[:, bass.ds(i, 1)], scale=rstd[:, bass.ds(i, 1)]).then_inc(s_xn, 1)

            @block.tensor
            def _(pe):
                pe.sem_inc(s_mm, RING)
                pe.wait_ge(s_cst, 6)
                pe.wait_ge(s_ef, 1)
                for k in range(KC):
                    pe.transpose(ps[k // 4][:, k % 4 * P:k % 4 * P + P], e_f[:, k * P:(k + 1) * P], ident[:, :]).then_inc(s_et, 1)
                pe.sem_inc(s_hm, OH)
                for u in range(OH):
                    pe.wait_ge(s_oh, 2 * u + 2)
                    pe.matmul(ps[2][:, 0:T], oh_lo[u][:, :], oh_hi[u][:, 0:T], start=(u == 0), stop=False, skip_group_check=True).then_inc(s_hm, 1)
                with pe.Fori(1, CHR // OH - 8) as i:
                    for u in range(OH):
                        pe.wait_ge(s_oh, 2 * OH * i + 2 * u + 2)
                        pe.matmul(ps[2][:, 0:T], oh_lo[u][:, :], oh_hi[u][:, 0:T], start=False, stop=False, skip_group_check=True).then_inc(s_hm, 1)
                pe.wait_ge(s_ds, 1)
                pe.matmul(ps[3][:, 0:T], ones[:, :], deg[:, :], start=True, stop=True).then_inc(s_tot, 1)
                for k in range(VC):
                    pe.wait_ge(s_vf, 2 * k + 2)
                    if k >= 2:
                        pe.wait_ge(s_ve, 2 * k - 2)
                    for a in range(2):
                        pe.transpose(ps[4 + k % 2][:, a * P:a * P + P], work[:, (2 * (k % 2) + a) * P:(2 * (k % 2) + a + 1) * P],
                                     ident[:, :]).then_inc(s_vt, 1)

            @block.vector
            def _(v):
                link = Chain(v, s_v0)
                v.sem_inc(s_ac, 4)
                v.wait_ge(s_iota, 2)
                link(v.tensor_copy(iota[:, :], hi_i[:, 0:P]))
                link(v.tensor_copy(iota_b[:, :], iota[:, :]))
                vf = gtmp[:, 8:8 + VC]
                link(v.tensor_copy(vf, idx_stage[:, 0:VC]))
                v.wait_ge(s_e, 6 * 16)
                v.tensor_copy(e_f, e_i[:, 1, :, :].rearrange("p k e -> p (k e)")).then_inc(s_ef, 1)
                v.wait_ge(s_et, KC)
                d_i = e_f.bitcast(I32)
                for h in range(2):
                    n = min(512, CHR - 512 * h)
                    link(v.tensor_copy(d_t[:, 512 * h:512 * h + n], ps[h][:, 0:n]))
                    link(v.tensor_copy(d_i[:, 512 * h:512 * h + n], ps[h][:, 0:n]))
                link(v.tensor_scalar(hi_i, d_i, 7, None, ALU.arith_shift_right))
                link(v.tensor_copy(hi, hi_i))
                link(v.scalar_tensor_tensor(lo, hi, -float(P), d_t, ALU.mult, ALU.add))
                with v.Fori(0, CHR // OH - 8) as i:
                    for u in range(OH):
                        v.wait_ge(s_hm, OH * i + u + 1)
                        c = OH * i + u
                        v.tensor_scalar(oh_lo[u][:, :], iota_b[:, :], lo[:, bass.ds(c, 1)], None, ALU.is_equal).then_inc(s_oh, 1)
                        v.tensor_scalar(oh_hi[u][:, 0:T], iota_b[:, 0:T], hi[:, bass.ds(c, 1)], None, ALU.is_equal).then_inc(s_oh, 1)
                v.wait_ge(s_hm, CHR - 8 * OH + OH)
                link(v.tensor_copy(deg[:, :], ps[2][:, 0:T]))
                v.sem_inc(s_ds, 1)
                t49 = newton[:, T:2 * T]
                link(v.tensor_scalar(t49, deg[:, :], 1.0, None, ALU.add))
                rsqrt(v, link, t49, dinv[:, :], newton[:, 0:T], T)
                link(v.tensor_scalar(t49, deg[:, :], 1.0, None, ALU.max))
                link(v.reciprocal(invdeg[:, :], t49))
                v.wait_ge(s_tot, 1)
                c = [work[:, 1024 + 64 * n:1024 + 64 * n + T] for n in range(8)]
                tot, end, first, last, cnt, vend, dlt, junk = c
                link(v.tensor_copy(tot, ps[3][:, 0:T]))
                link(v.tensor_tensor_scan(end, ones[:, 0:T], tot, 0.0, ALU.mult, ALU.add))
                ji, fi, li = junk.bitcast(I32), first.bitcast(I32), last.bitcast(I32)
                link(v.tensor_tensor(junk, end, tot, ALU.subtract))
                link(v.tensor_copy(fi, junk))
                link(v.tensor_scalar(fi, fi, 7, None, ALU.arith_shift_right))
                link(v.tensor_scalar(li, end, -1.0, None, ALU.add))
                link(v.tensor_scalar(li, li, 7, None, ALU.arith_shift_right))
                link(v.tensor_copy(junk, fi))
                link(v.tensor_copy(cnt, li))
                link(v.tensor_tensor(cnt, cnt, junk, ALU.subtract))
                link(v.tensor_scalar(cnt, cnt, 1.0, None, ALU.add))
                link(v.scalar_tensor_tensor(cnt, tot, 0.0, cnt, ALU.is_gt, ALU.mult))
                link(v.tensor_tensor_scan(vend, ones[:, 0:T], cnt, 0.0, ALU.mult, ALU.add))
                link(v.tensor_tensor(dlt, junk, vend, ALU.subtract))
                link(v.tensor_tensor(dlt, dlt, cnt, ALU.add))
                tv, cd = gtmp[:, 16:16 + VC], gtmp[:, 24:24 + VC]
                for k in range(VC):
                    link(v.tensor_scalar(junk, vend, vf[:, k:k + 1], 0.0, ALU.is_le, ALU.add, accum_out=tv[:, k:k + 1]))
                    link(v.scalar_tensor_tensor(junk, iota[:, 0:T], tv[:, k:k + 1], dlt, ALU.is_equal, ALU.mult,
                                                accum_out=cd[:, k:k + 1]))
                link(v.tensor_tensor(cd, cd, vf, ALU.add))
                link(v.tensor_scalar(newton[:, 0:VC].bitcast(I32), cd, 0.0, CHR - 1.0, ALU.max, ALU.min))
                v.sem_inc(s_cv, 1)
                link(v.tensor_scalar(cd, tv, T - 1.0, float(D), ALU.min, ALU.mult))
                link(v.tensor_copy(gtmp[:, 0:VC].bitcast(I32), cd))
                v.sem_inc(s_at, 1)
                link(v.tensor_scalar(tv, tv, -float(P), None, ALU.mult))
                v.wait_ge(s_x, 5 * 16)
                row_stats(v, XN, s_sl)
                norm_factors(v, link, gsml[:, 0:T], gsml[:, T:2 * T])
                v.sem_inc(s_lnf, 1)
                v.wait_ge(s_vr, 2 * VC * 16)
                for k in range(VC):
                    if k >= 2:
                        v.wait_ge(s_vt, 2 * k - 2)
                    at = 2 * (k % 2) * P
                    v.tensor_copy(work[:, at:at + P], e_i[:, 0, k, :]).then_inc(s_vf, 1)
                    v.tensor_scalar(work[:, at + P:at + 2 * P], e_i[:, 1, k, :], tv[:, k:k + 1], None, ALU.add).then_inc(s_vf, 1)
                    v.wait_ge(s_vt, 2 * k + 2)
                    v.tensor_copy(src_idx[:, k * P:(k + 1) * P], ps[4 + k % 2][:, 0:P]).then_inc(s_ve, 1)
                    v.tensor_copy(dst_rel[:, k * P:(k + 1) * P], ps[4 + k % 2][:, P:2 * P]).then_inc(s_ve, 1)

        def col(t):
            return bass.ds(t * D, D)

        xrow = [work[:, b * D:(b + 1) * D] for b in range(2)]
        xT = [work[:, (2 + b) * D:(3 + b) * D] for b in range(2)]
        small = work[:, 1024:2048]
        bias_ps = ps[7]

        def load_bias(sp, dst, src, s):
            sp.dma_start(dst, src.partition_broadcast(P)).then_inc(s, 16)

        def start(eng, *steps):
            for step in steps:
                eng.sem_inc(step.sem, step.depth)

        def steps(prefix, names):
            return [Step(sem(prefix + n)) for n in names.split()]

        def to_table(sp, n, h, s_tab):
            with sp.Fori(0, T) as i:
                sp.wait_ge(*h.after(i))
                sp.dma_start(table[n][bass.ds(i * P, P), :], ACC[:, bass.ds(i * D, D)]).then_inc(s_tab, 16)
            sp.wait_ge(s_tab, T * 16)

        w1kv = wreg[:, 0:1024].rearrange("p (c n) -> p c n", c=2)
        kmax = small[:, 0:P]
        with nc.Block() as block:
            row, tp, xt, mm, kv, h, mx = steps("a_", "row tp xt mm kv h mx")
            s_w, s_tab, s_km, s_one = sem("a_w"), sem("a_tab"), sem("a_km"), sem("a_one")

            @block.sync
            def _(sp):
                sp.dma_start(w1kv[:, :, 0:D], A["L0_gnn_W1"].rearrange("(c p) n -> p c n", p=P)).then_inc(s_w, 16)
                sp.dma_start(w1kv[:, :, D:2 * D], A["L0_mix_W_qkv"][:, P:3 * P].rearrange("(c p) n -> p c n", p=P)).then_inc(s_w, 16)
                to_table(sp, 0, h, s_tab)

            @block.gpsimd
            def _(g):
                g.memset(KV[:, :, D:D + 1], 1.0).then_inc(s_one, 1)

            @block.scalar
            def _(a):
                start(a, row, xt)

                def a_row(t, b):
                    a.wait_ge(*tp.room(t))
                    a.copy(xrow[b], XN[:, col(t)]).then_inc(row.sem, 1)

                def a_xt(t, b):
                    a.wait_ge(*tp.after(t))
                    a.wait_ge(*mm.room(t))
                    a.copy(xT[b], ps[b][:, 0:D]).then_inc(xt.sem, 1)
                tiles(a, (a_row, 0), (a_xt, 0))

            @block.tensor
            def _(pe):
                start(pe, tp, mm)
                pe.wait_ge(s_w, 32)

                def p_tp(t, b):
                    pe.wait_ge(*row.after(t))
                    pe.wait_ge(*xt.room(t))
                    pe.transpose(ps[b][:, 0:P], xrow[b][:, 0:P], ident[:, :])
                    pe.transpose(ps[b][:, P:D], xrow[b][:, P:D], ident[:, :]).then_inc(tp.sem, 1)

                def p_mm(t, b):
                    pe.wait_ge(*xt.after(t))
                    for s in (kv, h, mx):
                        pe.wait_ge(*s.room(t))
                    pe.matmul(ps[2 + b][:, :], xT[b][:, 0:P], w1kv[:, 0, :], start=True, stop=False)
                    pe.matmul(ps[2 + b][:, :], xT[b][:, P:D], w1kv[:, 1, :], start=False, stop=True).then_inc(mm.sem, 1)
                tiles(pe, (p_tp, 0), (p_mm, 1))

            @block.vector
            def _(v):
                start(v, h, mx, kv)
                v.memset(kmax, -3.0e38).then_inc(s_km, 1)
                v.wait_ge(s_km, 1)

                def v_h(t, b):
                    v.wait_ge(*mm.after(t))
                    v.tensor_scalar(ACC[:, col(t)], ps[2 + b][:, 0:D], dinv[:, bass.ds(t, 1)], None, ALU.mult).then_inc(h.sem, 1)

                def v_mx(t, b):
                    v.wait_ge(*mx.after(t - 1))
                    n = LAST if isinstance(t, int) and t == T - 1 else P
                    v.tensor_tensor(kmax[0:n], kmax[0:n], ps[2 + b][0:n, D:D + P], ALU.max).then_inc(mx.sem, 1)

                def v_kv(t, b):
                    v.tensor_copy(KV[:, bass.ds(t, 1), 0:D].rearrange("p t c -> p (t c)"), ps[2 + b][:, D:2 * D]).then_inc(kv.sem, 1)
                tiles(v, (v_h, 0), (v_mx, 0), (v_kv, 0))

        erow = [small[:, (1 + b) * P:(2 + b) * P] for b in range(2)]
        nmax, nmat = gsml[:, 0:1], small[:, 3 * P:4 * P]
        wq = wreg[:, 0:D].rearrange("p (c n) -> p c n", c=2)
        wout = wreg[:, D:2 * D]
        g0 = wreg[:, 1024:1536].rearrange("p (c n) -> p c n", c=2)
        w2 = wreg[:, 1536:2048].rearrange("p (c n) -> p c n", c=2)
        wqT, m1 = wreg[:, 2048:2304], wreg[:, 2304:2560]
        cbd, cT = small[:, 4 * P:5 * P], small[:, 5 * P:6 * P]
        with nc.Block() as block:
            sub, ex, cx = steps("c_", "sub ex cx")
            s_w, s_v, s_p, s_a = sem("c_w"), sem("c_v"), sem("c_p"), sem("c_a")

            @block.sync
            def _(sp):
                sp.dma_start(wq, A["L0_mix_W_qkv"][:, 0:P].rearrange("(c p) n -> p c n", p=P)).then_inc(s_w, 16)
                sp.dma_start(wout, A["L0_mix_W_out"]).then_inc(s_w, 16)
                sp.dma_start(w2, A["L0_gnn_W2"].rearrange("(c p) n -> p c n", p=P)).then_inc(s_w, 16)
                sp.wait_ge(s_w, 48)

            @block.scalar
            def _(a):
                start(a, ex)

                def a_ex(t, b):
                    a.wait_ge(*sub.after(t))
                    a.wait_ge(*cx.room(t))
                    a.activation(erow[b], KV[:, bass.ds(t, 1), 0:P].rearrange("p t c -> p (t c)"), ACT.Exp).then_inc(ex.sem, 1)
                tiles(a, (a_ex, 0))

            @block.tensor
            def _(pe):
                start(pe, cx)
                pe.transpose(ps[0][:, 0:P], kmax, ident[:, :]).then_inc(s_p, 1)
                pe.wait_ge(s_v, 2)
                pe.matmul(ps[1][:, 0:P], nmat, ident[:, :], start=True, stop=True).then_inc(s_p, 1)

                def p_cx(t, b):
                    n = LAST if isinstance(t, int) and t == T - 1 else P
                    pe.wait_ge(*ex.after(t))
                    pe.matmul(ps[2][:, 0:P + 1], erow[b][0:n], KV[0:n, bass.ds(t, 1), P:D + 1].rearrange("p t c -> p (t c)"),
                              start=isinstance(t, int) and t == 0, stop=isinstance(t, int) and t == T - 1,
                              skip_group_check=True).then_inc(cx.sem, 1)
                tiles(pe, (p_cx, 0))
                pe.wait_ge(s_w, 48)
                for c in range(2):
                    pe.transpose(ps[3][:, c * P:(c + 1) * P], wq[:, c, :], ident[:, :]).then_inc(s_p, 1)
                pe.wait_ge(s_v, 9)
                pe.transpose(ps[4][:, 0:P], cbd, ident[:, :]).then_inc(s_p, 1)
                pe.wait_ge(s_v, 10)
                pe.matmul(ps[5][:, 0:D], cT, wout, start=True, stop=True).then_inc(s_p, 1)
                pe.wait_ge(s_v, 11)
                for c in range(2):
                    pe.matmul(ps[6][:, c * D:(c + 1) * D], wqT[:, c * P:(c + 1) * P], m1, start=True, stop=True).then_inc(s_p, 1)

            @block.vector
            def _(v):
                link = Chain(v, s_v)
                start(v, sub)
                v.wait_ge(s_p, 1)
                link(v.tensor_reduce(nmax, ps[0][:, 0:P], AX.X, ALU.max, negate=True))
                link(v.tensor_copy(nmat, nmax.broadcast_to([P, P])))
                v.wait_ge(s_p, 2)

                def v_sub(t, b):
                    k = KV[:, bass.ds(t, 1), 0:P].rearrange("p t c -> p (t c)")
                    v.tensor_tensor(k, k, ps[1][:, 0:P], ALU.add).then_inc(sub.sem, 1)
                tiles(v, (v_sub, 0))
                v.wait_ge(*cx.after(T - 1))
                link(v.reciprocal(nmax, ps[2][:, P:P + 1]))
                link(v.memset(cbd, 0.0))
                for q in range(4):
                    r = slice(32 * q, 32 * q + 32)
                    link(v.tensor_scalar(cbd[r, r], ps[2][r, r], nmax[r], 32.0 ** -0.5, ALU.mult, ALU.mult))
                v.wait_ge(s_p, 4)
                link(v.tensor_copy(wqT, ps[3][:, 0:D]))
                v.wait_ge(s_p, 5)
                link(v.tensor_copy(cT, ps[4][:, 0:P]))
                v.wait_ge(s_p, 6)
                link(v.tensor_copy(m1, ps[5][:, 0:D]))
                v.wait_ge(s_p, 8)
                link(v.tensor_copy(wreg[:, 1024:1536], ps[6][:, :]))

        def aggregate(phase, tab, sync=None):
            with nc.Block() as block:
                if sync:
                    block.sync(sync)

                @block.scalar
                def _(a):
                    with a.Fori(0, VI) as i:
                        for q in range(RING // 4):
                            a.wait_ge(s_mm, (i + phase * VI) * RING + 4 * q + 4)
                            a.copy(idx_stage[:, 4 * q:4 * q + 4], src_idx[:, bass.ds(i * RING + 4 * q, 4)]).then_inc(s_st, 1)

                @block.gpsimd
                def _(g):
                    with g.Fori(0, VI) as i:
                        for q in range(RING // 4):
                            g.wait_ge(s_st, (i + phase * VI) * (RING // 4) + q + 1)
                            g.sem_inc(s_go, 1)
                            for u in range(4 * q, 4 * q + 4):
                                g.indirect_dma_start(out=rows[:, u * D:(u + 1) * D], out_offset=None, in_=tab,
                                                     in_offset=bass.IndirectOffsetOnAxis(ap=idx_stage[:, u:u + 1], axis=0)
                                                     ).then_inc(s_g[u], 16)

                @block.tensor
                def _(pe):
                    with pe.Fori(0, VI) as i:
                        turn = i + phase * VI
                        for u in range(RING):
                            pe.wait_ge(s_g[u], turn * 16 + 16)
                            pe.wait_ge(s_m, turn * RING + u + 1)
                            pe.wait_ge(s_ac, turn * RING + u + 1)
                            pe.matmul(ps[u % 4][:, 0:D], mring[:, u % 4 * P:(u % 4 + 1) * P], rows[:, u * D:(u + 1) * D],
                                      start=True, stop=True).then_inc(s_mm, 1)

                @block.vector
                def _(v):
                    def matrix(i, u):
                        v.wait_ge(s_mm, (i + phase * VI) * RING + u + 1 + RING - 4)
                        v.tensor_scalar(mring[:, u % 4 * P:(u % 4 + 1) * P], iota[:, :], dst_rel[:, bass.ds(i * RING + u, 1)], None,
                                        ALU.is_equal).then_inc(s_m, 1)

                    def add(i, u, at):
                        v.wait_ge(s_mm, (i + phase * VI) * RING + u + 1 + RING)
                        v.wait_ge(s_ac, (i + phase * VI) * RING + u + 4)
                        acc = ACC[:, bass.ds(at, D)]
                        v.tensor_tensor(acc, acc, ps[u % 4][:, 0:D], ALU.add).then_inc(s_ac, 1)

                    with v.Fori(0, VI) as i:
                        at = loads(mybir.EngineType.DVE, acc_at[0:1, bass.ds(i * RING, RING)], (T - 1) * D)
                        for u in range(RING + 2):
                            if u < RING:
                                matrix(i, u)
                            if u >= 2:
                                add(i, u - 2, at[u - 2])

        b_row, b_row2 = bias_rows[:, 0:D], bias_rows[:, D:2 * D]
        s_r0 = sem("r_in", keep=True)
        Rt = R.rearrange("p (t d) -> p t d", d=D)

        def fetch_x(sp):
            sp.wait_ge(s_z, 1)
            for q in range(4):
                sp.dma_start(Rt[:, 12 * q:12 * q + 12, :],
                             A["x"][12 * q * P:12 * (q + 1) * P, :].rearrange("(t p) d -> p t d", p=P)).then_inc(s_r0, 16)
            sp.dma_start(Rt[0:LAST, T - 1, :], A["x"][(T - 1) * P:N, :]).then_inc(s_r0, 16)
            load_bias(sp, b_row, A["L0_gnn_b1"], s_r0)
            load_bias(sp, b_row2, A["L0_mix_b_out"], s_r0)
            sp.wait_ge(s_r0, 7 * 16)

        s_z = sem("r_zero")
        with nc.Block() as block:
            @block.gpsimd
            def _(g):
                g.memset(R[:, (T - 1) * D:T * D], 0.0).then_inc(s_z, 1)
        aggregate(0, table[0], fetch_x)

        x1 = [small[:, b * D:(b + 1) * D] for b in range(2)]
        zt = [small[:, (2 + b) * D:(3 + b) * D] for b in range(2)]
        xT2 = [rows[:, b * 512:(b + 1) * 512] for b in range(2)]
        with nc.Block() as block:
            row, tp, xt, mm, z, w1, r, h, rb, wr = steps("b_", "row tp xt mm z x1 r h rb wr")
            s_tab, s_b = sem("b_tab"), sem("b_bias")

            @block.sync
            def _(sp):
                to_table(sp, 1, h, s_tab)

            @block.gpsimd
            def _(g):
                start(g, rb, wr)

                def g_rb(t, b):
                    g.tensor_tensor(R[:, col(t)], R[:, col(t)], b_row2, ALU.add).then_inc(rb.sem, 1)

                def g_wr(t, b):
                    g.wait_ge(*row.after(t))
                    g.wait_ge(*w1.after(t))
                    g.tensor_copy(XN[:, col(t)], x1[b]).then_inc(wr.sem, 1)
                tiles(g, (g_rb, 0), (g_wr, 1))

            @block.scalar
            def _(a):
                start(a, row, xt)

                def a_row(t, b):
                    a.wait_ge(*tp.room(t))
                    a.copy(xrow[b], XN[:, col(t)]).then_inc(row.sem, 1)

                def a_xt(t, b):
                    a.wait_ge(*tp.after(t))
                    a.wait_ge(*mm.room(t))
                    a.copy(xT2[b], ps[b][:, :]).then_inc(xt.sem, 1)
                tiles(a, (a_row, 0), (a_xt, 0))

            @block.tensor
            def _(pe):
                start(pe, tp, mm)

                def p_tp(t, b):
                    pe.wait_ge(*row.after(t))
                    pe.wait_ge(*w1.after(t))
                    pe.wait_ge(*xt.room(t))
                    for c in range(2):
                        pe.transpose(ps[b][:, c * P:(c + 1) * P], xrow[b][:, c * P:(c + 1) * P], ident[:, :])
                    pe.transpose(ps[b][:, 2 * P:3 * P], x1[b][:, 0:P], ident[:, :])
                    pe.transpose(ps[b][:, 3 * P:4 * P], x1[b][:, P:D], ident[:, :]).then_inc(tp.sem, 1)

                def p_mm(t, b):
                    pe.wait_ge(*xt.after(t))
                    pe.wait_ge(*r.room(t))
                    pe.wait_ge(*h.room(t))
                    for c in range(2):
                        pe.matmul(ps[2 + b][:, 0:D], xT2[b][:, c * P:(c + 1) * P], g0[:, c, :], start=c == 0, stop=c == 1)
                    pe.matmul(ps[2 + b][:, D:2 * D], xT2[b][:, 2 * P:3 * P], w2[:, 0, :], start=True, stop=False)
                    pe.matmul(ps[2 + b][:, D:2 * D], xT2[b][:, 3 * P:4 * P], w2[:, 1, :], start=False, stop=True).then_inc(mm.sem, 1)
                tiles(pe, (p_tp, 0), (p_mm, 1))

            @block.vector
            def _(v):
                start(v, z, w1, r, h)
                v.tensor_copy(bias_ps[:, 0:D], b_row).then_inc(s_b, 1)
                v.wait_ge(s_b, 1)

                def v_z(t, b):
                    v.wait_ge(*w1.room(t))
                    v.scalar_tensor_tensor(ps[4 + b][:, 0:D], ACC[:, col(t)], dinv[:, bass.ds(t, 1)], bias_ps[:, 0:D],
                                           ALU.mult, ALU.add).then_inc(z.sem, 1)

                def v_x1(t, b):
                    v.wait_ge(*z.after(t))
                    v.wait_ge(*tp.room(t))
                    v.wait_ge(*wr.room(t))
                    v.scalar_tensor_tensor(x1[b], ps[4 + b][:, 0:D], 0.0, XN[:, col(t)], ALU.max, ALU.add).then_inc(w1.sem, 1)

                def v_r(t, b):
                    v.wait_ge(*mm.after(t))
                    v.wait_ge(*rb.after(t))
                    v.tensor_tensor(R[:, col(t)], R[:, col(t)], ps[2 + b][:, 0:D], ALU.add).then_inc(r.sem, 1)

                def v_h(t, b):
                    v.wait_ge(*z.after(t))
                    v.tensor_scalar(ACC[:, col(t)], ps[2 + b][:, D:2 * D], dinv[:, bass.ds(t, 1)], None, ALU.mult).then_inc(h.sem, 1)
                tiles(v, (v_z, 0), (v_x1, 0), (v_r, 2), (v_h, 2))

        def fetch_b2(sp):
            load_bias(sp, b_row, A["L0_gnn_b2"], s_r0)
            sp.wait_ge(s_r0, 8 * 16)
        aggregate(1, table[1], fetch_b2)
        STAGE_AGG2_DONE = True

        with nc.Block() as block:
            z, xp, rx = steps("d_", "z xp rx")
            s_b, s_sl, s_n = sem("d_bias"), sem("d_stats"), sem("d_norm")

            @block.gpsimd
            def _(g):
                start(g, rx)

                def g_rx(t, b):
                    g.tensor_tensor(R[:, col(t)], R[:, col(t)], XN[:, col(t)], ALU.add).then_inc(rx.sem, 1)
                tiles(g, (g_rx, 0))

            @block.vector
            def _(v):
                start(v, z, xp)

                def v_z(t, b):
                    v.wait_ge(*xp.room(t))
                    v.scalar_tensor_tensor(ps[4 + b][:, 0:D], ACC[:, col(t)], dinv[:, bass.ds(t, 1)], b_row,
                                           ALU.mult, ALU.add).then_inc(z.sem, 1)

                def v_xp(t, b):
                    v.wait_ge(*z.after(t))
                    v.wait_ge(*rx.after(t))
                    v.scalar_tensor_tensor(XN[:, col(t)], ps[4 + b][:, 0:D], 0.0, R[:, col(t)], ALU.max, ALU.add).then_inc(xp.sem, 1)
                tiles(v, (v_z, 0), (v_xp, 1))
                v.wait_ge(*xp.after(T - 1))
                row_stats(v, XN, s_sl)
                norm_factors(v, Chain(v, s_n))

        ff1 = wreg[:, 0:2048].rearrange("p (c n) -> p c n", c=2)
        b1row = wreg[:, 2048:2048 + HID]
        wg = wreg[:, 3072:3072 + HC * NE].rearrange("p (k n) -> p k n", n=NE)
        bgr, i8 = wreg[:, 3136:3144], wreg[:, 3144:3152]
        ltri = wreg[:, 3152:3152 + P]
        ones = wreg[:, 3280:3280 + P]
        valid, junk_row = wreg[:, 3408:3408 + T], wreg[:, 3457:3457 + T]
        cnt = wreg[:, 3506:3514]
        pcol = wreg[:, 3514:3515]
        hr = [AR[:, NE * (HC + 1) * D + b * HID:NE * (HC + 1) * D + (b + 1) * HID] for b in range(4)]
        hT = [rows[:, b % 2 * HID:(b % 2 + 1) * HID] for b in range(4)]
        l8, key, rnk = ([small[:, 64 * q + 8 * b:64 * q + 8 * b + 8] for b in (0, 1, 0, 1)] for q in range(3))
        m1x, km, pos = ([small[:, 256 + 2 * q + b:257 + 2 * q + b] for b in (0, 1, 0, 1)] for q in range(3))
        s_wd = sem("s_wd")
        bdtab = AR[:, NE * HC * D:NE * HC * D + NE * D]
        gate3 = gate[:, :].rearrange("p (t e) -> p t e", e=NE)
        gtmp3 = gtmp[:, :].rearrange("p (t e) -> p t e", e=NE)
        with nc.Block() as block:
            row, tp, xt, mm, hb, gl, t8, ht, lg, sl, pf, ps_ = steps("f_", "row tp xt mm hb gl t8 ht lg sl pf pos")
            s_w, s_sc, s_c1, s_c2, s_k, s_kc = sem("f_w"), [sem(f"f_sc{b}") for b in range(4)], sem("f_c1"), sem("f_c2"), sem("f_k"), sem("f_kc")

            @block.sync
            def _(sp):
                sp.dma_start(ff1, A["L0_ffn_W1"].rearrange("(c p) n -> p c n", p=P)).then_inc(s_w, 16)
                sp.dma_start(wg, A["L0_ffn_Wg"].rearrange("(k p) n -> p k n", p=P)).then_inc(s_w, 16)
                load_bias(sp, b1row, A["L0_ffn_b1"], s_w)
                load_bias(sp, bgr, A["L0_ffn_bg"], s_w)
                sp.wait_ge(s_w, 4 * 16)
                for e in range(NE):
                    sp.dma_start(WD[:, e * HC * D:(e + 1) * HC * D].rearrange("p (k n) -> p k n", n=D),
                                 A["L0_ffn_Wd"][e].rearrange("(k p) n -> p k n", p=P)).then_inc(s_wd, 16)
                load_bias(sp, bdtab, A["L0_ffn_bd"].rearrange("e n -> (e n)"), s_wd)

            @block.gpsimd
            def _(g):
                g.memset(ltri, 1.0).then_inc(s_k, 1)
                g.memset(ones, 1.0).then_inc(s_k, 1)
                g.memset(valid, 1.0).then_inc(s_k, 1)
                g.memset(junk_row, 0.0).then_inc(s_k, 1)
                g.iota(idx_stage[:, 0:1], pattern=[[0, 1]], base=0, channel_multiplier=1).then_inc(s_k, 1)
                g.iota(idx_stage[:, 8:16], pattern=[[REG, NE]], base=0, channel_multiplier=0).then_inc(s_k, 1)
                g.wait_ge(s_k, 6)
                g.affine_select(out=ltri, in_=ltri, compare_op=ALU.is_gt, fill=0.0, base=0, pattern=[[1, P]],
                                channel_multiplier=-1).then_inc(s_k, 1)
                g.affine_select(out=valid[:, T - 1:T], in_=valid[:, T - 1:T], compare_op=ALU.is_gt, fill=0.0, base=LAST,
                                pattern=[[0, 1]], channel_multiplier=-1).then_inc(s_k, 1)
                def g_sc(t, b):
                    g.wait_ge(*ps_.after(t))
                    g.wait_ge(*gl.after(t))
                    g.sem_inc(s_go, 1)
                    g.indirect_dma_start(out=h_sorted, out_offset=bass.IndirectOffsetOnAxis(ap=idx_stage[:, b:b + 1], axis=0),
                                         in_=hr[b], in_offset=None).then_inc(s_sc[b], 16)
                tiles(g, (g_sc, 0), unroll=4)
                for b in range(4):
                    g.wait_ge(s_sc[b], 16 * ((T - 1 - b) // 4 + 1))

            @block.scalar
            def _(a):
                start(a, row, gl, ht)

                def a_row(t, b):
                    a.wait_ge(*tp.room(t))
                    a.activation(xrow[b % 2], XN[:, col(t)], ACT.Identity, bias=nmr[:, bass.ds(t, 1)],
                                 scale=rstd[:, bass.ds(t, 1)]).then_inc(row.sem, 1)

                def a_gl(t, b):
                    a.wait_ge(*hb.after(t))
                    a.activation(hr[b], hr[b], ACT.Gelu).then_inc(gl.sem, 1)

                def a_ht(t, b):
                    a.wait_ge(*t8.after(t))
                    a.wait_ge(*lg.room(t))
                    a.copy(hT[b][:, 0:512], ps[6][:, :])
                    a.copy(hT[b][:, 512:1024], ps[7][:, :]).then_inc(ht.sem, 1)
                tiles(a, (a_row, 0), (a_ht, 2), (a_gl, 1), unroll=4)

            @block.tensor
            def _(pe):
                start(pe, tp, mm, t8, lg, pf)
                pe.wait_ge(s_w, 4 * 16)
                pe.wait_ge(s_k, 8)

                def p_tp(t, b):
                    pe.wait_ge(*row.after(t))
                    pe.wait_ge(*xt.room(t))
                    pe.transpose(ps[b % 2][:, 0:P], xrow[b % 2][:, 0:P], ident[:, :])
                    pe.transpose(ps[b % 2][:, P:D], xrow[b % 2][:, P:D], ident[:, :]).then_inc(tp.sem, 1)

                def p_mm(t, b):
                    pe.wait_ge(*xt.after(t))
                    pe.wait_ge(*hb.after(t - 1))
                    for c in range(2):
                        for h in range(2):
                            ins = pe.matmul(ps[2 + h][:, :], xT[b % 2][:, c * P:(c + 1) * P], ff1[:, c, h * 512:(h + 1) * 512],
                                            start=c == 0, stop=c == 1)
                    ins.then_inc(mm.sem, 1)

                def p_t8(t, b):
                    pe.wait_ge(*gl.after(t))
                    pe.wait_ge(*ht.after(t - 1))
                    for k in range(HC):
                        ins = pe.transpose(ps[6 + k // 4][:, k % 4 * P:(k % 4 + 1) * P], hr[b][:, k * P:(k + 1) * P], ident[:, :])
                    ins.then_inc(t8.sem, 1)

                def p_lg(t, b):
                    pe.wait_ge(*ht.after(t))
                    pe.wait_ge(*sl.after(t - 1))
                    for k in range(HC):
                        ins = pe.matmul(ps[4][:, 0:NE], hT[b][:, k * P:(k + 1) * P], wg[:, k, :], start=k == 0, stop=k == HC - 1)
                    ins.then_inc(lg.sem, 1)

                def p_pf(t, b):
                    pe.wait_ge(*sl.after(t))
                    pe.wait_ge(*ps_.after(t - 1))
                    pe.matmul(ps[5][:, 0:NE], ltri, gtmp[:, bass.ds(t * NE, NE)], start=True, stop=True)
                    pe.matmul(ps[5][:, NE:2 * NE], ones, gtmp[:, bass.ds(t * NE, NE)], start=True, stop=True).then_inc(pf.sem, 1)
                tiles(pe, (p_tp, 0), (p_pf, 4), (p_lg, 3), (p_mm, 1), (p_t8, 2), unroll=4)

            @block.vector
            def _(v):
                start(v, xt, hb, sl, ps_)
                link = Chain(v, s_kc)
                v.wait_ge(s_w, 4 * 16)
                v.wait_ge(s_k, 8)
                link(v.tensor_copy(pcol, idx_stage[:, 0:1]))
                link(v.tensor_copy(cnt, idx_stage[:, 8:16]))
                link(v.tensor_scalar(i8, iota[:, 0:NE], -1.0, float(NE), ALU.mult, ALU.add))
                link(v.tensor_scalar(junk_row, valid, -1.0, 1.0, ALU.mult, ALU.add))
                link(v.tensor_scalar(pos[0], pcol, float(JUNK), None, ALU.add))
                link(v.tensor_scalar(junk_row, junk_row, pos[0], None, ALU.mult))
                c1, c2 = Chain(v, s_c1, 5), Chain(v, s_c2, 4)

                def v_xt(t, b):
                    v.wait_ge(*tp.after(t))
                    v.wait_ge(*mm.room(t))
                    v.tensor_copy(xT[b % 2], ps[b % 2][:, 0:D]).then_inc(xt.sem, 1)

                def v_hb(t, b):
                    v.wait_ge(*mm.after(t))
                    v.wait_ge(*t8.room(t))
                    if not isinstance(t, int) or t >= 4:
                        v.wait_ge(s_sc[b], 4 * (t - b))
                    v.tensor_tensor(hr[b][:, 0:512], ps[2][:, :], b1row[:, 0:512], ALU.add)
                    v.tensor_tensor(hr[b][:, 512:1024], ps[3][:, :], b1row[:, 512:1024], ALU.add).then_inc(hb.sem, 1)

                def v_sl(t, b):
                    c1.tile(t)
                    v.wait_ge(*lg.after(t))
                    v.wait_ge(*pf.room(t))
                    c1(v.tensor_tensor(l8[b], ps[4][:, 0:NE], bgr, ALU.add))
                    c1(v.tensor_copy(gate[:, bass.ds(t * NE, NE)], l8[b]))
                    c1(v.tensor_reduce(m1x[b], l8[b], AX.X, ALU.max))
                    c1(v.scalar_tensor_tensor(key[b], l8[b], m1x[b], i8, ALU.is_equal, ALU.mult))
                    c1(v.tensor_reduce(km[b], key[b], AX.X, ALU.max))
                    v.tensor_scalar(gtmp[:, bass.ds(t * NE, NE)], key[b], km[b], valid[:, bass.ds(t, 1)], ALU.is_equal, ALU.mult).then_inc(sl.sem, 1)

                def v_pos(t, b):
                    c2.tile(t)
                    v.wait_ge(*pf.after(t))
                    if not isinstance(t, int) or t >= 4:
                        v.wait_ge(s_sc[b], 4 * (t - b))
                    c2(v.tensor_tensor(rnk[b], ps[5][:, 0:NE], cnt, ALU.add))
                    c2(v.scalar_tensor_tensor(key[b], rnk[b], 1.0, gtmp[:, bass.ds(t * NE, NE)], ALU.mult, ALU.mult, accum_out=pos[b]))
                    c2(v.tensor_tensor(cnt, cnt, ps[5][:, NE:2 * NE], ALU.add))
                    c2(v.tensor_scalar(idx_stage[:, b:b + 1], pos[b], junk_row[:, bass.ds(t, 1)], None, ALU.add))
                    v.tensor_copy(pos_f[:, bass.ds(t, 1)], idx_stage[:, b:b + 1]).then_inc(ps_.sem, 1)
                tiles(v, (v_xt, 0), (v_pos, 4), (v_sl, 3), (v_hb, 1), unroll=4)

        def wide(x, n):
            return x.unsqueeze(2).broadcast_to([P, T, n])

        zrow = rows[:, 0:HID]
        tail_i = idx_stage[:, 0:NE]
        ecol = small[:, 600:664]
        bt = [ecol[:, 8 * q:8 * q + 8] for q in range(4)]
        bcol = [ecol[:, 32 + q:33 + q] for q in range(8)]
        btab = [rows[0:1, 3 * HID + q * P:3 * HID + q * P + P].bitcast(I32) for q in range(3)]
        with nc.Block() as block:
            s_v, s_a, s_ti, s_z, s_zt, s_bt, s_bp = (sem("g_" + n) for n in "v a ti z zt bt bp".split())
            mxg, sm = gsml[:, 0:T], gsml[:, T:2 * T]

            @block.sync
            def _(sp):
                sp.wait_ge(s_z, 1)
                sp.dma_start(h_sorted[ZERO:ZERO + P, :], zrow).then_inc(s_zt, 16)
                sp.wait_ge(s_zt, 16)

            @block.gpsimd
            def _(g):
                g.memset(zrow, 0.0).then_inc(s_z, 1)
                g.wait_ge(s_z, 1)
                g.wait_ge(s_ti, 1)
                for e in range(NE):
                    g.indirect_dma_start(out=h_sorted, out_offset=bass.IndirectOffsetOnAxis(ap=tail_i[:, e:e + 1], axis=0),
                                         in_=zrow, in_offset=None).then_inc(s_bt, 16)
                g.wait_ge(s_bt, NE * 16)

            @block.scalar
            def _(a):
                a.wait_ge(s_a, 1)
                a.activation(gate[:, :], gate[:, :], ACT.Exp).then_inc(s_a, 1)

            @block.tensor
            def _(pe):
                pe.wait_ge(s_bp, 1)
                for q in range(3):
                    pe.transpose(ps[0][0:1, q * P:(q + 1) * P], bcol[4 + q], ident[:, :]).then_inc(s_bp, 1)

            @block.vector
            def _(v):
                link = Chain(v, s_v)
                link(v.tensor_scalar(tail_i, cnt, pcol, None, ALU.add))
                v.sem_inc(s_ti, 1)
                link(v.tensor_reduce(mxg, gate3, AX.X, ALU.max))
                link(v.tensor_tensor(gate3, gate3, wide(mxg, NE), ALU.subtract))
                v.sem_inc(s_a, 1)
                nb, end, st, jk = bt
                nbi = nb.bitcast(I32)
                link(v.tensor_scalar(nb, iota[:, 0:NE], -float(REG), float(P - 1), ALU.mult, ALU.add))
                link(v.tensor_tensor(nb, nb, cnt, ALU.add))
                link(v.tensor_copy(nbi, nb))
                link(v.tensor_scalar(nbi, nbi, 7, None, ALU.arith_shift_right))
                link(v.tensor_copy(jk, nbi))
                link(v.tensor_copy(nb, jk))
                link(v.tensor_tensor_scan(end, ones[:, 0:NE], nb, 0.0, ALU.mult, ALU.add))
                link(v.tensor_tensor(st, end, nb, ALU.subtract))
                eb, sb_, rw, ok, hoff, eoff, doff, _ = bcol
                link(v.tensor_scalar(jk, end, pcol, 0.0, ALU.is_le, ALU.add, accum_out=eb))
                link(v.scalar_tensor_tensor(jk, iota[:, 0:NE], eb, st, ALU.is_equal, ALU.mult, accum_out=sb_))
                link(v.tensor_tensor(rw, pcol, sb_, ALU.subtract))
                link(v.tensor_scalar(rw, rw, float(P), None, ALU.mult))
                link(v.scalar_tensor_tensor(rw, eb, float(REG), rw, ALU.mult, ALU.add))
                link(v.tensor_scalar(ok, eb, float(NE), None, ALU.is_lt))
                link(v.tensor_scalar(rw, rw, ok, None, ALU.mult))
                link(v.tensor_scalar(ok, ok, -1.0, 1.0, ALU.mult, ALU.add))
                link(v.scalar_tensor_tensor(hoff, ok, float(ZERO), rw, ALU.mult, ALU.add))
                link(v.scalar_tensor_tensor(jk, iota[:, 0:NE], -float(REG / P), st, ALU.mult, ALU.add))
                link(v.tensor_scalar(jk, jk, float(P), None, ALU.mult))
                link(v.tensor_tensor(gtmp3, gtmp3, jk.unsqueeze(1).broadcast_to([P, T, NE]), ALU.mult))
                link(v.tensor_reduce(mxg, gtmp3, AX.X, ALU.add))
                link(v.tensor_tensor(mxg, mxg, pos_f[:, :], ALU.add))
                link(v.tensor_tensor(pos_all[:, :], mxg, valid, ALU.mult))
                link(v.tensor_scalar(eb, eb, NE - 1.0, None, ALU.min))
                link(v.tensor_scalar(eoff, eb, float(HC * D), None, ALU.mult))
                link(v.tensor_scalar(doff, eb, float(D), None, ALU.mult))
                v.sem_inc(s_bp, 1)
                v.wait_ge(s_bp, 4)
                for q in range(3):
                    link(v.tensor_copy(btab[q], ps[0][0:1, q * P:(q + 1) * P]))
                v.wait_ge(s_a, 2)
                link(v.tensor_reduce(sm, gate3, AX.X, ALU.add))
                link(v.reciprocal(prob[:, :], sm))

        hoff, eoff, doff = btab
        hL = [rows[:, b * HID:(b + 1) * HID] for b in range(2)]
        bT = [(rows[:, 2 * HID:3 * HID], work[:, 0:HID])[b] for b in range(2)]
        yb = [small[:, b * D:(b + 1) * D] for b in range(2)]
        with nc.Block() as block:
            t8, c1, c2, ex, y = steps("e_", "t8 c1 c2 ex y")
            s_hl = [sem("e_h0"), sem("e_h1")]
            s_ys = [sem("e_y0"), sem("e_y1")]

            @block.sync
            def _(sp):
                def s_h(t, b):
                    at = sp.value_load(hoff[0:1, bass.ds(t, 1)], min_val=0, max_val=ZERO)
                    sp.wait_ge(*t8.room(t))
                    sp.dma_start(hL[b], h_sorted[bass.ds(at, P), :]).then_inc(s_hl[b], 16)

                def s_y(t, b):
                    sp.wait_ge(*y.after(t))
                    sp.dma_start(y_sorted[bass.ds(t * P, P), :], yb[b]).then_inc(s_ys[b], 16)
                tiles(sp, (s_h, 0), (s_y, 2), n=BLK)
                for b in range(2):
                    sp.wait_ge(s_ys[b], 16 * (BLK // 2))

            @block.scalar
            def _(a):
                start(a, c2)

                def a_c(t, b):
                    a.wait_ge(*t8.after(t))
                    a.wait_ge(*ex.room(t))
                    a.copy(bT[b][:, 512:1024], ps[2 * b + 1][:, :]).then_inc(c2.sem, 1)
                tiles(a, (a_c, 0), n=BLK)

            @block.tensor
            def _(pe):
                start(pe, t8, ex)
                pe.wait_ge(s_wd, (NE + 1) * 16)

                def p_t8(t, b):
                    pe.wait_ge(s_hl[b], 8 * (t - b) + 16)
                    pe.wait_ge(*c1.room(t))
                    pe.wait_ge(*c2.room(t))
                    for k in range(HC):
                        ins = pe.transpose(ps[2 * b + k // 4][:, k % 4 * P:(k % 4 + 1) * P], hL[b][:, k * P:(k + 1) * P], ident[:, :])
                    ins.then_inc(t8.sem, 1)

                def p_ex(t, b):
                    at = pe.value_load(eoff[0:1, bass.ds(t, 1)], min_val=0, max_val=(NE - 1) * HC * D)
                    pe.wait_ge(*c1.after(t))
                    pe.wait_ge(*c2.after(t))
                    pe.wait_ge(*y.room(t))
                    for k in range(HC):
                        ins = pe.matmul(ps[4 + b][:, 0:D], bT[b][:, k * P:(k + 1) * P], WD[:, bass.ds(at + k * D, D)],
                                        start=k == 0, stop=k == HC - 1)
                    ins.then_inc(ex.sem, 1)
                tiles(pe, (p_t8, 0), (p_ex, 1), n=BLK)

            @block.vector
            def _(v):
                start(v, c1, y)

                def v_c(t, b):
                    v.wait_ge(*t8.after(t))
                    v.wait_ge(*ex.room(t))
                    v.tensor_copy(bT[b][:, 0:512], ps[2 * b][:, :]).then_inc(c1.sem, 1)

                def v_y(t, b):
                    at = v.value_load(doff[0:1, bass.ds(t, 1)], min_val=0, max_val=(NE - 1) * D)
                    v.wait_ge(*ex.after(t))
                    if not isinstance(t, int) or t >= 2:
                        v.wait_ge(s_ys[b], 8 * (t - b))
                    v.tensor_tensor(yb[b], ps[4 + b][:, 0:D], bdtab[:, bass.ds(at, D)], ALU.add).then_inc(y.sem, 1)
                tiles(v, (v_c, 0), (v_y, 1), n=BLK)

        retire_sems()

        wns = wreg[:, 0:1024].rearrange("p (c n) -> p c n", c=2)
        yg = [rows[:, b * D:(b + 1) * D] for b in range(2)]
        x3 = [work[:, b * (D + 1):(b + 1) * (D + 1)] for b in range(2)]
        xT3 = [small[:, b * D:(b + 1) * D] for b in range(2)]
        with nc.Block() as block:
            row, tp, xt, mm, tb, r, rb, wr, pc, ya = steps("h_", "row tp xt mm tb r rb wr pc ya")
            s_yg = [sem("h_yg0"), sem("h_yg1")]
            s_w, s_sl, s_n, s_nf, s_one, s_tab, s_bs = (sem("h_" + n) for n in "w sl n nf one tab bs".split())

            @block.sync
            def _(sp):
                sp.dma_start(wns[:, :, 0:D], A["L1_gnn_W_neigh"].rearrange("(c p) n -> p c n", p=P)).then_inc(s_w, 16)
                sp.dma_start(wns[:, :, D:2 * D], A["L1_gnn_W_self"].rearrange("(c p) n -> p c n", p=P)).then_inc(s_w, 16)
                load_bias(sp, b_row, A["L1_gnn_b"], s_w)
                load_bias(sp, b_row2, A["L1_mix_b_fc2"], s_w)
                to_table(sp, 2, tb, s_tab)

            @block.gpsimd
            def _(g):
                start(g, rb, wr)

                def g_y(t, b):
                    g.wait_ge(*pc.after(t))
                    g.sem_inc(s_go, 1)
                    g.indirect_dma_start(out=yg[b], out_offset=None, in_=y_sorted,
                                         in_offset=bass.IndirectOffsetOnAxis(ap=pos_stage[:, b:b + 1], axis=0)).then_inc(s_yg[b], 16)
                tiles(g, (g_y, 0))
                for b in range(2):
                    g.memset(x3[b][:, D:D + 1], 1.0).then_inc(s_one, 1)
                g.wait_ge(s_w, 4 * 16)
                g.tensor_tensor(b_row, b_row, b_row2, ALU.add).then_inc(s_bs, 1)
                g.wait_ge(s_bs, 1)

                def g_rb(t, b):
                    g.wait_ge(*r.after(t))
                    g.tensor_tensor(R[:, col(t)], R[:, col(t)], b_row, ALU.add).then_inc(rb.sem, 1)

                def g_wr(t, b):
                    g.tensor_copy(XN[:, col(t)], x3[b][:, 0:D]).then_inc(wr.sem, 1)
                tiles(g, (g_rb, 0), (g_wr, 0))

            @block.scalar
            def _(a):
                start(a, row, pc)

                def a_pc(t, b):
                    a.wait_ge(*ya.room(t))
                    a.copy(pos_stage[:, b:b + 1], pos_all[:, bass.ds(t, 1)]).then_inc(pc.sem, 1)
                tiles(a, (a_pc, 0))
                a.wait_ge(s_nf, 1)

                def a_row(t, b):
                    a.wait_ge(*mm.room(t))
                    a.wait_ge(*wr.room(t))
                    a.activation(x3[b][:, 0:D], XN[:, col(t)], ACT.Identity, bias=nmr[:, bass.ds(t, 1)],
                                 scale=rstd[:, bass.ds(t, 1)]).then_inc(row.sem, 1)
                tiles(a, (a_row, 0))

            @block.tensor
            def _(pe):
                start(pe, tp, mm)
                pe.wait_ge(s_w, 4 * 16)
                pe.wait_ge(s_one, 2)

                def p_tp(t, b):
                    pe.wait_ge(*row.after(t))
                    pe.wait_ge(*xt.room(t))
                    pe.transpose(ps[b][:, 0:P], x3[b][:, 0:P], ident[:, :])
                    pe.transpose(ps[b][:, P:D], x3[b][:, P:D], ident[:, :]).then_inc(tp.sem, 1)

                def p_mm(t, b):
                    first, last = (isinstance(t, int) and t == q for q in (0, T - 1))
                    n = LAST if last else P
                    for c in range(2):
                        pe.matmul(ps[5 + c][:, 0:D + 1], x3[b][0:n, c * P:(c + 1) * P], x3[b][0:n, :], start=first, stop=last,
                                  skip_group_check=True)
                    pe.wait_ge(*xt.after(t))
                    pe.wait_ge(*tb.room(t))
                    pe.wait_ge(*r.room(t))
                    pe.matmul(ps[2 + b][:, :], xT3[b][:, 0:P], wns[:, 0, :], start=True, stop=False)
                    pe.matmul(ps[2 + b][:, :], xT3[b][:, P:D], wns[:, 1, :], start=False, stop=True).then_inc(mm.sem, 1)
                tiles(pe, (p_tp, 0), (p_mm, 0))

            @block.vector
            def _(v):
                start(v, xt, r, tb, ya)

                def v_ya(t, b):
                    v.wait_ge(s_yg[b], 8 * (t - b) + 16)
                    v.scalar_tensor_tensor(XN[:, col(t)], yg[b], prob[:, bass.ds(t, 1)], XN[:, col(t)], ALU.mult, ALU.add).then_inc(ya.sem, 1)
                tiles(v, (v_ya, 0))
                v.wait_ge(*ya.after(T - 1))
                row_stats(v, XN, s_sl)
                norm_factors(v, Chain(v, s_n))
                v.sem_inc(s_nf, 1)

                def v_xt(t, b):
                    v.wait_ge(*tp.after(t))
                    v.wait_ge(*mm.room(t))
                    v.tensor_copy(xT3[b], ps[b][:, 0:D]).then_inc(xt.sem, 1)

                def v_r(t, b):
                    v.wait_ge(*mm.after(t))
                    v.tensor_tensor(R[:, col(t)], XN[:, col(t)], ps[2 + b][:, D:2 * D], ALU.add).then_inc(r.sem, 1)

                def v_tb(t, b):
                    v.tensor_copy(ACC[:, col(t)], ps[2 + b][:, 0:D]).then_inc(tb.sem, 1)
                tiles(v, (v_xt, 0), (v_r, 0), (v_tb, 0))

        wqkv = rows[:, 0:1536].rearrange("p (c n) -> p c n", c=2)
        gram = rows[:, 1536:2048].rearrange("p (c n) -> p c n", c=2)
        t1 = rows[:, 2048:2560].rearrange("p (c n) -> p c n", c=2)
        wq1T = rows[:, 2560:3072].rearrange("p (c n) -> p c n", c=2)
        abd = rows[:, 3072:3328].rearrange("p (c n) -> p c n", c=2)
        abT = rows[:, 3328:3584].rearrange("p (c n) -> p c n", c=2)
        bqc = rows[:, 3584:3586]
        bqm = rows[:, 3600:3728]
        csum, nmx = rows[:, 3586:3588], rows[:, 3588:3590]
        rsm = rows[:, 3590:3592]
        nval = rows[0:1, 3592:3593]
        att = rows[:, 3728:3856].rearrange("p (c n) -> p c n", c=2)
        bqkv = work[0:1, 0:768]
        crow = work[0:1, 768:1024]
        t2row = work[0:1, 1024:1280]
        g1 = wreg[:, 0:512].rearrange("p (c n) -> p c n", c=2)
        c1row = bias_rows[:, D:2 * D]
        fc1 = wreg[:, 512:2048].rearrange("p (c n) -> p c n", c=2)
        fc2 = wreg[:, 2048:3584].rearrange("p (k n) -> p k n", n=D)
        lng, lnb, fb1 = wreg[:, 3584:3586], wreg[:, 3586:3588], wreg[:, 3588:3594]
        with nc.Block() as block:
            s_w, s_v, s_p, s_a, s_z3 = (sem("i_" + n) for n in "w v p a z".split())

            @block.sync
            def _(sp):
                sp.dma_start(wqkv, A["L1_mix_w_qkv"].rearrange("(c p) n -> p c n", p=P)).then_inc(s_w, 16)
                sp.dma_start(bqkv, A["L1_mix_b_qkv"].rearrange("(a n) -> a n", a=1)).then_inc(s_w, 16)
                sp.dma_start(bqc, A["L1_mix_b_qkv"][0:D].rearrange("(c p) -> p c", p=P), allow_slow_non_contiguous=True).then_inc(s_w, 16)
                sp.dma_start(fc1, A["L1_mix_w_fc1"].rearrange("(c p) n -> p c n", p=P)).then_inc(s_w, 16)
                sp.dma_start(fc2, A["L1_mix_w_fc2"].rearrange("(k p) n -> p k n", p=P)).then_inc(s_w, 16)
                sp.dma_start(lng, A["L1_mix_norm_g"].rearrange("(c p) -> p c", p=P), allow_slow_non_contiguous=True).then_inc(s_w, 16)
                sp.dma_start(lnb, A["L1_mix_norm_b"].rearrange("(c p) -> p c", p=P), allow_slow_non_contiguous=True).then_inc(s_w, 16)
                sp.dma_start(fb1, A["L1_mix_b_fc1"].rearrange("(k p) -> p k", p=P), allow_slow_non_contiguous=True).then_inc(s_w, 16)
                sp.wait_ge(s_w, 8 * 16)

            @block.gpsimd
            def _(g):
                g.memset(ACC, 0.0).then_inc(s_z3, 1)
                g.memset(rows[:, 3072:3328], 0.0).then_inc(s_z3, 1)
                g.memset(nval, float(N)).then_inc(s_z3, 1)

            @block.scalar
            def _(a):
                a.wait_ge(s_v, 13)
                for c in range(2):
                    a.activation(att[:, c, :], att[:, c, :], ACT.Exp, bias=nmx[:, c:c + 1], scale=64.0 ** -0.5).then_inc(s_a, 1)

            @block.tensor
            def _(pe):
                pe.wait_ge(s_w, 8 * 16)
                pe.wait_ge(s_z3, 3)
                pe.wait_ge(s_v, 4)
                for c in range(2):
                    pe.matmul(ps[0][0:1, c * P:(c + 1) * P], csum[:, c:c + 1], ident[:, :], start=True, stop=True).then_inc(s_p, 1)
                pe.wait_ge(s_v, 5)
                for m in range(2):
                    for c in range(2):
                        pe.matmul(ps[1][:, m * D:(m + 1) * D], gram[:, c, m * P:(m + 1) * P], wqkv[:, c, 2 * D:3 * D], start=c == 0, stop=False)
                    pe.matmul(ps[1][:, m * D:(m + 1) * D], crow[:, m * P:(m + 1) * P], bqkv[:, 2 * D:3 * D], start=False, stop=True).then_inc(s_p, 1)
                for c in range(2):
                    pe.matmul(ps[2][0:1, 0:D], csum[:, c:c + 1], wqkv[:, c, 2 * D:3 * D], start=c == 0, stop=False)
                pe.matmul(ps[2][0:1, 0:D], nval, bqkv[:, 2 * D:3 * D], start=False, stop=True).then_inc(s_p, 1)
                pe.wait_ge(s_v, 7)
                for m in range(2):
                    for c in range(2):
                        pe.matmul(ps[3][:, m * D:(m + 1) * D], wqkv[:, c, D + m * P:D + (m + 1) * P], t1[:, c, :], start=c == 0, stop=False)
                    pe.matmul(ps[3][:, m * D:(m + 1) * D], bqkv[:, D + m * P:D + (m + 1) * P], t2row, start=False, stop=True).then_inc(s_p, 1)
                for m in range(2):
                    for c in range(2):
                        ins = pe.transpose(ps[4][:, m * D + c * P:m * D + (c + 1) * P], wqkv[:, c, m * P:(m + 1) * P], ident[:, :])
                ins.then_inc(s_p, 1)
                pe.wait_ge(s_v, 21)
                for m in range(2):
                    pe.transpose(ps[5][:, m * P:(m + 1) * P], abd[:, m, :], ident[:, :]).then_inc(s_p, 1)
                pe.wait_ge(s_v, 22)
                for rr in range(2):
                    for m in range(2):
                        pe.matmul(ps[6][:, rr * D + m * P:rr * D + (m + 1) * P], wq1T[:, m, rr * P:(rr + 1) * P], abT[:, m, :],
                                  start=True, stop=True).then_inc(s_p, 1)
                for m in range(2):
                    pe.wait_ge(s_v, 23 + 2 * m)
                    pe.matmul(ps[2][:, m * P:(m + 1) * P], bqm, abT[:, m, :], start=True, stop=True).then_inc(s_p, 1)

            @block.vector
            def _(v):
                link = Chain(v, s_v)
                for c in range(2):
                    link(v.tensor_copy(gram[:, c, :], ps[5 + c][:, 0:D]))
                    link(v.tensor_copy(csum[:, c:c + 1], ps[5 + c][:, D:D + 1]))
                v.wait_ge(s_p, 2)
                link(v.tensor_copy(crow, ps[0][0:1, 0:D]))
                v.wait_ge(s_p, 5)
                link(v.tensor_copy(rows[:, 2048:2560], ps[1][:, :]))
                link(v.tensor_copy(t2row, ps[2][0:1, 0:D]))
                v.wait_ge(s_p, 7)
                for m in range(2):
                    link(v.tensor_copy(att[0:64, m, :], ps[3][0:64, m * D + 2 * m * 64:m * D + (2 * m + 1) * 64]))
                    link(v.tensor_copy(att[64:128, m, :], ps[3][64:128, m * D + (2 * m + 1) * 64:m * D + (2 * m + 2) * 64]))
                link(v.tensor_reduce(nmx, att, AX.X, ALU.max, negate=True))
                link(v.tensor_scalar(nmx, nmx, 64.0 ** -0.5, None, ALU.mult))
                v.wait_ge(s_p, 8)
                link(v.tensor_copy(rows[:, 2560:3072], ps[4][:, :]))
                v.wait_ge(s_a, 2)
                link(v.tensor_reduce(rsm, att, AX.X, ALU.add))
                link(v.reciprocal(rsm, rsm))
                v.wait_ge(s_z3, 3)
                link(v.tensor_scalar(bqm, bqc[:, 0:1].broadcast_to([P, P]), 1.0, None, ALU.mult))
                for m in range(2):
                    for q in range(2):
                        rr = slice(64 * q, 64 * q + 64)
                        link(v.tensor_scalar(abd[rr, m, rr], att[rr, m, :], rsm[rr, m:m + 1], None, ALU.mult))
                v.wait_ge(s_p, 10)
                link(v.tensor_copy(rows[:, 3328:3584], ps[5][:, 0:D]))
                v.wait_ge(s_p, 14)
                link(v.tensor_copy(wreg[:, 0:512], ps[6][:, :]))
                v.wait_ge(s_p, 15)
                link(v.tensor_scalar(bqm, bqc[:, 1:2].broadcast_to([P, P]), 1.0, None, ALU.mult))
                link(v.tensor_copy(c1row[:, 0:P], ps[2][:, 0:P]))
                v.wait_ge(s_p, 16)
                link(v.tensor_copy(c1row[:, P:D], ps[2][:, P:D]))

        aggregate(2, table[2])

        yt = [work[:, 1024 + b * D:1024 + (b + 1) * D] for b in range(2)]
        ht = [work[:, 1536 + b * D:1536 + (b + 1) * D] for b in range(2)]
        hT1 = [rows[:, b * D:(b + 1) * D] for b in range(2)]
        uT = [rows[:, 512 + b * 768:512 + (b + 1) * 768] for b in range(2)]
        mw = [newton[:, 8 * b:8 * b + 8] for b in range(2)]
        with nc.Block() as block:
            row, xc, tp, xt, gm, y, ln, t2, hx, f1, gl, f2, o, ry = steps("j_", "row xc tp xt gm y ln t2 hx f1 gl f2 o ry")
            s_c = sem("j_chain")

            @block.gpsimd
            def _(g):
                start(g, xc, ry)

                def g_xc(t, b):
                    g.wait_ge(*row.after(t))
                    g.tensor_tensor(XN[:, col(t)], XN[:, col(t)], c1row, ALU.add).then_inc(xc.sem, 1)

                def g_ry(t, b):
                    g.wait_ge(*y.after(t))
                    g.tensor_tensor(R[:, col(t)], R[:, col(t)], yt[b], ALU.add).then_inc(ry.sem, 1)
                tiles(g, (g_xc, 0), (g_ry, 0))

            @block.scalar
            def _(a):
                start(a, row, hx, gl)

                def a_row(t, b):
                    a.wait_ge(*tp.room(t))
                    a.copy(xrow[b], XN[:, col(t)]).then_inc(row.sem, 1)

                def a_hx(t, b):
                    a.wait_ge(*t2.after(t))
                    a.wait_ge(*f1.room(t))
                    for c in range(2):
                        ins = a.activation(hT1[b][:, c * P:(c + 1) * P], ps[1][:, c * P:(c + 1) * P], ACT.Identity,
                                           bias=lnb[:, c:c + 1], scale=lng[:, c:c + 1])
                    ins.then_inc(hx.sem, 1)

                def a_gl(t, b):
                    a.wait_ge(*f1.after(t))
                    a.wait_ge(*f2.room(t))
                    for k in range(6):
                        ins = a.activation(uT[b][:, k * P:(k + 1) * P], ps[4 + 2 * b + k // 4][:, k % 4 * P:(k % 4 + 1) * P], ACT.Gelu,
                                           bias=fb1[:, k:k + 1])
                    ins.then_inc(gl.sem, 1)
                tiles(a, (a_row, 0), (a_gl, 2), (a_hx, 1))

            @block.tensor
            def _(pe):
                start(pe, tp, gm, t2, f1, f2)

                def p_tp(t, b):
                    pe.wait_ge(*row.after(t))
                    pe.wait_ge(*xt.after(t - 1))
                    pe.transpose(ps[0][:, 0:P], xrow[b][:, 0:P], ident[:, :])
                    pe.transpose(ps[0][:, P:D], xrow[b][:, P:D], ident[:, :]).then_inc(tp.sem, 1)

                def p_gm(t, b):
                    pe.wait_ge(*xt.after(t))
                    pe.wait_ge(*y.after(t - 1))
                    for c in range(2):
                        ins = pe.matmul(ps[2][:, 0:D], xT[b][:, c * P:(c + 1) * P], g1[:, c, :], start=c == 0, stop=c == 1)
                    ins.then_inc(gm.sem, 1)

                def p_t2(t, b):
                    pe.wait_ge(*ln.after(t))
                    pe.wait_ge(*hx.after(t - 1))
                    pe.transpose(ps[1][:, 0:P], ht[b][:, 0:P], ident[:, :])
                    pe.transpose(ps[1][:, P:D], ht[b][:, P:D], ident[:, :]).then_inc(t2.sem, 1)

                def p_f1(t, b):
                    pe.wait_ge(*hx.after(t))
                    pe.wait_ge(*gl.room(t))
                    for k in range(6):
                        for c in range(2):
                            ins = pe.matmul(ps[4 + 2 * b + k // 4][:, k % 4 * P:(k % 4 + 1) * P], fc1[:, c, k * P:(k + 1) * P],
                                            hT1[b][:, c * P:(c + 1) * P], start=c == 0, stop=c == 1)
                    ins.then_inc(f1.sem, 1)

                def p_f2(t, b):
                    pe.wait_ge(*gl.after(t))
                    pe.wait_ge(*o.after(t - 1))
                    for k in range(6):
                        ins = pe.matmul(ps[3][:, 0:D], uT[b][:, k * P:(k + 1) * P], fc2[:, k, :], start=k == 0, stop=k == 5)
                    ins.then_inc(f2.sem, 1)
                tiles(pe, (p_tp, 0), (p_t2, 1), (p_gm, 0), (p_f2, 2), (p_f1, 1))

            @block.vector
            def _(v):
                start(v, xt, y, ln, o)
                chain = Chain(v, s_c, 24)

                def v_xt(t, b):
                    v.wait_ge(*tp.after(t))
                    v.wait_ge(*gm.room(t))
                    v.tensor_copy(xT[b], ps[0][:, 0:D]).then_inc(xt.sem, 1)

                def v_y(t, b):
                    v.wait_ge(*gm.after(t))
                    v.wait_ge(*xc.after(t))
                    v.wait_ge(*ry.room(t))
                    v.tensor_tensor(yt[b], XN[:, col(t)], ps[2][:, 0:D], ALU.add).then_inc(y.sem, 1)

                def v_ln(t, b):
                    chain.tile(t)
                    m = mw[b]
                    v.wait_ge(*y.after(t))
                    chain(v.bn_stats(stats[:, :], yt[b]))
                    chain(v.tensor_scalar(m[:, 0:1], stats[:, 1:2], stats[:, 4:5], 0.5, ALU.add, ALU.mult))
                    chain(v.tensor_scalar(m[:, 1:2], stats[:, 1:2], stats[:, 4:5], 0.5, ALU.subtract, ALU.mult))
                    chain(v.tensor_scalar(m[:, 2:3], stats[:, 2:3], stats[:, 5:6], 1.0 / D, ALU.add, ALU.mult))
                    chain(v.scalar_tensor_tensor(m[:, 2:3], m[:, 1:2], m[:, 1:2], m[:, 2:3], ALU.mult, ALU.add))
                    chain(v.tensor_scalar(m[:, 2:3], m[:, 2:3], EPS, None, ALU.add))
                    rsqrt(v, chain, m[:, 2:3], m[:, 3:4], m[:, 4:5], 1)
                    v.wait_ge(*t2.room(t))
                    v.tensor_scalar(ht[b], yt[b], m[:, 0:1], m[:, 3:4], ALU.subtract, ALU.mult).then_inc(ln.sem, 1)

                def v_o(t, b):
                    v.wait_ge(*f2.after(t))
                    v.wait_ge(*ry.after(t))
                    v.tensor_tensor(R[:, col(t)], R[:, col(t)], ps[3][:, 0:D], ALU.add).then_inc(o.sem, 1)
                tiles(v, (v_xt, 0), (v_y, 0), (v_o, 2), (v_ln, 0))

        gw = wreg[:, 0:8].rearrange("p (c n) -> p c n", c=2)
        gbr = wreg[:, 8:12]
        with nc.Block() as block:
            s_r, s_sl, s_n, s_w9 = sem("k_r"), sem("k_sl"), sem("k_n"), sem("k_w")

            @block.sync
            def _(sp):
                sp.dma_start(gw, A["L1_ffn_gW"].rearrange("(c p) n -> p c n", p=P)).then_inc(s_w9, 16)
                load_bias(sp, gbr, A["L1_ffn_gb"], s_w9)
                sp.wait_ge(s_w9, 32)

            @block.vector
            def _(v):
                with v.Fori(0, T) as i:
                    v.scalar_tensor_tensor(R[:, col(i)], ACC[:, col(i)], invdeg[:, bass.ds(i, 1)], R[:, col(i)], ALU.mult,
                                           ALU.add).then_inc(s_r, 1)
                v.wait_ge(s_r, T)
                row_stats(v, R, s_sl)
                norm_factors(v, Chain(v, s_n))

        NG = 4
        lgt = gate[:, 0:T * NG].rearrange("p (t e) -> p t e", e=NG)
        with nc.Block() as block:
            row, tp, xt, gt, gc, wr = steps("l_", "row tp xt gt gc wr")

            @block.gpsimd
            def _(g):
                start(g, wr)

                def g_wr(t, b):
                    g.wait_ge(*xt.after(t))
                    g.tensor_copy(XN[:, col(t)], xT[b]).then_inc(wr.sem, 1)
                tiles(g, (g_wr, 0))

            @block.scalar
            def _(a):
                start(a, row)

                def a_row(t, b):
                    a.wait_ge(*tp.room(t))
                    a.activation(xrow[b], R[:, col(t)], ACT.Identity, bias=nmr[:, bass.ds(t, 1)],
                                 scale=rstd[:, bass.ds(t, 1)]).then_inc(row.sem, 1)
                tiles(a, (a_row, 0))

            @block.tensor
            def _(pe):
                start(pe, tp, gt)

                def p_tp(t, b):
                    pe.wait_ge(*row.after(t))
                    pe.wait_ge(*xt.room(t))
                    pe.transpose(ps[b][:, 0:P], xrow[b][:, 0:P], ident[:, :])
                    pe.transpose(ps[b][:, P:D], xrow[b][:, P:D], ident[:, :]).then_inc(tp.sem, 1)

                def p_gt(t, b):
                    pe.wait_ge(*xt.after(t))
                    pe.wait_ge(*gc.room(t))
                    for c in range(2):
                        ins = pe.matmul(ps[2 + b][:, 0:NG], xT[b][:, c * P:(c + 1) * P], gw[:, c, :], start=c == 0, stop=c == 1)
                    ins.then_inc(gt.sem, 1)
                tiles(pe, (p_tp, 0), (p_gt, 1))

            @block.vector
            def _(v):
                start(v, xt, gc)

                def v_xt(t, b):
                    v.wait_ge(*tp.after(t))
                    v.wait_ge(*gt.room(t))
                    v.wait_ge(*wr.room(t))
                    v.tensor_copy(xT[b], ps[b][:, 0:D]).then_inc(xt.sem, 1)

                def v_gc(t, b):
                    v.wait_ge(*gt.after(t))
                    v.tensor_tensor(gate[:, bass.ds(t * NG, NG)], ps[2 + b][:, 0:NG], gbr, ALU.add).then_inc(gc.sem, 1)
                tiles(v, (v_xt, 0), (v_gc, 1))

        sw1 = wreg[:, 0:512].rearrange("p (c n) -> p c n", c=2)
        sw2 = wreg[:, 512:768].rearrange("p (c n) -> p c n", c=2)
        sw3 = wreg[:, 768:1024]
        ew1 = wreg[:, 1024:2048].rearrange("p (e c n) -> p e c n", e=NG, c=2)
        ew2 = wreg[:, 2048:2560].rearrange("p (e n) -> p e n", n=P)
        ew3 = wreg[:, 2560:3072].rearrange("p (q n) -> p q n", n=D)
        sb1c, eb1c, sb2c, eb2c = wreg[:, 3072:3074], wreg[:, 3074:3078], wreg[:, 3078:3079], wreg[:, 3079:3081]
        bend = wreg[0:NG + 1, 3328:3584]
        with nc.Block() as block:
            s_v, s_a, s_w, s_z5 = sem("m_v"), sem("m_a"), sem("m_w"), sem("m_z")
            mxg, sm, rk, t_a, t_b = gsml[:, 0:T], gsml[:, T:2 * T], newton[:, 0:T], gtmp[:, 200:200 + T], gtmp[:, 250:250 + T]
            rank = gtmp[:, 0:T * NG].rearrange("p (t e) -> p t e", e=NG)

            @block.gpsimd
            def _(g):
                g.memset(wreg[:, 2048:2560], 0.0).then_inc(s_z5, 1)

            @block.sync
            def _(sp):
                def ld(dst, src, slow=False):
                    sp.dma_start(dst, src, allow_slow_non_contiguous=slow).then_inc(s_w, 16)
                ld(sw1, A["L1_ffn_sW1"].rearrange("(c p) n -> p c n", p=P))
                ld(sw2, A["L1_ffn_sW2"].rearrange("(c p) n -> p c n", p=P))
                ld(sw3, A["L1_ffn_sW3"])
                for e in range(NG):
                    ld(ew1[:, e, :, :], A["L1_ffn_eW1"][e].rearrange("(c p) n -> p c n", p=P))
                    ld(ew3[64 * (e % 2):64 * (e % 2) + 64, e // 2, :], A["L1_ffn_eW3"][e])
                    ld(eb2c[64 * (e % 2):64 * (e % 2) + 64, e // 2:e // 2 + 1], A["L1_ffn_eb2"][e].rearrange("(p a) -> p a", a=1), slow=True)
                sp.wait_ge(s_z5, 1)
                for e in range(NG):
                    ld(ew2[:, e, 64 * (e % 2):64 * (e % 2) + 64], A["L1_ffn_eW2"][e])
                ld(sb1c, A["L1_ffn_sb1"].rearrange("(c p) -> p c", p=P), slow=True)
                ld(eb1c, A["L1_ffn_eb1"].rearrange("e p -> p e"), slow=True)
                ld(sb2c, A["L1_ffn_sb2"].rearrange("(p a) -> p a", a=1), slow=True)
                ld(bend[0:NG], A["L1_ffn_eb3"])
                ld(bend[NG:NG + 1], A["L1_ffn_sb3"].rearrange("(a n) -> a n", a=1))
                sp.wait_ge(s_w, (3 + 3 * NG + NG + 5) * 16)

            @block.scalar
            def _(a):
                a.wait_ge(s_v, 2)
                a.activation(lgt, lgt, ACT.Exp).then_inc(s_a, 1)
                a.wait_ge(s_v, 42)
                a.activation(rank, rank, ACT.Exp).then_inc(s_a, 1)

            @block.vector
            def _(v):
                link = Chain(v, s_v)
                link(v.tensor_reduce(mxg, lgt, AX.X, ALU.max))
                link(v.tensor_tensor(lgt, lgt, wide(mxg, NG), ALU.subtract))
                v.wait_ge(s_a, 1)
                link(v.tensor_reduce(sm, lgt, AX.X, ALU.add))
                link(v.reciprocal(sm, sm))
                link(v.tensor_tensor(lgt, lgt, wide(sm, NG), ALU.mult))
                for e in range(NG):
                    first = True
                    for j in range(NG):
                        if j == e:
                            continue
                        dst = rank[:, :, e] if first else t_a
                        link(v.tensor_tensor(dst, lgt[:, :, j], lgt[:, :, e], ALU.is_ge if j < e else ALU.is_gt))
                        if not first:
                            link(v.tensor_tensor(rank[:, :, e], rank[:, :, e], t_a, ALU.add))
                        first = False
                link(v.tensor_reduce(mxg, lgt, AX.X, ALU.max))
                for e in range(NG):
                    link(v.tensor_scalar(rank[:, :, e], rank[:, :, e], 2.0, None, ALU.is_lt))
                    link(v.tensor_tensor(lgt[:, :, e], lgt[:, :, e], mxg, ALU.subtract))
                for e in range(NG):
                    link(v.tensor_copy(gate[:, 200 + e * T:200 + (e + 1) * T] if e < 3 else newton[:, T:2 * T], rank[:, :, e]))
                for e in range(NG):
                    link(v.tensor_copy(rank[:, :, e], lgt[:, :, e]))
                v.wait_ge(s_a, 2)
                for e in range(NG):
                    sel = gate[:, 200 + e * T:200 + (e + 1) * T] if e < 3 else newton[:, T:2 * T]
                    link(v.tensor_tensor(rank[:, :, e], rank[:, :, e], sel, ALU.mult))
                link(v.tensor_reduce(sm, rank, AX.X, ALU.add))
                link(v.reciprocal(sm, sm))
                link(v.tensor_tensor(lgt, rank, wide(sm, NG), ALU.mult))

        wst = [small[:, 8 * b:8 * b + NG + 1] for b in range(2)]
        wT = [small[0:NG + 1, 64 + b * P:64 + (b + 1) * P] for b in range(2)]
        a1 = [rows[:, b * 768:(b + 1) * 768] for b in range(2)]
        a2 = [rows[:, 1536 + b * 384:1536 + (b + 1) * 384] for b in range(2)]
        with nc.Block() as block:
            l1, r1, l2, r2, l3, wc, wt, wtc, ad = steps("n_", "l1 r1 l2 r2 l3 wc wt wtc ad")
            s_o, s_c, s_one = sem("n_out"), sem("n_chain"), sem("n_one")

            @block.sync
            def _(sp):
                with sp.Fori(0, T - 1) as i:
                    sp.wait_ge(*ad.after(i))
                    sp.dma_start(out[bass.ds(i * P, P), :], R[:, bass.ds(i * D, D)]).then_inc(s_o, 16)
                sp.wait_ge(*ad.after(T - 1))
                sp.dma_start(out[(T - 1) * P:N, :], R[0:LAST, (T - 1) * D:T * D]).then_inc(s_o, 16)
                sp.wait_ge(s_o, T * 16)

            @block.scalar
            def _(a):
                start(a, r1, r2)

                def a_r1(t, b):
                    a.wait_ge(*l1.after(t))
                    a.wait_ge(*l2.room(t))
                    for k in range(6):
                        bias = sb1c[:, k:k + 1] if k < 2 else eb1c[:, k - 2:k - 1]
                        ins = a.activation(a1[b][:, k * P:(k + 1) * P], ps[k // 4][:, k % 4 * P:(k % 4 + 1) * P], ACT.Relu, bias=bias)
                    ins.then_inc(r1.sem, 1)

                def a_r2(t, b):
                    a.wait_ge(*l2.after(t))
                    a.wait_ge(*l3.room(t))
                    for k in range(3):
                        bias = sb2c if k < 1 else eb2c[:, k - 1:k]
                        ins = a.activation(a2[b][:, k * P:(k + 1) * P], ps[2][:, k * P:(k + 1) * P], ACT.Relu, bias=bias)
                    ins.then_inc(r2.sem, 1)
                tiles(a, (a_r1, 0), (a_r2, 0))

            @block.tensor
            def _(pe):
                start(pe, l1, l2, l3, wt)

                def p_l1(t, b):
                    pe.wait_ge(*r1.after(t - 1))
                    for k in range(6):
                        for c in range(2):
                            w = sw1[:, c, k * P:(k + 1) * P] if k < 2 else ew1[:, k - 2, c, :]
                            ins = pe.matmul(ps[k // 4][:, k % 4 * P:(k % 4 + 1) * P], w, XN[:, bass.ds(t * D + c * P, P)],
                                            start=c == 0, stop=c == 1)
                    ins.then_inc(l1.sem, 1)

                def p_l2(t, b):
                    pe.wait_ge(*r1.after(t))
                    pe.wait_ge(*r2.after(t - 1))
                    for c in range(2):
                        pe.matmul(ps[2][:, 0:P], sw2[:, c, :], a1[b][:, c * P:(c + 1) * P], start=c == 0, stop=c == 1)
                    for e in range(NG):
                        ins = pe.matmul(ps[2][:, (1 + e // 2) * P:(2 + e // 2) * P], ew2[:, e, :], a1[b][:, (2 + e) * P:(3 + e) * P],
                                        start=e % 2 == 0, stop=e % 2 == 1)
                    ins.then_inc(l2.sem, 1)
                    pe.wait_ge(*wc.after(t))
                    pe.wait_ge(*wtc.room(t))
                    pe.transpose(ps[6 + b][0:NG + 1, 0:P], wst[b], ident[:, :]).then_inc(wt.sem, 1)

                def p_l3(t, b):
                    pe.wait_ge(*r2.after(t))
                    pe.wait_ge(*ad.after(t - 1))
                    for e in range(NG):
                        q = slice(64 * (e % 2), 64 * (e % 2) + 64)
                        pe.matmul(ps[3 + e % 2][:, e // 2 * D:(e // 2 + 1) * D], a2[b][q, (1 + e // 2) * P:(2 + e // 2) * P], ew3[q, e // 2, :],
                                  start=True, stop=True)
                    pe.matmul(ps[5][:, 0:D], a2[b][:, 0:P], sw3, start=True, stop=False)
                    pe.wait_ge(*wtc.after(t))
                    pe.matmul(ps[5][:, 0:D], wT[b], bend, start=False, stop=True).then_inc(l3.sem, 1)
                tiles(pe, (p_l1, 0), (p_l3, 1), (p_l2, 0))

            @block.vector
            def _(v):
                start(v, wc, wtc, ad)
                chain = Chain(v, s_c, NG)
                for b in range(2):
                    v.memset(wst[b][:, NG:NG + 1], 1.0).then_inc(s_one, 1)

                def v_w(t, b):
                    v.wait_ge(*wt.room(t))
                    v.tensor_copy(wst[b][:, 0:NG], gate[:, bass.ds(t * NG, NG)]).then_inc(wc.sem, 1)

                def v_wt(t, b):
                    v.wait_ge(*wt.after(t))
                    v.wait_ge(*l3.room(t))
                    v.tensor_copy(wT[b], ps[6 + b][0:NG + 1, 0:P]).then_inc(wtc.sem, 1)

                def v_ad(t, b):
                    v.wait_ge(*l3.after(t))
                    chain.tile(t)
                    x = R[:, col(t)]
                    chain(v.tensor_tensor(x, x, ps[5][:, 0:D], ALU.add))
                    for e in range(NG):
                        ins = v.scalar_tensor_tensor(x, ps[3 + e % 2][:, e // 2 * D:(e // 2 + 1) * D], gate[:, bass.ds(t * NG + e, 1)], x,
                                                     ALU.mult, ALU.add)
                        if e < NG - 1:
                            chain(ins)
                        else:
                            ins.then_inc(ad.sem, 1)
                tiles(v, (v_w, 0), (v_wt, 0), (v_ad, 1))


_INPUTS = ["x", "src", "dst", "L0_gnn_W1", "L0_gnn_b1", "L0_gnn_W2", "L0_gnn_b2", "L0_mix_W_qkv", "L0_mix_W_out", "L0_mix_b_out",
           "L0_ffn_W1", "L0_ffn_b1", "L0_ffn_Wg", "L0_ffn_bg", "L0_ffn_Wd", "L0_ffn_bd", "L1_gnn_W_self", "L1_gnn_W_neigh", "L1_gnn_b",
           "L1_mix_w_qkv", "L1_mix_b_qkv", "L1_mix_norm_g", "L1_mix_norm_b", "L1_mix_w_fc1", "L1_mix_b_fc1", "L1_mix_w_fc2",
           "L1_mix_b_fc2", "L1_ffn_sW1", "L1_ffn_sb1", "L1_ffn_sW2", "L1_ffn_sb2", "L1_ffn_sW3", "L1_ffn_sb3", "L1_ffn_eW1",
           "L1_ffn_eb1", "L1_ffn_eW2", "L1_ffn_eb2", "L1_ffn_eW3", "L1_ffn_eb3", "L1_ffn_gW", "L1_ffn_gb"]


def kernel(**inputs):
    import numpy as np
    import concourse.bacc as bacc
    from concourse.bass_utils import run_bass_kernel_spmd

    nc = bacc.Bacc("TRN2", target_bir_lowering=False, num_devices=1)
    arrays, aps = {}, {}
    for name in _INPUTS:
        a = np.ascontiguousarray(inputs[name])
        arrays["in_" + name] = a
        aps[name] = nc.dram_tensor("in_" + name, a.shape, mybir.dt.from_np(a.dtype), kind="ExternalInput").ap()
    out = nc.dram_tensor("out_x", (N, D), F32, kind="ExternalOutput").ap()
    build(nc, aps, out)
    return run_bass_kernel_spmd(nc, [arrays], core_ids=[0]).results[0]["out_x"]
```

```python
from contextlib import ExitStack

import concourse.bass as bass
from concourse import mybir

F32 = mybir.dt.float32
BF16 = mybir.dt.bfloat16
I32 = mybir.dt.int32
ALU = mybir.AluOpType
ACT = mybir.ActivationFunctionType
AX = mybir.AxisListType

P = 128
N = 6250
D = 256
E = 106250
T = -(-N // P)
LAST = N - (T - 1) * P
CH = -(-E // P)
CHR = 896
KC = CHR // P
PAD_DST = 8191
RING = 16
VIS = -(-(CH + T - 1) // RING) * RING
VI = VIS // RING
VC = CHR // P
HID = 1024
NE = 8
HC = HID // P
REG = (T + 1) * P
JUNK = NE * REG
ZERO = JUNK + P
BLK = (N + NE * (P - 1)) // P
EPS = 1e-5
MAGIC = 1597463007.0


class Chain:

    def __init__(self, eng, sem, per=0):
        self.eng, self.sem, self.per, self.base, self.k = eng, sem, per, 0, 0

    def tile(self, t):
        assert self.k in (0, self.per)
        self.base, self.k = t * self.per, 0
        return self

    def __call__(self, ins):
        self.k += 1
        ins.then_inc(self.sem, 1)
        self.eng.wait_ge(self.sem, self.base + self.k)


class Step:

    def __init__(self, sem, depth=2):
        self.sem, self.depth = sem, depth

    def after(self, t):
        return self.sem, t + 1 + self.depth

    def room(self, t):
        return self.sem, t + 1


def tiles(eng, *parts, n=T, unroll=2):
    def turn(t, b):
        for part, lag in parts:
            if not isinstance(t, int) or 0 <= t - lag < n:
                part(t - lag, (b - lag) % unroll)

    lags = max(lag for _, lag in parts)
    head = max(3, lags) + (n - 2 - max(3, lags)) % unroll
    for t in range(head):
        turn(t, t % unroll)
    with eng.Fori(0, (n - 2 - head) // unroll) as i:
        for q in range(unroll):
            turn(unroll * i + head + q, (head + q) % unroll)
    for t in range(n - 2, n + lags):
        turn(t, t % unroll)


def build(nc, A, out):
    with ExitStack() as ctx:
        def sb(name, shape, dt=F32):
            return ctx.enter_context(nc.sbuf_tensor(name, shape, dt))

        stage_sems = []

        def sem(name, keep=False):
            s = nc.alloc_semaphore(name=name)
            if not keep:
                stage_sems.append(s)
            return s

        def retire_sems():
            nc.clear_and_free_semaphores(list(stage_sems))
            nc.all_engine_barrier()
            stage_sems.clear()

        def dram(name, shape, dt=F32):
            return nc.dram_tensor(name, shape, dt, kind="Internal").ap()

        XN = sb("XN", [P, T * D])
        AR = sb("AR", [P, T * D + T * (D + 1)])
        ACC = AR[:, 0:T * D]
        KV = AR[:, T * D:T * (2 * D + 1)].rearrange("p (t c) -> p t c", c=D + 1)
        KVf = AR[:, T * D:T * (2 * D + 1)]
        R = AR[:, T * D:2 * T * D]
        WD = AR[:, 0:NE * HC * D]
        rows = sb("rows", [P, RING * D])
        wreg = sb("wreg", [P, 3600])
        work = sb("work", [P, 2048])
        mring = sb("mring", [P, 4 * P])
        idx_stage = sb("idx_stage", [P, RING], I32)
        src_idx = sb("src_idx", [P, CHR], I32)
        dst_rel = sb("dst_rel", [P, CHR])
        acc_at = sb("acc_at", [1, CHR], I32)
        ident = sb("ident", [P, P])
        iota = sb("iota", [P, P])
        one = sb("one", [P, 1])
        bias_rows = sb("bias_rows", [P, 2 * D])
        stats = sb("stats", [P, 6])
        mv = sb("mv", [P, T, 6])
        rstd = sb("rstd", [P, T])
        nmr = sb("nmr", [P, T])
        dinv = sb("dinv", [P, T])
        invdeg = sb("invdeg", [P, T])
        deg = sb("deg", [P, T])
        newton = sb("newton", [P, 2 * T])
        gates = sb("gates", [P, 2 * T * NE])
        gate = gates[:, 0:T * NE]
        gtmp = gates[:, T * NE:2 * T * NE]
        gsml = sb("gsml", [P, 2 * T])
        ps = [ctx.enter_context(nc.psum_tensor(f"ps{b}", [P, 512], F32)) for b in range(8)]
        table = [dram(f"table{n}", [T * P, D]) for n in range(3)]
        src_pad, dst_pad = dram("src_pad", [CHR, P], I32), dram("dst_pad", [CHR, P], I32)
        at_dram = dram("at_dram", [CHR], I32)
        h_sorted = dram("h_sorted", [ZERO + P, HID])
        y_sorted = dram("y_sorted", [BLK * P, D])
        pos_f = sb("pos_f", [P, T])
        pos_all = sb("pos_all", [P, T], I32)
        prob = sb("prob", [P, T])

        s_pool0 = sem("s_pool0", keep=True)
        s_mm = sem("s_mm", keep=True)
        s_ac = sem("s_ac", keep=True)
        s_ab = sem("s_ab", keep=True)
        s_m = sem("s_m", keep=True)
        s_st = sem("s_st", keep=True)
        s_go = sem("s_go", keep=True)
        s_g = [sem(f"s_g{u}", keep=True) for u in range(RING)]

        def bc(ap, parts=P):
            return ap.partition_broadcast(parts)

        def loads(engine, ap, most):
            return nc.values_load_multi_w_load_instructions(ap, engines=(engine,), min_val=0, max_val=most)[1]

        def rsqrt(v, link, x, y, t, n):
            yi, ti = y.bitcast(I32), t.bitcast(I32)
            link(v.tensor_scalar(ti, x.bitcast(I32), 1, None, ALU.logical_shift_right))
            link(v.tensor_scalar(yi, ti, -1.0, MAGIC, ALU.mult, ALU.add))
            for _ in range(4):
                link(v.tensor_tensor(t, y, y, ALU.mult))
                link(v.tensor_tensor(t, t, x, ALU.mult))
                link(v.tensor_scalar(t, t, -0.5, 1.5, ALU.mult, ALU.add))
                link(v.tensor_tensor(y, y, t, ALU.mult))

        def stats_of(v, x, s_chain):
            def part(t, b):
                v.bn_stats(mv[:, bass.ds(t, 1), :].rearrange("p t c -> p (t c)"), x[:, bass.ds(t * D, D)]).then_inc(s_chain, 1)
            return part

        def norm_factors(v, link, var=newton[:, T:2 * T], tmp=newton[:, 0:T]):
            mean = nmr[:, :]
            link(v.tensor_tensor(tmp, mv[:, :, 1], mv[:, :, 4], ALU.subtract))
            link(v.tensor_tensor(tmp, tmp, tmp, ALU.mult))
            link(v.tensor_tensor(var, mv[:, :, 2], mv[:, :, 5], ALU.add))
            link(v.tensor_scalar(var, var, 1.0 / D, EPS, ALU.mult, ALU.add))
            link(v.scalar_tensor_tensor(var, tmp, 0.25, var, ALU.mult, ALU.add))
            rsqrt(v, link, var, rstd[:, :], tmp, T)
            link(v.tensor_tensor(mean, mv[:, :, 1], mv[:, :, 4], ALU.add))
            link(v.scalar_tensor_tensor(nmr[:, :], mean, -0.5, rstd[:, :], ALU.mult, ALU.mult))

        e_i = KVf[:, 0:2 * KC * P].bitcast(I32).rearrange("p (a k e) -> p a k e", a=2, k=KC)
        e_f = KVf[:, 2000:2000 + KC * P]
        d_t = KVf[:, 3000:3000 + CHR]
        hi_i = KVf[:, 4000:4000 + CHR].bitcast(I32)
        hi = KVf[:, 5000:5000 + CHR]
        ones = KVf[:, 7000:7000 + P]
        iota_b = KVf[:, 7200:7200 + P // 2].bitcast(BF16)
        GR = 16
        oh_lo = [rows[:, b * 1024:b * 1024 + GR * P // 2].bitcast(BF16) for b in range(2)]
        oh_hi = [rows[:, 2048 + b * 512:2048 + b * 512 + GR * 32].bitcast(BF16) for b in range(2)]
        half = 512 // GR
        groups = (half, -(-CH // GR) - half)
        with nc.Block() as block:
            s_x, s_e, s_sp, s_cst, s_iota = (sem(n) for n in ("x_in", "e_in", "e_pad", "consts", "iotas"))
            s_ef, s_et, s_hr, s_lo, s_hd, s_ha, s_hi, s_hm = (sem(n) for n in "ef et high_ready one_lo hi_diff hi_abs one_hi hm".split())
            s_ds, s_tot, s_cv, s_vr, s_vf, s_vt = (sem(n) for n in ("ds", "tot", "cv", "vr", "vf", "vt"))
            s_at, s_ad, s_v0, s_lnf, s_xn, s_ve, s_sl = (sem(n) for n in ("at", "ad", "v0", "lnf", "xn0", "ve", "sl"))

            @block.sync
            def _(sp):
                sp.wait_ge(s_pool0, 1)
                for a, name in enumerate(("src", "dst")):
                    full = (CH - 1) // P * P
                    e = A[name]
                    sp.dma_start(e_i[:, a, 0:KC - 1, :], e[0:full * P].rearrange("(k p e) -> p k e", p=P, e=P)).then_inc(s_e, 16)
                    sp.dma_start(e_i[0:CH - 1 - full, a, KC - 1, :],
                                 e[full * P:(CH - 1) * P].rearrange("(p e) -> p e", e=P)).then_inc(s_e, 16)
                    sp.dma_start(e_i[CH - 1 - full:CH - full, a, KC - 1, 0:E - (CH - 1) * P],
                                 e[(CH - 1) * P:E].rearrange("(p e) -> p e", p=1)).then_inc(s_e, 16)
                xv = XN[:, :].rearrange("p (t d) -> p t d", d=D)
                for q in range(4):
                    sp.dma_start(xv[:, 12 * q:12 * q + 12, :],
                                 A["x"][12 * q * P:12 * (q + 1) * P, :].rearrange("(t p) d -> p t d", p=P)).then_inc(s_x, 16)
                sp.dma_start(xv[0:LAST, T - 1, :], A["x"][(T - 1) * P:N, :]).then_inc(s_x, 16)
                sp.wait_ge(s_e, 6 * 16)
                sp.dma_start(src_pad.rearrange("(k p) e -> p k e", p=P), e_i[:, 0, :, :]).then_inc(s_sp, 16)
                sp.dma_start(dst_pad.rearrange("(k p) e -> p k e", p=P), e_i[:, 1, :, :]).then_inc(s_sp, 16)
                sp.wait_ge(s_at, 1)
                sp.dma_start(at_dram.rearrange("(k p) -> p k", p=P), gtmp[:, 0:VC].bitcast(I32), allow_slow_non_contiguous=True).then_inc(s_ad, 16)
                sp.wait_ge(s_ad, 16)
                sp.dma_start(acc_at[0:1, :], at_dram.rearrange("(a n) -> a n", a=1)).then_inc(s_ad, 16)
                sp.wait_ge(s_ad, 32)

            @block.gpsimd
            def _(g):
                g.memset(e_i[:, 0, :, :], 0).then_inc(s_cst, 1)
                g.memset(e_i[:, 1, :, :], PAD_DST).then_inc(s_cst, 1)
                g.memset(XN[:, (T - 1) * D:T * D], 0.0).then_inc(s_cst, 1)
                g.wait_ge(s_cst, 3)
                g.sem_inc(s_pool0, 1)
                g.memset(ident[:, :], 0.0).then_inc(s_cst, 1)
                g.memset(ones[:, :], 1.0).then_inc(s_cst, 1)
                g.wait_ge(s_cst, 5)
                g.affine_select(out=ident[:, :], in_=ident[:, :], compare_op=ALU.not_equal, fill=1.0, base=0,
                                pattern=[[-1, P]], channel_multiplier=1).then_inc(s_cst, 1)
                g.memset(one[:, :], 1.0).then_inc(s_cst, 1)
                iv = idx_stage[:, 0:VC]
                g.iota(hi_i[:, 0:P], pattern=[[1, P]], base=0, channel_multiplier=0).then_inc(s_iota, 1)
                g.iota(iv, pattern=[[P, VC]], base=0, channel_multiplier=1).then_inc(s_iota, 1)
                g.wait_ge(s_hr, 1)
                with g.Fori(0, sum(groups) // 2) as i:
                    for b in range(2):
                        g.wait_ge(s_hm, 2 * i + b + 1)
                        g.tensor_tensor(oh_hi[b][:, 0:GR * T].rearrange("p (k n) -> p k n", n=T), iota[:, 0:T].unsqueeze(1).broadcast_to([P, GR, T]),
                                        hi[:, bass.ds((2 * i + b) * GR, GR)].unsqueeze(2).broadcast_to([P, GR, T]),
                                        ALU.subtract).then_inc(s_hd, 1)
                g.wait_ge(s_sp, 32)
                g.wait_ge(s_cv, 1)
                for k in range(VC):
                    for a, pad in enumerate((src_pad, dst_pad)):
                        g.indirect_dma_start(out=e_i[:, a, k, :], out_offset=None, in_=pad,
                                             in_offset=bass.IndirectOffsetOnAxis(ap=newton[:, k:k + 1].bitcast(I32), axis=0)
                                             ).then_inc(s_vr, 16)

            @block.scalar
            def _(a):
                a.wait_ge(s_cst, 7)
                a.activation(prob[:, 0:1], ident[:, 0:1], ACT.Identity)
                with a.Fori(0, sum(groups) // 2) as i:
                    for b in range(2):
                        d = oh_hi[b][:, 0:GR * T]
                        a.wait_ge(s_hd, 2 * i + b + 1)
                        a.activation(d, d, ACT.Abs).then_inc(s_ha, 1)
                        a.wait_ge(s_ha, 2 * i + b + 1)
                        a.activation(d, d, ACT.Relu, scale=-1.0, bias=one[:, :]).then_inc(s_hi, 1)
                a.wait_ge(s_lnf, 1)
                with a.Fori(0, T) as i:
                    x = XN[:, bass.ds(i * D, D)]
                    a.activation(x, x, ACT.Identity, bias=nmr[:, bass.ds(i, 1)], scale=rstd[:, bass.ds(i, 1)]).then_inc(s_xn, 1)

            @block.tensor
            def _(pe):
                pe.sem_inc(s_mm, RING)
                pe.wait_ge(s_cst, 6)
                pe.wait_ge(s_ef, 1)
                for k in range(KC):
                    pe.transpose(ps[k // 4][:, k % 4 * P:k % 4 * P + P], e_f[:, k * P:(k + 1) * P], ident[:, :]).then_inc(s_et, 1)
                pe.sem_inc(s_hm, 2)

                def count(c, b):
                    pe.wait_ge(s_lo, c + 1)
                    pe.wait_ge(s_hi, c + 1)
                    for k in range(GR):
                        ins = pe.matmul(ps[2][:, 0:T], oh_lo[b][:, k * P:(k + 1) * P], oh_hi[b][:, k * T:(k + 1) * T],
                                        start=isinstance(c, int) and c == k == 0, stop=False, skip_group_check=True)
                    ins.then_inc(s_hm, 1)
                for c in range(2):
                    count(c, c)
                with pe.Fori(1, sum(groups) // 2) as i:
                    for b in range(2):
                        count(2 * i + b, b)
                pe.wait_ge(s_ds, 1)
                pe.matmul(ps[3][:, 0:T], ones[:, :], deg[:, :], start=True, stop=True).then_inc(s_tot, 1)
                for k in range(VC):
                    pe.wait_ge(s_vf, 2 * k + 2)
                    if k >= 2:
                        pe.wait_ge(s_ve, 2 * k - 2)
                    for a in range(2):
                        pe.transpose(ps[4 + k % 2][:, a * P:a * P + P], work[:, (2 * (k % 2) + a) * P:(2 * (k % 2) + a + 1) * P],
                                     ident[:, :]).then_inc(s_vt, 1)

            @block.vector
            def _(v):
                link = Chain(v, s_v0)
                v.sem_inc(s_ac, 4)
                v.wait_ge(s_iota, 2)
                link(v.tensor_copy(iota[:, :], hi_i[:, 0:P]))
                link(v.tensor_copy(iota_b[:, :], iota[:, :]))
                vf = gtmp[:, 8:8 + VC]
                link(v.tensor_copy(vf, idx_stage[:, 0:VC]))
                v.wait_ge(s_e, 6 * 16)
                v.tensor_copy(e_f, e_i[:, 1, :, :].rearrange("p k e -> p (k e)")).then_inc(s_ef, 1)
                v.wait_ge(s_et, KC)
                d_i = e_f.bitcast(I32)
                for h in range(2):
                    n = min(512, CHR - 512 * h)
                    link(v.tensor_copy(d_t[:, 512 * h:512 * h + n], ps[h][:, 0:n]))
                    link(v.tensor_copy(d_i[:, 512 * h:512 * h + n], ps[h][:, 0:n]))
                link(v.tensor_scalar(hi_i, d_i, 7, None, ALU.arith_shift_right))
                link(v.tensor_copy(hi, hi_i))
                v.sem_inc(s_hr, 1)
                for h in range(2):
                    n = min(512, CHR - 512 * h)
                    link(v.scalar_tensor_tensor(ps[4 + h][:, 0:n], hi[:, 512 * h:512 * h + n], -float(P), d_t[:, 512 * h:512 * h + n],
                                                ALU.mult, ALU.add))
                for h in range(2):
                    with v.Fori(0, groups[h] // 2) as i:
                        for b in range(2):
                            v.wait_ge(s_hm, 2 * i + b + h * half + 1)
                            v.tensor_tensor(oh_lo[b].rearrange("p (k n) -> p k n", n=P), iota_b.unsqueeze(1).broadcast_to([P, GR, P]),
                                            ps[4 + h][:, bass.ds((2 * i + b) * GR, GR)].unsqueeze(2).broadcast_to([P, GR, P]),
                                            ALU.is_equal).then_inc(s_lo, 1)
                v.wait_ge(s_hm, sum(groups) + 2)
                link(v.tensor_copy(deg[:, :], ps[2][:, 0:T]))
                v.sem_inc(s_ds, 1)
                t49 = newton[:, T:2 * T]
                link(v.tensor_scalar(t49, deg[:, :], 1.0, None, ALU.add))
                rsqrt(v, link, t49, dinv[:, :], newton[:, 0:T], T)
                link(v.tensor_scalar(t49, deg[:, :], 1.0, None, ALU.max))
                link(v.reciprocal(invdeg[:, :], t49))
                v.wait_ge(s_tot, 1)
                c = [work[:, 1024 + 64 * n:1024 + 64 * n + T] for n in range(8)]
                tot, end, first, last, cnt, vend, dlt, junk = c
                link(v.tensor_copy(tot, ps[3][:, 0:T]))
                link(v.tensor_tensor_scan(end, ones[:, 0:T], tot, 0.0, ALU.mult, ALU.add))
                ji, fi, li = junk.bitcast(I32), first.bitcast(I32), last.bitcast(I32)
                link(v.tensor_tensor(junk, end, tot, ALU.subtract))
                link(v.tensor_copy(fi, junk))
                link(v.tensor_scalar(fi, fi, 7, None, ALU.arith_shift_right))
                link(v.tensor_scalar(li, end, -1.0, None, ALU.add))
                link(v.tensor_scalar(li, li, 7, None, ALU.arith_shift_right))
                link(v.tensor_copy(junk, fi))
                link(v.tensor_copy(cnt, li))
                link(v.tensor_tensor(cnt, cnt, junk, ALU.subtract))
                link(v.tensor_scalar(cnt, cnt, 1.0, None, ALU.add))
                link(v.scalar_tensor_tensor(cnt, tot, 0.0, cnt, ALU.is_gt, ALU.mult))
                link(v.tensor_tensor_scan(vend, ones[:, 0:T], cnt, 0.0, ALU.mult, ALU.add))
                link(v.tensor_tensor(dlt, junk, vend, ALU.subtract))
                link(v.tensor_tensor(dlt, dlt, cnt, ALU.add))
                tv, cd = gtmp[:, 16:16 + VC], gtmp[:, 24:24 + VC]
                for k in range(VC):
                    link(v.tensor_scalar(junk, vend, vf[:, k:k + 1], 0.0, ALU.is_le, ALU.add, accum_out=tv[:, k:k + 1]))
                    link(v.scalar_tensor_tensor(junk, iota[:, 0:T], tv[:, k:k + 1], dlt, ALU.is_equal, ALU.mult,
                                                accum_out=cd[:, k:k + 1]))
                link(v.tensor_tensor(cd, cd, vf, ALU.add))
                link(v.tensor_scalar(newton[:, 0:VC].bitcast(I32), cd, 0.0, CHR - 1.0, ALU.max, ALU.min))
                v.sem_inc(s_cv, 1)
                link(v.tensor_scalar(cd, tv, T - 1.0, float(D), ALU.min, ALU.mult))
                link(v.tensor_copy(gtmp[:, 0:VC].bitcast(I32), cd))
                v.sem_inc(s_at, 1)
                link(v.tensor_scalar(tv, tv, -float(P), None, ALU.mult))
                v.wait_ge(s_x, 5 * 16)
                tiles(v, (stats_of(v, XN, s_sl), 0))
                v.wait_ge(s_sl, T)
                norm_factors(v, link, gsml[:, 0:T], gsml[:, T:2 * T])
                v.sem_inc(s_lnf, 1)
                v.wait_ge(s_vr, 2 * VC * 16)
                for k in range(VC):
                    if k >= 2:
                        v.wait_ge(s_vt, 2 * k - 2)
                    at = 2 * (k % 2) * P
                    v.tensor_copy(work[:, at:at + P], e_i[:, 0, k, :]).then_inc(s_vf, 1)
                    v.tensor_scalar(work[:, at + P:at + 2 * P], e_i[:, 1, k, :], tv[:, k:k + 1], None, ALU.add).then_inc(s_vf, 1)
                    v.wait_ge(s_vt, 2 * k + 2)
                    v.tensor_copy(src_idx[:, k * P:(k + 1) * P], ps[4 + k % 2][:, 0:P]).then_inc(s_ve, 1)
                    v.tensor_copy(dst_rel[:, k * P:(k + 1) * P], ps[4 + k % 2][:, P:2 * P]).then_inc(s_ve, 1)

        def col(t):
            return bass.ds(t * D, D)

        xrow = [work[:, b * D:(b + 1) * D] for b in range(2)]
        xT = [work[:, (2 + b) * D:(3 + b) * D] for b in range(2)]
        small = work[:, 1024:2048]
        bias_ps = ps[7]

        def load_bias(sp, dst, src, s):
            sp.dma_start(dst, src.partition_broadcast(P)).then_inc(s, 16)

        def start(eng, *steps):
            for step in steps:
                eng.sem_inc(step.sem, step.depth)

        def steps(prefix, names):
            return [Step(sem(prefix + n)) for n in names.split()]

        def to_table(sp, n, h, s_tab):
            with sp.Fori(0, T) as i:
                sp.wait_ge(*h.after(i))
                sp.dma_start(table[n][bass.ds(i * P, P), :], ACC[:, bass.ds(i * D, D)]).then_inc(s_tab, 16)
            sp.wait_ge(s_tab, T * 16)

        w1kv = wreg[:, 0:1024].rearrange("p (c n) -> p c n", c=2)
        kmax = small[:, 0:P]
        with nc.Block() as block:
            row, tp, xt, mm, kv, h, mx = steps("a_", "row tp xt mm kv h mx")
            s_w, s_tab, s_km, s_one = sem("a_w"), sem("a_tab"), sem("a_km"), sem("a_one")

            @block.sync
            def _(sp):
                sp.dma_start(w1kv[:, :, 0:D], A["L0_gnn_W1"].rearrange("(c p) n -> p c n", p=P)).then_inc(s_w, 16)
                sp.dma_start(w1kv[:, :, D:2 * D], A["L0_mix_W_qkv"][:, P:3 * P].rearrange("(c p) n -> p c n", p=P)).then_inc(s_w, 16)
                to_table(sp, 0, h, s_tab)

            @block.gpsimd
            def _(g):
                g.memset(KV[:, :, D:D + 1], 1.0).then_inc(s_one, 1)

            @block.scalar
            def _(a):
                start(a, row, xt)

                def a_row(t, b):
                    a.wait_ge(*tp.room(t))
                    a.copy(xrow[b], XN[:, col(t)]).then_inc(row.sem, 1)

                def a_xt(t, b):
                    a.wait_ge(*tp.after(t))
                    a.wait_ge(*mm.room(t))
                    a.copy(xT[b], ps[b][:, 0:D]).then_inc(xt.sem, 1)
                tiles(a, (a_row, 0), (a_xt, 0))

            @block.tensor
            def _(pe):
                start(pe, tp, mm)
                pe.wait_ge(s_w, 32)

                def p_tp(t, b):
                    pe.wait_ge(*row.after(t))
                    pe.wait_ge(*xt.room(t))
                    pe.transpose(ps[b][:, 0:P], xrow[b][:, 0:P], ident[:, :])
                    pe.transpose(ps[b][:, P:D], xrow[b][:, P:D], ident[:, :]).then_inc(tp.sem, 1)

                def p_mm(t, b):
                    pe.wait_ge(*xt.after(t))
                    for s in (kv, h, mx):
                        pe.wait_ge(*s.room(t))
                    pe.matmul(ps[2 + b][:, :], xT[b][:, 0:P], w1kv[:, 0, :], start=True, stop=False)
                    pe.matmul(ps[2 + b][:, :], xT[b][:, P:D], w1kv[:, 1, :], start=False, stop=True).then_inc(mm.sem, 1)
                tiles(pe, (p_tp, 0), (p_mm, 1))

            @block.vector
            def _(v):
                start(v, h, mx, kv)
                v.memset(kmax, -3.0e38).then_inc(s_km, 1)
                v.wait_ge(s_km, 1)

                def v_h(t, b):
                    v.wait_ge(*mm.after(t))
                    v.tensor_scalar(ACC[:, col(t)], ps[2 + b][:, 0:D], dinv[:, bass.ds(t, 1)], None, ALU.mult).then_inc(h.sem, 1)

                def v_mx(t, b):
                    v.wait_ge(*mx.after(t - 1))
                    n = LAST if isinstance(t, int) and t == T - 1 else P
                    v.tensor_tensor(kmax[0:n], kmax[0:n], ps[2 + b][0:n, D:D + P], ALU.max).then_inc(mx.sem, 1)

                def v_kv(t, b):
                    v.tensor_copy(KV[:, bass.ds(t, 1), 0:D].rearrange("p t c -> p (t c)"), ps[2 + b][:, D:2 * D]).then_inc(kv.sem, 1)
                tiles(v, (v_h, 0), (v_mx, 0), (v_kv, 0))

        erow = [small[:, (1 + b) * P:(2 + b) * P] for b in range(2)]
        nmax, nmat = gsml[:, 0:1], small[:, 3 * P:4 * P]
        wq = wreg[:, 0:D].rearrange("p (c n) -> p c n", c=2)
        wout = wreg[:, D:2 * D]
        g0 = wreg[:, 1024:1536].rearrange("p (c n) -> p c n", c=2)
        w2 = wreg[:, 1536:2048].rearrange("p (c n) -> p c n", c=2)
        wqT, m1 = wreg[:, 2048:2304], wreg[:, 2304:2560]
        cbd, cT = small[:, 4 * P:5 * P], small[:, 5 * P:6 * P]
        with nc.Block() as block:
            sub, ex, cx = steps("c_", "sub ex cx")
            s_w, s_v, s_p, s_a = sem("c_w"), sem("c_v"), sem("c_p"), sem("c_a")

            @block.sync
            def _(sp):
                sp.dma_start(wq, A["L0_mix_W_qkv"][:, 0:P].rearrange("(c p) n -> p c n", p=P)).then_inc(s_w, 16)
                sp.dma_start(wout, A["L0_mix_W_out"]).then_inc(s_w, 16)
                sp.dma_start(w2, A["L0_gnn_W2"].rearrange("(c p) n -> p c n", p=P)).then_inc(s_w, 16)
                sp.wait_ge(s_w, 48)

            @block.scalar
            def _(a):
                start(a, ex)

                def a_ex(t, b):
                    a.wait_ge(*sub.after(t))
                    a.wait_ge(*cx.room(t))
                    a.activation(erow[b], KV[:, bass.ds(t, 1), 0:P].rearrange("p t c -> p (t c)"), ACT.Exp).then_inc(ex.sem, 1)
                tiles(a, (a_ex, 0))

            @block.tensor
            def _(pe):
                start(pe, cx)
                pe.transpose(ps[0][:, 0:P], kmax, ident[:, :]).then_inc(s_p, 1)
                pe.wait_ge(s_v, 2)
                pe.matmul(ps[1][:, 0:P], nmat, ident[:, :], start=True, stop=True).then_inc(s_p, 1)

                def p_cx(t, b):
                    n = LAST if isinstance(t, int) and t == T - 1 else P
                    pe.wait_ge(*ex.after(t))
                    pe.matmul(ps[2][:, 0:P + 1], erow[b][0:n], KV[0:n, bass.ds(t, 1), P:D + 1].rearrange("p t c -> p (t c)"),
                              start=isinstance(t, int) and t == 0, stop=isinstance(t, int) and t == T - 1,
                              skip_group_check=True).then_inc(cx.sem, 1)
                tiles(pe, (p_cx, 0))
                pe.wait_ge(s_w, 48)
                for c in range(2):
                    pe.transpose(ps[3][:, c * P:(c + 1) * P], wq[:, c, :], ident[:, :]).then_inc(s_p, 1)
                pe.wait_ge(s_v, 9)
                pe.transpose(ps[4][:, 0:P], cbd, ident[:, :]).then_inc(s_p, 1)
                pe.wait_ge(s_v, 10)
                pe.matmul(ps[5][:, 0:D], cT, wout, start=True, stop=True).then_inc(s_p, 1)
                pe.wait_ge(s_v, 11)
                for c in range(2):
                    pe.matmul(ps[6][:, c * D:(c + 1) * D], wqT[:, c * P:(c + 1) * P], m1, start=True, stop=True).then_inc(s_p, 1)

            @block.vector
            def _(v):
                link = Chain(v, s_v)
                start(v, sub)
                v.wait_ge(s_p, 1)
                link(v.tensor_reduce(nmax, ps[0][:, 0:P], AX.X, ALU.max, negate=True))
                link(v.tensor_copy(nmat, nmax.broadcast_to([P, P])))
                v.wait_ge(s_p, 2)

                def v_sub(t, b):
                    k = KV[:, bass.ds(t, 1), 0:P].rearrange("p t c -> p (t c)")
                    v.tensor_tensor(k, k, ps[1][:, 0:P], ALU.add).then_inc(sub.sem, 1)
                tiles(v, (v_sub, 0))
                v.wait_ge(*cx.after(T - 1))
                link(v.reciprocal(nmax, ps[2][:, P:P + 1]))
                link(v.memset(cbd, 0.0))
                for q in range(4):
                    r = slice(32 * q, 32 * q + 32)
                    link(v.tensor_scalar(cbd[r, r], ps[2][r, r], nmax[r], 32.0 ** -0.5, ALU.mult, ALU.mult))
                v.wait_ge(s_p, 4)
                link(v.tensor_copy(wqT, ps[3][:, 0:D]))
                v.wait_ge(s_p, 5)
                link(v.tensor_copy(cT, ps[4][:, 0:P]))
                v.wait_ge(s_p, 6)
                link(v.tensor_copy(m1, ps[5][:, 0:D]))
                v.wait_ge(s_p, 8)
                link(v.tensor_copy(wreg[:, 1024:1536], ps[6][:, :]))

        def over_turns(eng, turn, lead, side):
            def some(i, parts):
                turn(i + lead, [i - n if n in parts else None for n in range(4)])

            if side is None:
                turn(0, [None] * 4)
                with eng.Fori(1, VI) as i:
                    turn(i, [None] * 4)
                return
            for i in range(lead):
                turn(i, [None] * 4)
            some(0, (0,))
            some(1, (0, 1))
            some(2, (0, 1, 2))
            with eng.Fori(3, T) as i:
                some(i, (0, 1, 2, 3))
            some(T, (1, 2, 3))
            some(T + 1, (2, 3))
            some(T + 2, (3,))
            with eng.Fori(T + 3, VI - lead) as i:
                some(i, ())

        def aggregate(phase, tab, sync=None, side=None):
            mats = (mring[:, :], gates[:, 0:4 * P])

            def of(name, eng):
                return side[name](eng) if side and name in side else lambda u, work: None

            with nc.Block() as block:
                if sync:
                    block.sync(sync)

                @block.scalar
                def _(a):
                    extra = of("scalar", a)

                    def matrices(i, q):
                        m = mats[q % 2]
                        for k in range(4):
                            a.activation(m[:, k * P:(k + 1) * P], iota[:, :], ACT.Abs, scale=-1.0,
                                         bias=dst_rel[:, bass.ds(i * RING + 4 * q + k, 1)]).then_inc(s_ab, 1)
                        a.wait_ge(s_ab, (i + phase * VI) * RING + 4 * q + 4)
                        a.activation(m, m, ACT.Relu, scale=-1.0, bias=one[:, :]).then_inc(s_m, 1)

                    def turn(i, work):
                        for q in range(RING // 4):
                            extra(4 * q, work)
                            a.wait_ge(s_mm, (i + phase * VI) * RING + 4 * q + 4)
                            if not isinstance(i, int) or i < VI:
                                a.copy(idx_stage[:, 4 * q:4 * q + 4], src_idx[:, bass.ds(i * RING + 4 * q, 4)]).then_inc(s_st, 1)
                            if q < 2 and not (isinstance(i, int) and i == 0):
                                matrices(i - 1, q + 2)
                            if q >= 2 and not (isinstance(i, int) and i == VI):
                                matrices(i, q - 2)
                    over_turns(a, turn, 1, side)
                    turn(VI, [None] * 4)

                @block.gpsimd
                def _(g):
                    extra = of("gpsimd", g)

                    def turn(i, work):
                        for q in range(RING // 4):
                            extra(4 * q, work)
                            g.wait_ge(s_st, (i + phase * VI) * (RING // 4) + q + 1)
                            g.sem_inc(s_go, 1)
                            for u in range(4 * q, 4 * q + 4):
                                g.indirect_dma_start(out=rows[:, u * D:(u + 1) * D], out_offset=None, in_=tab,
                                                     in_offset=bass.IndirectOffsetOnAxis(ap=idx_stage[:, u:u + 1], axis=0)
                                                     ).then_inc(s_g[u], 16)
                    over_turns(g, turn, 1, side)

                @block.tensor
                def _(pe):
                    extra = of("tensor", pe)

                    def turn(i, work):
                        at = i + phase * VI
                        for u in range(RING):
                            extra(u, work)
                            pe.wait_ge(s_g[u], at * 16 + 16)
                            pe.wait_ge(s_m, at * (RING // 4) + u // 4 + 1)
                            pe.wait_ge(s_ac, at * RING + u + 1)
                            pe.matmul(ps[u % 4][:, 0:D], mats[u // 4 % 2][:, u % 4 * P:(u % 4 + 1) * P], rows[:, u * D:(u + 1) * D],
                                      start=True, stop=True).then_inc(s_mm, 1)
                    over_turns(pe, turn, 0, side)

                @block.vector
                def _(v):
                    extra = of("vector", v)

                    def turn(i, work):
                        first = (i + phase * VI) * RING
                        for u in range(RING):
                            extra(u, work)
                            if u % 4 == 0:
                                at = loads(mybir.EngineType.DVE, acc_at[0:1, bass.ds(i * RING + u, 4)], (T - 1) * D)
                            v.wait_ge(s_mm, first + u + 1 + RING)
                            v.wait_ge(s_ac, first + u + 4)
                            acc = ACC[:, bass.ds(at[u % 4], D)]
                            v.tensor_tensor(acc, acc, ps[u % 4][:, 0:D], ALU.add).then_inc(s_ac, 1)
                        extra(RING, work)
                    over_turns(v, turn, 0, side)

        b_row, b_row2 = bias_rows[:, 0:D], bias_rows[:, D:2 * D]
        s_r0 = sem("r_in", keep=True)
        Rt = R.rearrange("p (t d) -> p t d", d=D)

        def fetch_x(sp):
            sp.wait_ge(s_z, 1)
            for q in range(4):
                sp.dma_start(Rt[:, 12 * q:12 * q + 12, :],
                             A["x"][12 * q * P:12 * (q + 1) * P, :].rearrange("(t p) d -> p t d", p=P)).then_inc(s_r0, 16)
            sp.dma_start(Rt[0:LAST, T - 1, :], A["x"][(T - 1) * P:N, :]).then_inc(s_r0, 16)
            load_bias(sp, b_row, A["L0_gnn_b1"], s_r0)
            load_bias(sp, b_row2, A["L0_mix_b_out"], s_r0)
            sp.wait_ge(s_r0, 7 * 16)

        s_z = sem("r_zero")
        with nc.Block() as block:
            @block.gpsimd
            def _(g):
                g.memset(R[:, (T - 1) * D:T * D], 0.0).then_inc(s_z, 1)
        r_row, r_xT = xrow[0], xT[0]
        row, tp, xt, gm, rb, r = [Step(sem("r_" + n), 1) for n in "row tp xt gm rb r".split()]

        def mix_scalar(a):
            start(a, row, xt)

            def side(u, work):
                t0 = work[0]
                if u == 0 and t0 is not None:
                    a.wait_ge(*tp.room(t0))
                    a.copy(r_row, XN[:, col(t0)]).then_inc(row.sem, 1)
                if u == 8 and t0 is not None:
                    a.wait_ge(*tp.after(t0))
                    a.wait_ge(*gm.room(t0))
                    a.copy(r_xT, ps[4][:, 0:D]).then_inc(xt.sem, 1)
            return side

        def mix_tensor(pe):
            start(pe, tp, gm)

            def side(u, work):
                t0 = work[0]
                if u == 5 and t0 is not None:
                    pe.wait_ge(*row.after(t0))
                    pe.wait_ge(*r.room(t0))
                    pe.transpose(ps[4][:, 0:P], r_row[:, 0:P], ident[:, :])
                    pe.transpose(ps[4][:, P:D], r_row[:, P:D], ident[:, :]).then_inc(tp.sem, 1)
                if u == 13 and t0 is not None:
                    pe.wait_ge(*xt.after(t0))
                    for c in range(2):
                        ins = pe.matmul(ps[4][:, 0:D], r_xT[:, c * P:(c + 1) * P], g0[:, c, :], start=c == 0, stop=c == 1)
                    ins.then_inc(gm.sem, 1)
            return side

        def mix_vector(v):
            start(v, rb, r)

            def side(u, work):
                t0 = work[0]
                if u == 9 and t0 is not None:
                    v.wait_ge(s_r0, 7 * 16)
                    v.tensor_tensor(R[:, col(t0)], R[:, col(t0)], b_row2, ALU.add).then_inc(rb.sem, 1)
                if u == RING and t0 is not None:
                    v.wait_ge(*gm.after(t0))
                    v.wait_ge(*rb.after(t0))
                    v.tensor_tensor(R[:, col(t0)], R[:, col(t0)], ps[4][:, 0:D], ALU.add).then_inc(r.sem, 1)
            return side

        aggregate(0, table[0], fetch_x, side=dict(scalar=mix_scalar, tensor=mix_tensor, vector=mix_vector))

        x1 = [small[:, b * D:(b + 1) * D] for b in range(2)]
        with nc.Block() as block:
            tp, xt, mm, z, w1, h, wr = steps("b_", "tp xt mm z x1 h wr")
            s_tab, s_b = sem("b_tab"), sem("b_bias")

            @block.sync
            def _(sp):
                to_table(sp, 1, h, s_tab)

            @block.gpsimd
            def _(g):
                start(g, wr)

                def g_wr(t, b):
                    g.wait_ge(*w1.after(t))
                    g.tensor_copy(XN[:, col(t)], x1[b]).then_inc(wr.sem, 1)
                tiles(g, (g_wr, 0))

            @block.scalar
            def _(a):
                start(a, xt)

                def a_xt(t, b):
                    a.wait_ge(*tp.after(t))
                    a.wait_ge(*mm.room(t))
                    a.copy(xT[b], ps[b][:, 0:D]).then_inc(xt.sem, 1)
                tiles(a, (a_xt, 0))

            @block.tensor
            def _(pe):
                start(pe, tp, mm)

                def p_tp(t, b):
                    pe.wait_ge(*w1.after(t))
                    pe.wait_ge(*xt.room(t))
                    pe.transpose(ps[b][:, 0:P], x1[b][:, 0:P], ident[:, :])
                    pe.transpose(ps[b][:, P:D], x1[b][:, P:D], ident[:, :]).then_inc(tp.sem, 1)

                def p_mm(t, b):
                    pe.wait_ge(*xt.after(t))
                    pe.wait_ge(*h.room(t))
                    pe.matmul(ps[2 + b][:, 0:D], xT[b][:, 0:P], w2[:, 0, :], start=True, stop=False)
                    pe.matmul(ps[2 + b][:, 0:D], xT[b][:, P:D], w2[:, 1, :], start=False, stop=True).then_inc(mm.sem, 1)
                tiles(pe, (p_tp, 0), (p_mm, 1))

            @block.vector
            def _(v):
                start(v, z, w1, h)
                v.tensor_copy(bias_ps[:, 0:D], b_row).then_inc(s_b, 1)
                v.wait_ge(s_b, 1)

                def v_z(t, b):
                    v.wait_ge(*w1.room(t))
                    v.scalar_tensor_tensor(ps[4 + b][:, 0:D], ACC[:, col(t)], dinv[:, bass.ds(t, 1)], bias_ps[:, 0:D],
                                           ALU.mult, ALU.add).then_inc(z.sem, 1)

                def v_x1(t, b):
                    v.wait_ge(*z.after(t))
                    v.wait_ge(*tp.room(t))
                    v.wait_ge(*wr.room(t))
                    v.scalar_tensor_tensor(x1[b], ps[4 + b][:, 0:D], 0.0, XN[:, col(t)], ALU.max, ALU.add).then_inc(w1.sem, 1)

                def v_h(t, b):
                    v.wait_ge(*mm.after(t))
                    v.wait_ge(*z.after(t))
                    v.tensor_scalar(ACC[:, col(t)], ps[2 + b][:, 0:D], dinv[:, bass.ds(t, 1)], None, ALU.mult).then_inc(h.sem, 1)
                tiles(v, (v_z, 0), (v_x1, 1), (v_h, 3))

        def fetch_b2(sp):
            load_bias(sp, b_row, A["L0_gnn_b2"], s_r0)
            sp.wait_ge(s_r0, 8 * 16)
        aggregate(1, table[1], fetch_b2)

        with nc.Block() as block:
            z, xp, rx = steps("d_", "z xp rx")
            s_b, s_sl, s_n = sem("d_bias"), sem("d_stats"), sem("d_norm")

            @block.gpsimd
            def _(g):
                start(g, rx)

                def g_rx(t, b):
                    g.tensor_tensor(R[:, col(t)], R[:, col(t)], XN[:, col(t)], ALU.add).then_inc(rx.sem, 1)
                tiles(g, (g_rx, 0))

            @block.vector
            def _(v):
                start(v, z, xp)

                def v_z(t, b):
                    v.wait_ge(*xp.room(t))
                    v.scalar_tensor_tensor(ps[4 + b][:, 0:D], ACC[:, col(t)], dinv[:, bass.ds(t, 1)], b_row,
                                           ALU.mult, ALU.add).then_inc(z.sem, 1)

                def v_xp(t, b):
                    v.wait_ge(*z.after(t))
                    v.wait_ge(*rx.after(t))
                    v.scalar_tensor_tensor(XN[:, col(t)], ps[4 + b][:, 0:D], 0.0, R[:, col(t)], ALU.max, ALU.add).then_inc(xp.sem, 1)
                def v_st(t, b):
                    v.wait_ge(*xp.after(t))
                    st(t, b)
                st = stats_of(v, XN, s_sl)
                tiles(v, (v_z, 0), (v_xp, 1), (v_st, 2))
                v.wait_ge(s_sl, T)
                norm_factors(v, Chain(v, s_n))

        ff1 = wreg[:, 0:2048].rearrange("p (c n) -> p c n", c=2)
        b1row = wreg[:, 2048:2048 + HID]
        wg = wreg[:, 3072:3072 + HC * NE].rearrange("p (k n) -> p k n", n=NE)
        bgr, i8 = wreg[:, 3136:3144], wreg[:, 3144:3152]
        ltri = wreg[:, 3152:3152 + P]
        ones = wreg[:, 3280:3280 + P]
        valid, junk_row = wreg[:, 3408:3408 + T], wreg[:, 3457:3457 + T]
        cnt = wreg[:, 3506:3514]
        pcol = wreg[:, 3514:3515]
        hr = [AR[:, NE * (HC + 1) * D + b * HID:NE * (HC + 1) * D + (b + 1) * HID] for b in range(4)]
        hT = [rows[:, b % 2 * HID:(b % 2 + 1) * HID] for b in range(4)]
        l8, key, rnk = ([small[:, 64 * q + 8 * b:64 * q + 8 * b + 8] for b in (0, 1, 0, 1)] for q in range(3))
        m1x, km, pos = ([small[:, 256 + 2 * q + b:257 + 2 * q + b] for b in (0, 1, 0, 1)] for q in range(3))
        s_wd = sem("s_wd")
        bdtab = AR[:, NE * HC * D:NE * HC * D + NE * D]
        gate3 = gate.rearrange("p (t e) -> p t e", e=NE)
        gtmp3 = gtmp.rearrange("p (t e) -> p t e", e=NE)
        with nc.Block() as block:
            row, tp, xt, mm, hb, gl, t8, ht, lg, sl, pf, ps_ = steps("f_", "row tp xt mm hb gl t8 ht lg sl pf pos")
            s_w, s_sc, s_c1, s_c2, s_k, s_kc = sem("f_w"), [sem(f"f_sc{b}") for b in range(4)], sem("f_c1"), sem("f_c2"), sem("f_k"), sem("f_kc")

            @block.sync
            def _(sp):
                sp.dma_start(ff1, A["L0_ffn_W1"].rearrange("(c p) n -> p c n", p=P)).then_inc(s_w, 16)
                sp.dma_start(wg, A["L0_ffn_Wg"].rearrange("(k p) n -> p k n", p=P)).then_inc(s_w, 16)
                load_bias(sp, b1row, A["L0_ffn_b1"], s_w)
                load_bias(sp, bgr, A["L0_ffn_bg"], s_w)
                sp.wait_ge(s_w, 4 * 16)
                for e in range(NE):
                    sp.dma_start(WD[:, e * HC * D:(e + 1) * HC * D].rearrange("p (k n) -> p k n", n=D),
                                 A["L0_ffn_Wd"][e].rearrange("(k p) n -> p k n", p=P)).then_inc(s_wd, 16)
                load_bias(sp, bdtab, A["L0_ffn_bd"].rearrange("e n -> (e n)"), s_wd)

            @block.gpsimd
            def _(g):
                g.memset(ltri, 1.0).then_inc(s_k, 1)
                g.memset(ones, 1.0).then_inc(s_k, 1)
                g.memset(valid, 1.0).then_inc(s_k, 1)
                g.memset(junk_row, 0.0).then_inc(s_k, 1)
                g.iota(idx_stage[:, 0:1], pattern=[[0, 1]], base=0, channel_multiplier=1).then_inc(s_k, 1)
                g.iota(idx_stage[:, 8:16], pattern=[[REG, NE]], base=0, channel_multiplier=0).then_inc(s_k, 1)
                g.wait_ge(s_k, 6)
                g.affine_select(out=ltri, in_=ltri, compare_op=ALU.is_gt, fill=0.0, base=0, pattern=[[1, P]],
                                channel_multiplier=-1).then_inc(s_k, 1)
                g.affine_select(out=valid[:, T - 1:T], in_=valid[:, T - 1:T], compare_op=ALU.is_gt, fill=0.0, base=LAST,
                                pattern=[[0, 1]], channel_multiplier=-1).then_inc(s_k, 1)
                def g_sc(t, b):
                    g.wait_ge(*ps_.after(t))
                    g.wait_ge(*gl.after(t))
                    g.sem_inc(s_go, 1)
                    g.indirect_dma_start(out=h_sorted, out_offset=bass.IndirectOffsetOnAxis(ap=idx_stage[:, b:b + 1], axis=0),
                                         in_=hr[b], in_offset=None).then_inc(s_sc[b], 16)
                tiles(g, (g_sc, 0), unroll=4)
                for b in range(4):
                    g.wait_ge(s_sc[b], 16 * ((T - 1 - b) // 4 + 1))

            @block.scalar
            def _(a):
                start(a, row, gl, ht)

                def a_row(t, b):
                    a.wait_ge(*tp.room(t))
                    a.activation(xrow[b % 2], XN[:, col(t)], ACT.Identity, bias=nmr[:, bass.ds(t, 1)],
                                 scale=rstd[:, bass.ds(t, 1)]).then_inc(row.sem, 1)

                def a_gl(t, b):
                    a.wait_ge(*hb.after(t))
                    a.activation(hr[b], hr[b], ACT.Gelu).then_inc(gl.sem, 1)

                def a_ht(t, b):
                    a.wait_ge(*t8.after(t))
                    a.wait_ge(*lg.room(t))
                    a.copy(hT[b][:, 0:512], ps[6][:, :])
                    a.copy(hT[b][:, 512:1024], ps[7][:, :]).then_inc(ht.sem, 1)
                tiles(a, (a_row, 0), (a_ht, 3), (a_gl, 2), unroll=4)

            @block.tensor
            def _(pe):
                start(pe, tp, mm, t8, lg, pf)
                pe.wait_ge(s_w, 4 * 16)
                pe.wait_ge(s_k, 8)

                def p_tp(t, b):
                    pe.wait_ge(*row.after(t))
                    pe.wait_ge(*xt.room(t))
                    pe.transpose(ps[b % 2][:, 0:P], xrow[b % 2][:, 0:P], ident[:, :])
                    pe.transpose(ps[b % 2][:, P:D], xrow[b % 2][:, P:D], ident[:, :]).then_inc(tp.sem, 1)

                def p_mm(t, b):
                    pe.wait_ge(*xt.after(t))
                    pe.wait_ge(*hb.after(t - 1))
                    for c in range(2):
                        for h in range(2):
                            ins = pe.matmul(ps[2 + h][:, :], xT[b % 2][:, c * P:(c + 1) * P], ff1[:, c, h * 512:(h + 1) * 512],
                                            start=c == 0, stop=c == 1)
                    ins.then_inc(mm.sem, 1)

                def p_t8(t, b):
                    pe.wait_ge(*gl.after(t))
                    pe.wait_ge(*ht.after(t - 1))
                    for k in range(HC):
                        ins = pe.transpose(ps[6 + k // 4][:, k % 4 * P:(k % 4 + 1) * P], hr[b][:, k * P:(k + 1) * P], ident[:, :])
                    ins.then_inc(t8.sem, 1)

                def p_lg(t, b):
                    pe.wait_ge(*ht.after(t))
                    pe.wait_ge(*sl.after(t - 1))
                    for k in range(HC):
                        ins = pe.matmul(ps[4][:, 0:NE], hT[b][:, k * P:(k + 1) * P], wg[:, k, :], start=k == 0, stop=k == HC - 1)
                    ins.then_inc(lg.sem, 1)

                def p_pf(t, b):
                    pe.wait_ge(*sl.after(t))
                    pe.wait_ge(*ps_.after(t - 1))
                    pe.matmul(ps[5][:, 0:NE], ltri, gtmp[:, bass.ds(t * NE, NE)], start=True, stop=True)
                    pe.matmul(ps[5][:, NE:2 * NE], ones, gtmp[:, bass.ds(t * NE, NE)], start=True, stop=True).then_inc(pf.sem, 1)
                tiles(pe, (p_tp, 0), (p_mm, 1), (p_pf, 4), (p_lg, 3), (p_t8, 2), unroll=4)

            @block.vector
            def _(v):
                start(v, xt, hb, sl, ps_)
                link = Chain(v, s_kc)
                v.wait_ge(s_w, 4 * 16)
                v.wait_ge(s_k, 8)
                link(v.tensor_copy(pcol, idx_stage[:, 0:1]))
                link(v.tensor_copy(cnt, idx_stage[:, 8:16]))
                link(v.tensor_scalar(i8, iota[:, 0:NE], -1.0, float(NE), ALU.mult, ALU.add))
                link(v.tensor_scalar(junk_row, valid, -1.0, 1.0, ALU.mult, ALU.add))
                link(v.tensor_scalar(pos[0], pcol, float(JUNK), None, ALU.add))
                link(v.tensor_scalar(junk_row, junk_row, pos[0], None, ALU.mult))
                c1, c2 = Chain(v, s_c1, 5), Chain(v, s_c2, 4)

                def v_xt(t, b):
                    v.wait_ge(*tp.after(t))
                    v.wait_ge(*mm.room(t))
                    v.tensor_copy(xT[b % 2], ps[b % 2][:, 0:D]).then_inc(xt.sem, 1)

                def v_hb(t, b):
                    v.wait_ge(*mm.after(t))
                    v.wait_ge(*t8.room(t))
                    if not isinstance(t, int) or t >= 4:
                        v.wait_ge(s_sc[b], 4 * (t - b))
                    v.tensor_tensor(hr[b][:, 0:512], ps[2][:, :], b1row[:, 0:512], ALU.add)
                    v.tensor_tensor(hr[b][:, 512:1024], ps[3][:, :], b1row[:, 512:1024], ALU.add).then_inc(hb.sem, 1)

                def v_sl(t, b):
                    c1.tile(t)
                    v.wait_ge(*lg.after(t))
                    v.wait_ge(*pf.room(t))
                    c1(v.tensor_tensor(l8[b], ps[4][:, 0:NE], bgr, ALU.add))
                    c1(v.tensor_copy(gate[:, bass.ds(t * NE, NE)], l8[b]))
                    c1(v.tensor_reduce(m1x[b], l8[b], AX.X, ALU.max))
                    c1(v.scalar_tensor_tensor(key[b], l8[b], m1x[b], i8, ALU.is_equal, ALU.mult))
                    c1(v.tensor_reduce(km[b], key[b], AX.X, ALU.max))
                    v.tensor_scalar(gtmp[:, bass.ds(t * NE, NE)], key[b], km[b], valid[:, bass.ds(t, 1)], ALU.is_equal, ALU.mult).then_inc(sl.sem, 1)

                def v_pos(t, b):
                    c2.tile(t)
                    v.wait_ge(*pf.after(t))
                    if not isinstance(t, int) or t >= 4:
                        v.wait_ge(s_sc[b], 4 * (t - b))
                    c2(v.tensor_tensor(rnk[b], ps[5][:, 0:NE], cnt, ALU.add))
                    c2(v.scalar_tensor_tensor(key[b], rnk[b], 1.0, gtmp[:, bass.ds(t * NE, NE)], ALU.mult, ALU.mult, accum_out=pos[b]))
                    c2(v.tensor_tensor(cnt, cnt, ps[5][:, NE:2 * NE], ALU.add))
                    c2(v.tensor_scalar(idx_stage[:, b:b + 1], pos[b], junk_row[:, bass.ds(t, 1)], None, ALU.add))
                    v.tensor_copy(pos_f[:, bass.ds(t, 1)], idx_stage[:, b:b + 1]).then_inc(ps_.sem, 1)
                tiles(v, (v_xt, 0), (v_hb, 1), (v_pos, 4), (v_sl, 3), unroll=4)

        def wide(x, n):
            return x.unsqueeze(2).broadcast_to([P, T, n])

        zrow = rows[:, 0:HID]
        tail_i = idx_stage[:, 0:NE]
        ecol = small[:, 600:664]
        bt = [ecol[:, 8 * q:8 * q + 8] for q in range(4)]
        bcol = [ecol[:, 32 + q:33 + q] for q in range(8)]
        btab = [rows[0:1, 3 * HID + q * P:3 * HID + q * P + P].bitcast(I32) for q in range(3)]
        with nc.Block() as block:
            s_v, s_a, s_ti, s_z, s_zt, s_bt, s_bp = (sem("g_" + n) for n in "v a ti z zt bt bp".split())
            mxg, sm = gsml[:, 0:T], gsml[:, T:2 * T]

            @block.sync
            def _(sp):
                sp.wait_ge(s_z, 1)
                sp.dma_start(h_sorted[ZERO:ZERO + P, :], zrow).then_inc(s_zt, 16)
                sp.wait_ge(s_zt, 16)

            @block.gpsimd
            def _(g):
                g.memset(zrow, 0.0).then_inc(s_z, 1)
                g.wait_ge(s_z, 1)
                g.wait_ge(s_ti, 1)
                for e in range(NE):
                    g.indirect_dma_start(out=h_sorted, out_offset=bass.IndirectOffsetOnAxis(ap=tail_i[:, e:e + 1], axis=0),
                                         in_=zrow, in_offset=None).then_inc(s_bt, 16)
                g.wait_ge(s_bt, NE * 16)

            @block.scalar
            def _(a):
                a.wait_ge(s_a, 1)
                a.activation(gate, gate, ACT.Exp).then_inc(s_a, 1)

            @block.tensor
            def _(pe):
                pe.wait_ge(s_bp, 1)
                for q in range(3):
                    pe.transpose(ps[0][0:1, q * P:(q + 1) * P], bcol[4 + q], ident[:, :]).then_inc(s_bp, 1)

            @block.vector
            def _(v):
                link = Chain(v, s_v)
                link(v.tensor_scalar(tail_i, cnt, pcol, None, ALU.add))
                v.sem_inc(s_ti, 1)
                link(v.tensor_reduce(mxg, gate3, AX.X, ALU.max))
                link(v.tensor_tensor(gate3, gate3, wide(mxg, NE), ALU.subtract))
                v.sem_inc(s_a, 1)
                nb, end, st, jk = bt
                nbi = nb.bitcast(I32)
                link(v.tensor_scalar(nb, iota[:, 0:NE], -float(REG), float(P - 1), ALU.mult, ALU.add))
                link(v.tensor_tensor(nb, nb, cnt, ALU.add))
                link(v.tensor_copy(nbi, nb))
                link(v.tensor_scalar(nbi, nbi, 7, None, ALU.arith_shift_right))
                link(v.tensor_copy(jk, nbi))
                link(v.tensor_copy(nb, jk))
                link(v.tensor_tensor_scan(end, ones[:, 0:NE], nb, 0.0, ALU.mult, ALU.add))
                link(v.tensor_tensor(st, end, nb, ALU.subtract))
                eb, sb_, rw, ok, hoff, eoff, doff, _ = bcol
                link(v.tensor_scalar(jk, end, pcol, 0.0, ALU.is_le, ALU.add, accum_out=eb))
                link(v.scalar_tensor_tensor(jk, iota[:, 0:NE], eb, st, ALU.is_equal, ALU.mult, accum_out=sb_))
                link(v.tensor_tensor(rw, pcol, sb_, ALU.subtract))
                link(v.tensor_scalar(rw, rw, float(P), None, ALU.mult))
                link(v.scalar_tensor_tensor(rw, eb, float(REG), rw, ALU.mult, ALU.add))
                link(v.tensor_scalar(ok, eb, float(NE), None, ALU.is_lt))
                link(v.tensor_scalar(rw, rw, ok, None, ALU.mult))
                link(v.tensor_scalar(ok, ok, -1.0, 1.0, ALU.mult, ALU.add))
                link(v.scalar_tensor_tensor(hoff, ok, float(ZERO), rw, ALU.mult, ALU.add))
                link(v.scalar_tensor_tensor(jk, iota[:, 0:NE], -float(REG / P), st, ALU.mult, ALU.add))
                link(v.tensor_scalar(jk, jk, float(P), None, ALU.mult))
                link(v.tensor_tensor(gtmp3, gtmp3, jk.unsqueeze(1).broadcast_to([P, T, NE]), ALU.mult))
                link(v.tensor_reduce(mxg, gtmp3, AX.X, ALU.add))
                link(v.tensor_tensor(mxg, mxg, pos_f[:, :], ALU.add))
                link(v.tensor_tensor(pos_all[:, :], mxg, valid, ALU.mult))
                link(v.tensor_scalar(eb, eb, NE - 1.0, None, ALU.min))
                link(v.tensor_scalar(eoff, eb, float(HC * D), None, ALU.mult))
                link(v.tensor_scalar(doff, eb, float(D), None, ALU.mult))
                v.sem_inc(s_bp, 1)
                v.wait_ge(s_bp, 4)
                for q in range(3):
                    link(v.tensor_copy(btab[q], ps[0][0:1, q * P:(q + 1) * P]))
                v.wait_ge(s_a, 2)
                link(v.tensor_reduce(sm, gate3, AX.X, ALU.add))
                link(v.reciprocal(prob[:, :], sm))

        hoff, eoff, doff = btab
        hL = hr
        bT = [(rows[:, 2 * HID:3 * HID], work[:, 0:HID])[b] for b in range(2)]
        yb = [small[:, b * D:(b + 1) * D] for b in range(2)]
        with nc.Block() as block:
            c1, c2, ex, y = steps("e_", "c1 c2 ex y")
            t8 = Step(sem("e_t8"), 4)
            s_hl = [sem(f"e_h{b}") for b in range(4)]
            s_ys = [sem("e_y0"), sem("e_y1")]

            @block.sync
            def _(sp):
                def s_h(t, b):
                    at = sp.value_load(hoff[0:1, bass.ds(t, 1)], min_val=0, max_val=ZERO)
                    sp.wait_ge(*t8.room(t))
                    sp.dma_start(hL[b], h_sorted[bass.ds(at, P), :]).then_inc(s_hl[b], 16)

                def s_y(t, b):
                    sp.wait_ge(*y.after(t))
                    sp.dma_start(y_sorted[bass.ds(t * P, P), :], yb[b % 2]).then_inc(s_ys[b % 2], 16)
                tiles(sp, (s_h, 0), (s_y, 4), n=BLK, unroll=4)
                for b in range(2):
                    sp.wait_ge(s_ys[b], 16 * (BLK // 2))

            @block.scalar
            def _(a):
                start(a, c2)

                def a_c(t, b):
                    a.wait_ge(*t8.after(t))
                    a.wait_ge(*ex.room(t))
                    a.copy(bT[b][:, 512:1024], ps[2 * b + 1][:, :]).then_inc(c2.sem, 1)
                tiles(a, (a_c, 0), n=BLK)

            @block.tensor
            def _(pe):
                start(pe, t8, ex)
                pe.wait_ge(s_wd, (NE + 1) * 16)

                def p_t8(t, b):
                    pe.wait_ge(s_hl[b], 4 * (t - b) + 16)
                    pe.wait_ge(*c1.room(t))
                    pe.wait_ge(*c2.room(t))
                    for k in range(HC):
                        ins = pe.transpose(ps[2 * (b % 2) + k // 4][:, k % 4 * P:(k % 4 + 1) * P], hL[b][:, k * P:(k + 1) * P], ident[:, :])
                    ins.then_inc(t8.sem, 1)

                def p_ex(t, b):
                    at = pe.value_load(eoff[0:1, bass.ds(t, 1)], min_val=0, max_val=(NE - 1) * HC * D)
                    pe.wait_ge(*c1.after(t))
                    pe.wait_ge(*c2.after(t))
                    pe.wait_ge(*y.room(t))
                    for k in range(HC):
                        ins = pe.matmul(ps[4 + b % 2][:, 0:D], bT[b % 2][:, k * P:(k + 1) * P], WD[:, bass.ds(at + k * D, D)],
                                        start=k == 0, stop=k == HC - 1)
                    ins.then_inc(ex.sem, 1)
                tiles(pe, (p_t8, 0), (p_ex, 1), n=BLK, unroll=4)

            @block.vector
            def _(v):
                start(v, c1, y)

                def v_c(t, b):
                    v.wait_ge(*t8.after(t))
                    v.wait_ge(*ex.room(t))
                    v.tensor_copy(bT[b][:, 0:512], ps[2 * b][:, :]).then_inc(c1.sem, 1)

                def v_y(t, b):
                    at = v.value_load(doff[0:1, bass.ds(t, 1)], min_val=0, max_val=(NE - 1) * D)
                    v.wait_ge(*ex.after(t))
                    if not isinstance(t, int) or t >= 2:
                        v.wait_ge(s_ys[b], 8 * (t - b))
                    v.tensor_tensor(yb[b], ps[4 + b][:, 0:D], bdtab[:, bass.ds(at, D)], ALU.add).then_inc(y.sem, 1)
                tiles(v, (v_c, 0), (v_y, 1), n=BLK)

        retire_sems()

        wns = wreg[:, 0:1024].rearrange("p (c n) -> p c n", c=2)
        YG = 8
        yg = [rows[:, b * D:(b + 1) * D] for b in range(YG)]
        x3 = [rows[:, YG * D + b * (D + 1):YG * D + (b + 1) * (D + 1)] for b in range(4)]
        xT3 = [small[:, b * D:(b + 1) * D] for b in range(2)]
        with nc.Block() as block:
            tp, xt, mm, tb, r, rb = steps("h_", "tp xt mm tb r rb")
            row, gr, wr = (Step(sem("h_" + n), 4) for n in "row gr wr".split())
            pc, ya = Step(sem("h_pc"), YG), Step(sem("h_ya"), YG)
            s_yg = [sem(f"h_yg{b}") for b in range(YG)]
            s_w, s_sl, s_n, s_nf, s_one, s_tab, s_bs = (sem("h_" + n) for n in "w sl n nf one tab bs".split())

            @block.sync
            def _(sp):
                sp.dma_start(wns[:, :, 0:D], A["L1_gnn_W_neigh"].rearrange("(c p) n -> p c n", p=P)).then_inc(s_w, 16)
                sp.dma_start(wns[:, :, D:2 * D], A["L1_gnn_W_self"].rearrange("(c p) n -> p c n", p=P)).then_inc(s_w, 16)
                load_bias(sp, b_row, A["L1_gnn_b"], s_w)
                load_bias(sp, b_row2, A["L1_mix_b_fc2"], s_w)
                to_table(sp, 2, tb, s_tab)

            @block.gpsimd
            def _(g):
                start(g, rb, wr)

                def g_y(t, b):
                    g.wait_ge(*pc.after(t))
                    g.sem_inc(s_go, 1)
                    g.indirect_dma_start(out=yg[b], out_offset=None, in_=y_sorted,
                                         in_offset=bass.IndirectOffsetOnAxis(ap=idx_stage[:, b:b + 1], axis=0)).then_inc(s_yg[b], 16)
                tiles(g, (g_y, 0), unroll=YG)
                for b in range(4):
                    g.memset(x3[b][:, D:D + 1], 1.0).then_inc(s_one, 1)
                g.wait_ge(s_w, 4 * 16)
                g.tensor_tensor(b_row, b_row, b_row2, ALU.add).then_inc(s_bs, 1)
                g.wait_ge(s_bs, 1)

                def g_rb(t, b):
                    g.wait_ge(*r.after(t))
                    g.tensor_tensor(R[:, col(t)], R[:, col(t)], b_row, ALU.add).then_inc(rb.sem, 1)

                def g_wr(t, b):
                    g.tensor_copy(XN[:, col(t)], x3[b][:, 0:D]).then_inc(wr.sem, 1)
                tiles(g, (g_rb, 0), (g_wr, 0), unroll=4)

            @block.scalar
            def _(a):
                start(a, row, pc)

                def a_pc(t, b):
                    a.wait_ge(*ya.room(t))
                    a.copy(idx_stage[:, b:b + 1], pos_all[:, bass.ds(t, 1)]).then_inc(pc.sem, 1)
                tiles(a, (a_pc, 0), unroll=YG)
                a.wait_ge(s_nf, 1)

                def a_row(t, b):
                    a.wait_ge(*gr.room(t))
                    a.wait_ge(*tp.room(t))
                    a.wait_ge(*wr.room(t))
                    a.activation(x3[b][:, 0:D], XN[:, col(t)], ACT.Identity, bias=nmr[:, bass.ds(t, 1)],
                                 scale=rstd[:, bass.ds(t, 1)]).then_inc(row.sem, 1)
                tiles(a, (a_row, 0), unroll=4)

            @block.tensor
            def _(pe):
                start(pe, tp, mm, gr)
                pe.wait_ge(s_w, 4 * 16)
                pe.wait_ge(s_one, 4)

                def p_tp(t, b):
                    pe.wait_ge(*row.after(t))
                    pe.wait_ge(*xt.room(t))
                    pe.transpose(ps[b % 2][:, 0:P], x3[b][:, 0:P], ident[:, :])
                    pe.transpose(ps[b % 2][:, P:D], x3[b][:, P:D], ident[:, :]).then_inc(tp.sem, 1)

                def p_mm(t, b):
                    first, last = (isinstance(t, int) and t == q for q in (0, T - 1))
                    n = LAST if last else P
                    for c in range(2):
                        ins = pe.matmul(ps[5 + c][:, 0:D + 1], x3[b][0:n, c * P:(c + 1) * P], x3[b][0:n, :], start=first, stop=last,
                                        skip_group_check=True)
                    ins.then_inc(gr.sem, 1)
                    pe.wait_ge(*xt.after(t))
                    pe.wait_ge(*tb.room(t))
                    pe.wait_ge(*r.room(t))
                    pe.matmul(ps[2 + b % 2][:, :], xT3[b % 2][:, 0:P], wns[:, 0, :], start=True, stop=False)
                    pe.matmul(ps[2 + b % 2][:, :], xT3[b % 2][:, P:D], wns[:, 1, :], start=False, stop=True).then_inc(mm.sem, 1)
                tiles(pe, (p_tp, 0), (p_mm, 1), unroll=4)

            @block.vector
            def _(v):
                start(v, xt, r, tb, ya)

                def v_ya(t, b):
                    v.wait_ge(s_yg[b], 16 // YG * (t - b) + 16)
                    v.scalar_tensor_tensor(XN[:, col(t)], yg[b], prob[:, bass.ds(t, 1)], XN[:, col(t)], ALU.mult, ALU.add).then_inc(ya.sem, 1)
                def v_st(t, b):
                    v.wait_ge(*ya.after(t))
                    st(t, b)
                st = stats_of(v, XN, s_sl)
                tiles(v, (v_ya, 0), (v_st, 1), unroll=YG)
                v.wait_ge(s_sl, T)
                norm_factors(v, Chain(v, s_n))
                v.sem_inc(s_nf, 1)

                def v_xt(t, b):
                    v.wait_ge(*tp.after(t))
                    v.wait_ge(*mm.room(t))
                    v.tensor_copy(xT3[b], ps[b][:, 0:D]).then_inc(xt.sem, 1)

                def v_r(t, b):
                    v.wait_ge(*mm.after(t))
                    v.tensor_tensor(R[:, col(t)], XN[:, col(t)], ps[2 + b][:, D:2 * D], ALU.add).then_inc(r.sem, 1)

                def v_tb(t, b):
                    v.tensor_copy(ACC[:, col(t)], ps[2 + b][:, 0:D]).then_inc(tb.sem, 1)
                tiles(v, (v_xt, 0), (v_r, 1), (v_tb, 1))

        wqkv = rows[:, 0:1536].rearrange("p (c n) -> p c n", c=2)
        gram = rows[:, 1536:2048].rearrange("p (c n) -> p c n", c=2)
        t1 = rows[:, 2048:2560].rearrange("p (c n) -> p c n", c=2)
        wq1T = rows[:, 2560:3072].rearrange("p (c n) -> p c n", c=2)
        abd = rows[:, 3072:3328].rearrange("p (c n) -> p c n", c=2)
        abT = rows[:, 3328:3584].rearrange("p (c n) -> p c n", c=2)
        bqc = rows[:, 3584:3586]
        bqm = rows[:, 3600:3728]
        csum, nmx = rows[:, 3586:3588], rows[:, 3588:3590]
        rsm = rows[:, 3590:3592]
        nval = rows[0:1, 3592:3593]
        att = rows[:, 3728:3856].rearrange("p (c n) -> p c n", c=2)
        bqkv = work[0:1, 0:768]
        crow = work[0:1, 768:1024]
        t2row = work[0:1, 1024:1280]
        g1 = wreg[:, 0:512].rearrange("p (c n) -> p c n", c=2)
        c1row = bias_rows[:, D:2 * D]
        fc1 = wreg[:, 512:2048].rearrange("p (c n) -> p c n", c=2)
        fc2 = wreg[:, 2048:3584].rearrange("p (k n) -> p k n", n=D)
        lng, lnb, fb1 = wreg[:, 3584:3586], wreg[:, 3586:3588], wreg[:, 3588:3594]
        with nc.Block() as block:
            s_w, s_v, s_p, s_a, s_z3 = (sem("i_" + n) for n in "w v p a z".split())

            @block.sync
            def _(sp):
                sp.dma_start(wqkv, A["L1_mix_w_qkv"].rearrange("(c p) n -> p c n", p=P)).then_inc(s_w, 16)
                sp.dma_start(bqkv, A["L1_mix_b_qkv"].rearrange("(a n) -> a n", a=1)).then_inc(s_w, 16)
                sp.dma_start(bqc, A["L1_mix_b_qkv"][0:D].rearrange("(c p) -> p c", p=P), allow_slow_non_contiguous=True).then_inc(s_w, 16)
                sp.dma_start(fc1, A["L1_mix_w_fc1"].rearrange("(c p) n -> p c n", p=P)).then_inc(s_w, 16)
                sp.dma_start(fc2, A["L1_mix_w_fc2"].rearrange("(k p) n -> p k n", p=P)).then_inc(s_w, 16)
                sp.dma_start(lng, A["L1_mix_norm_g"].rearrange("(c p) -> p c", p=P), allow_slow_non_contiguous=True).then_inc(s_w, 16)
                sp.dma_start(lnb, A["L1_mix_norm_b"].rearrange("(c p) -> p c", p=P), allow_slow_non_contiguous=True).then_inc(s_w, 16)
                sp.dma_start(fb1, A["L1_mix_b_fc1"].rearrange("(k p) -> p k", p=P), allow_slow_non_contiguous=True).then_inc(s_w, 16)
                sp.wait_ge(s_w, 8 * 16)

            @block.gpsimd
            def _(g):
                g.memset(ACC, 0.0).then_inc(s_z3, 1)
                g.memset(rows[:, 3072:3328], 0.0).then_inc(s_z3, 1)
                g.memset(nval, float(N)).then_inc(s_z3, 1)

            @block.scalar
            def _(a):
                a.wait_ge(s_v, 13)
                for c in range(2):
                    a.activation(att[:, c, :], att[:, c, :], ACT.Exp, bias=nmx[:, c:c + 1], scale=64.0 ** -0.5).then_inc(s_a, 1)

            @block.tensor
            def _(pe):
                pe.wait_ge(s_w, 8 * 16)
                pe.wait_ge(s_z3, 3)
                pe.wait_ge(s_v, 4)
                for c in range(2):
                    pe.matmul(ps[0][0:1, c * P:(c + 1) * P], csum[:, c:c + 1], ident[:, :], start=True, stop=True).then_inc(s_p, 1)
                pe.wait_ge(s_v, 5)
                for m in range(2):
                    for c in range(2):
                        pe.matmul(ps[1][:, m * D:(m + 1) * D], gram[:, c, m * P:(m + 1) * P], wqkv[:, c, 2 * D:3 * D], start=c == 0, stop=False)
                    pe.matmul(ps[1][:, m * D:(m + 1) * D], crow[:, m * P:(m + 1) * P], bqkv[:, 2 * D:3 * D], start=False, stop=True).then_inc(s_p, 1)
                for c in range(2):
                    pe.matmul(ps[2][0:1, 0:D], csum[:, c:c + 1], wqkv[:, c, 2 * D:3 * D], start=c == 0, stop=False)
                pe.matmul(ps[2][0:1, 0:D], nval, bqkv[:, 2 * D:3 * D], start=False, stop=True).then_inc(s_p, 1)
                pe.wait_ge(s_v, 7)
                for m in range(2):
                    for c in range(2):
                        pe.matmul(ps[3][:, m * D:(m + 1) * D], wqkv[:, c, D + m * P:D + (m + 1) * P], t1[:, c, :], start=c == 0, stop=False)
                    pe.matmul(ps[3][:, m * D:(m + 1) * D], bqkv[:, D + m * P:D + (m + 1) * P], t2row, start=False, stop=True).then_inc(s_p, 1)
                for m in range(2):
                    for c in range(2):
                        ins = pe.transpose(ps[4][:, m * D + c * P:m * D + (c + 1) * P], wqkv[:, c, m * P:(m + 1) * P], ident[:, :])
                ins.then_inc(s_p, 1)
                pe.wait_ge(s_v, 21)
                for m in range(2):
                    pe.transpose(ps[5][:, m * P:(m + 1) * P], abd[:, m, :], ident[:, :]).then_inc(s_p, 1)
                pe.wait_ge(s_v, 22)
                for rr in range(2):
                    for m in range(2):
                        pe.matmul(ps[6][:, rr * D + m * P:rr * D + (m + 1) * P], wq1T[:, m, rr * P:(rr + 1) * P], abT[:, m, :],
                                  start=True, stop=True).then_inc(s_p, 1)
                for m in range(2):
                    pe.wait_ge(s_v, 23 + 2 * m)
                    pe.matmul(ps[2][:, m * P:(m + 1) * P], bqm, abT[:, m, :], start=True, stop=True).then_inc(s_p, 1)

            @block.vector
            def _(v):
                link = Chain(v, s_v)
                for c in range(2):
                    link(v.tensor_copy(gram[:, c, :], ps[5 + c][:, 0:D]))
                    link(v.tensor_copy(csum[:, c:c + 1], ps[5 + c][:, D:D + 1]))
                v.wait_ge(s_p, 2)
                link(v.tensor_copy(crow, ps[0][0:1, 0:D]))
                v.wait_ge(s_p, 5)
                link(v.tensor_copy(rows[:, 2048:2560], ps[1][:, :]))
                link(v.tensor_copy(t2row, ps[2][0:1, 0:D]))
                v.wait_ge(s_p, 7)
                for m in range(2):
                    link(v.tensor_copy(att[0:64, m, :], ps[3][0:64, m * D + 2 * m * 64:m * D + (2 * m + 1) * 64]))
                    link(v.tensor_copy(att[64:128, m, :], ps[3][64:128, m * D + (2 * m + 1) * 64:m * D + (2 * m + 2) * 64]))
                link(v.tensor_reduce(nmx, att, AX.X, ALU.max, negate=True))
                link(v.tensor_scalar(nmx, nmx, 64.0 ** -0.5, None, ALU.mult))
                v.wait_ge(s_p, 8)
                link(v.tensor_copy(rows[:, 2560:3072], ps[4][:, :]))
                v.wait_ge(s_a, 2)
                link(v.tensor_reduce(rsm, att, AX.X, ALU.add))
                link(v.reciprocal(rsm, rsm))
                v.wait_ge(s_z3, 3)
                link(v.tensor_scalar(bqm, bqc[:, 0:1].broadcast_to([P, P]), 1.0, None, ALU.mult))
                for m in range(2):
                    for q in range(2):
                        rr = slice(64 * q, 64 * q + 64)
                        link(v.tensor_scalar(abd[rr, m, rr], att[rr, m, :], rsm[rr, m:m + 1], None, ALU.mult))
                v.wait_ge(s_p, 10)
                link(v.tensor_copy(rows[:, 3328:3584], ps[5][:, 0:D]))
                v.wait_ge(s_p, 14)
                link(v.tensor_copy(wreg[:, 0:512], ps[6][:, :]))
                v.wait_ge(s_p, 15)
                link(v.tensor_scalar(bqm, bqc[:, 1:2].broadcast_to([P, P]), 1.0, None, ALU.mult))
                link(v.tensor_copy(c1row[:, 0:P], ps[2][:, 0:P]))
                v.wait_ge(s_p, 16)
                link(v.tensor_copy(c1row[:, P:D], ps[2][:, P:D]))

        m_row, m_xT, m_y, m_h, m_hT = (work[:, q * D:(q + 1) * D] for q in range(5))
        m_u = work[:, 5 * D:8 * D]
        m_w = gsml[:, 0:8]
        m_steps = [Step(sem("j_" + n), 1) for n in "row xc tp xt gm y ln tn hx f1 gl f2 o ry".split()]
        row, xc, tp, xt, gm, y, ln, tn, hx, f1, gl, f2, o, ry = m_steps
        s_jc = sem("j_chain")

        def f1_out(k):
            return ps[6][:, k * P:(k + 1) * P] if k < 4 else ps[5][:, (k - 4) * P:(k - 3) * P]

        def side_scalar(a):
            start(a, row, xt, hx, gl)
            a.activation(gsml[:, 16:17], ident[:, 0:1], ACT.Gelu)

            def side(u, work):
                t0, t1, t2, t3 = work
                if u == 0 and t0 is not None:
                    a.wait_ge(*tp.room(t0))
                    a.copy(m_row, XN[:, col(t0)]).then_inc(row.sem, 1)
                if u == 4 and t2 is not None:
                    a.wait_ge(*tn.after(t2))
                    a.wait_ge(*f1.room(t2))
                    for c in range(2):
                        ins = a.activation(m_hT[:, c * P:(c + 1) * P], ps[7][:, c * P:(c + 1) * P], ACT.Identity,
                                           bias=lnb[:, c:c + 1], scale=lng[:, c:c + 1])
                    ins.then_inc(hx.sem, 1)
                if u == 4 and t3 is not None:
                    a.wait_ge(*f1.after(t3))
                    a.wait_ge(*f2.room(t3))
                    for k in range(6):
                        ins = a.activation(m_u[:, k * P:(k + 1) * P], f1_out(k), ACT.Gelu, bias=fb1[:, k:k + 1])
                    ins.then_inc(gl.sem, 1)
                if u == 8 and t0 is not None:
                    a.wait_ge(*tp.after(t0))
                    a.wait_ge(*gm.room(t0))
                    a.copy(m_xT, ps[4][:, 0:D]).then_inc(xt.sem, 1)
            return side

        def side_tensor(pe):
            start(pe, tp, gm, tn, f1, f2)

            def side(u, work):
                t0, t1, t2, t3 = work
                def first_product(k):
                    for c in range(2):
                        ins = pe.matmul(f1_out(k), fc1[:, c, k * P:(k + 1) * P], m_hT[:, c * P:(c + 1) * P], start=c == 0, stop=c == 1)
                    return ins

                if u in (0, 2) and t3 is not None:
                    ins = first_product(4 + u // 2)
                    if u == 2:
                        ins.then_inc(f1.sem, 1)
                if u == 1 and t2 is not None:
                    pe.wait_ge(*ln.after(t2))
                    if t3 is not None:
                        pe.wait_ge(*o.room(t3))
                    pe.transpose(ps[7][:, 0:P], m_h[:, 0:P], ident[:, :])
                    pe.transpose(ps[7][:, P:D], m_h[:, P:D], ident[:, :]).then_inc(tn.sem, 1)
                if u == 5 and t0 is not None:
                    pe.wait_ge(*row.after(t0))
                    pe.wait_ge(*y.room(t0))
                    pe.transpose(ps[4][:, 0:P], m_row[:, 0:P], ident[:, :])
                    pe.transpose(ps[4][:, P:D], m_row[:, P:D], ident[:, :]).then_inc(tp.sem, 1)
                if u in (10, 11, 13, 15) and t2 is not None:
                    if u == 10:
                        pe.wait_ge(*hx.after(t2))
                        if t3 is not None:
                            pe.wait_ge(*gl.after(t3))
                    first_product((10, 11, 13, 15).index(u))
                if u == 13 and t0 is not None:
                    pe.wait_ge(*xt.after(t0))
                    for c in range(2):
                        ins = pe.matmul(ps[4][:, 0:D], m_xT[:, c * P:(c + 1) * P], g1[:, c, :], start=c == 0, stop=c == 1)
                    ins.then_inc(gm.sem, 1)
                if 10 <= u < 15 and t3 is not None:
                    if u == 10:
                        pe.wait_ge(*gl.after(t3))
                        if t2 is not None:
                            pe.wait_ge(*hx.after(t2))
                    for k in ((0,), (1,), (2,), (3,), (4, 5))[u - 10]:
                        ins = pe.matmul(ps[7][:, 0:D], m_u[:, k * P:(k + 1) * P], fc2[:, k, :], start=k == 0, stop=k == 5)
                    if u == 14:
                        ins.then_inc(f2.sem, 1)
            return side

        def side_vector(v):
            start(v, xc, y, ry, ln, o)
            mean, dev, x, w, z = (m_w[:, q:q + 1] for q in range(5))
            wi, xi = w.bitcast(I32), x.bitcast(I32)

            def newton_step(s):
                return [lambda: v.scalar_tensor_tensor(z, w, x, w, ALU.mult, ALU.mult),
                        lambda: v.scalar_tensor_tensor(w, z, -3.0 * s * s, w, ALU.add, ALU.mult)]

            norm = [
                lambda: v.bn_stats(stats[:, :], m_y),
                lambda: v.tensor_scalar(mean, stats[:, 1:2], stats[:, 4:5], 0.5, ALU.add, ALU.mult),
                lambda: v.tensor_scalar(dev, stats[:, 1:2], stats[:, 4:5], (D / 4) ** 0.5, ALU.subtract, ALU.mult),
                lambda: v.tensor_scalar(x, stats[:, 2:3], stats[:, 5:6], D * EPS, ALU.add, ALU.add),
                lambda: v.scalar_tensor_tensor(x, dev, dev, x, ALU.mult, ALU.add),
                lambda: v.tensor_scalar(wi, xi, 1, None, ALU.logical_shift_right),
                lambda: v.tensor_scalar(wi, wi, -1.0, MAGIC, ALU.mult, ALU.add),
                *newton_step(1.0), *newton_step(-2.0), *newton_step(16.0),
                lambda: v.tensor_scalar(w, w, D ** 0.5 / -8192.0, None, ALU.mult),
            ]

            def side(u, work):
                t0, t1, t2, t3 = work
                if u == 9 and t0 is not None:
                    v.wait_ge(*row.after(t0))
                    v.tensor_tensor(XN[:, col(t0)], XN[:, col(t0)], c1row, ALU.add).then_inc(xc.sem, 1)
                if u == 3 and t1 is not None:
                    v.tensor_tensor(R[:, col(t1)], R[:, col(t1)], m_y, ALU.add).then_inc(ry.sem, 1)
                if t1 is not None and u < 14:
                    if u == 0:
                        v.wait_ge(*y.after(t1))
                    else:
                        v.wait_ge(s_jc, t1 * len(norm) + u)
                    norm[u]().then_inc(s_jc, 1)
                if t1 is not None and u == 14:
                    v.wait_ge(s_jc, (t1 + 1) * len(norm))
                    v.wait_ge(*tn.room(t1))
                    v.tensor_scalar(m_h, m_y, mean, w, ALU.subtract, ALU.mult).then_inc(ln.sem, 1)
                if u == RING and t3 is not None:
                    v.wait_ge(*f2.after(t3))
                    v.wait_ge(*ry.after(t3))
                    v.tensor_tensor(R[:, col(t3)], R[:, col(t3)], ps[7][:, 0:D], ALU.add).then_inc(o.sem, 1)
                if u == RING and t0 is not None:
                    v.wait_ge(*gm.after(t0))
                    v.wait_ge(*xc.after(t0))
                    v.wait_ge(*ry.room(t0))
                    v.tensor_tensor(m_y, XN[:, col(t0)], ps[4][:, 0:D], ALU.add).then_inc(y.sem, 1)
            return side

        aggregate(2, table[2], side=dict(scalar=side_scalar, tensor=side_tensor, vector=side_vector))

        gw = wreg[:, 0:8].rearrange("p (c n) -> p c n", c=2)
        gbr = wreg[:, 8:12]
        with nc.Block() as block:
            s_r, s_sl, s_n, s_w9 = sem("k_r"), sem("k_sl"), sem("k_n"), sem("k_w")

            @block.sync
            def _(sp):
                sp.dma_start(gw, A["L1_ffn_gW"].rearrange("(c p) n -> p c n", p=P)).then_inc(s_w9, 16)
                load_bias(sp, gbr, A["L1_ffn_gb"], s_w9)
                sp.wait_ge(s_w9, 32)

            @block.vector
            def _(v):
                def v_r(t, b):
                    v.scalar_tensor_tensor(R[:, col(t)], ACC[:, col(t)], invdeg[:, bass.ds(t, 1)], R[:, col(t)], ALU.mult,
                                           ALU.add).then_inc(s_r, 1)

                def v_st(t, b):
                    v.wait_ge(s_r, t + 1)
                    st(t, b)
                st = stats_of(v, R, s_sl)
                tiles(v, (v_r, 0), (v_st, 1))
                v.wait_ge(s_sl, T)
                norm_factors(v, Chain(v, s_n))

        NG = 4
        lgt = gate[:, 0:T * NG].rearrange("p (t e) -> p t e", e=NG)
        with nc.Block() as block:
            row, tp, xt, gt, gc, wr = steps("l_", "row tp xt gt gc wr")

            @block.gpsimd
            def _(g):
                start(g, wr)

                def g_wr(t, b):
                    g.wait_ge(*xt.after(t))
                    g.tensor_copy(XN[:, col(t)], xT[b]).then_inc(wr.sem, 1)
                tiles(g, (g_wr, 0))

            @block.scalar
            def _(a):
                start(a, row)

                def a_row(t, b):
                    a.wait_ge(*tp.room(t))
                    a.activation(xrow[b], R[:, col(t)], ACT.Identity, bias=nmr[:, bass.ds(t, 1)],
                                 scale=rstd[:, bass.ds(t, 1)]).then_inc(row.sem, 1)
                tiles(a, (a_row, 0))

            @block.tensor
            def _(pe):
                start(pe, tp, gt)

                def p_tp(t, b):
                    pe.wait_ge(*row.after(t))
                    pe.wait_ge(*xt.room(t))
                    pe.transpose(ps[b][:, 0:P], xrow[b][:, 0:P], ident[:, :])
                    pe.transpose(ps[b][:, P:D], xrow[b][:, P:D], ident[:, :]).then_inc(tp.sem, 1)

                def p_gt(t, b):
                    pe.wait_ge(*xt.after(t))
                    pe.wait_ge(*gc.room(t))
                    for c in range(2):
                        ins = pe.matmul(ps[2 + b][:, 0:NG], xT[b][:, c * P:(c + 1) * P], gw[:, c, :], start=c == 0, stop=c == 1)
                    ins.then_inc(gt.sem, 1)
                tiles(pe, (p_tp, 0), (p_gt, 1))

            @block.vector
            def _(v):
                start(v, xt, gc)

                def v_xt(t, b):
                    v.wait_ge(*tp.after(t))
                    v.wait_ge(*gt.room(t))
                    v.wait_ge(*wr.room(t))
                    v.tensor_copy(xT[b], ps[b][:, 0:D]).then_inc(xt.sem, 1)

                def v_gc(t, b):
                    v.wait_ge(*gt.after(t))
                    v.tensor_tensor(gate[:, bass.ds(t * NG, NG)], ps[2 + b][:, 0:NG], gbr, ALU.add).then_inc(gc.sem, 1)
                tiles(v, (v_xt, 0), (v_gc, 1))

        sw1 = wreg[:, 0:512].rearrange("p (c n) -> p c n", c=2)
        sw2 = wreg[:, 512:768].rearrange("p (c n) -> p c n", c=2)
        sw3 = wreg[:, 768:1024]
        ew1 = wreg[:, 1024:2048].rearrange("p (e c n) -> p e c n", e=NG, c=2)
        ew2 = wreg[:, 2048:2560].rearrange("p (e n) -> p e n", n=P)
        ew3 = wreg[:, 2560:3072].rearrange("p (q n) -> p q n", n=D)
        sb1c, eb1c, sb2c, eb2c = wreg[:, 3072:3074], wreg[:, 3074:3078], wreg[:, 3078:3079], wreg[:, 3079:3081]
        bend = wreg[0:NG + 1, 3328:3584]
        with nc.Block() as block:
            s_v, s_a, s_w, s_z5 = sem("m_v"), sem("m_a"), sem("m_w"), sem("m_z")
            mxg, sm, rk, t_a, t_b = gsml[:, 0:T], gsml[:, T:2 * T], newton[:, 0:T], gtmp[:, 200:200 + T], gtmp[:, 250:250 + T]
            rank = gtmp[:, 0:T * NG].rearrange("p (t e) -> p t e", e=NG)

            @block.gpsimd
            def _(g):
                g.memset(wreg[:, 2048:2560], 0.0).then_inc(s_z5, 1)

            @block.sync
            def _(sp):
                def ld(dst, src, slow=False):
                    sp.dma_start(dst, src, allow_slow_non_contiguous=slow).then_inc(s_w, 16)
                ld(sw1, A["L1_ffn_sW1"].rearrange("(c p) n -> p c n", p=P))
                ld(sw2, A["L1_ffn_sW2"].rearrange("(c p) n -> p c n", p=P))
                ld(sw3, A["L1_ffn_sW3"])
                for e in range(NG):
                    ld(ew1[:, e, :, :], A["L1_ffn_eW1"][e].rearrange("(c p) n -> p c n", p=P))
                    ld(ew3[64 * (e % 2):64 * (e % 2) + 64, e // 2, :], A["L1_ffn_eW3"][e])
                    ld(eb2c[64 * (e % 2):64 * (e % 2) + 64, e // 2:e // 2 + 1], A["L1_ffn_eb2"][e].rearrange("(p a) -> p a", a=1), slow=True)
                sp.wait_ge(s_z5, 1)
                for e in range(NG):
                    ld(ew2[:, e, 64 * (e % 2):64 * (e % 2) + 64], A["L1_ffn_eW2"][e])
                ld(sb1c, A["L1_ffn_sb1"].rearrange("(c p) -> p c", p=P), slow=True)
                ld(eb1c, A["L1_ffn_eb1"].rearrange("e p -> p e"), slow=True)
                ld(sb2c, A["L1_ffn_sb2"].rearrange("(p a) -> p a", a=1), slow=True)
                ld(bend[0:NG], A["L1_ffn_eb3"])
                ld(bend[NG:NG + 1], A["L1_ffn_sb3"].rearrange("(a n) -> a n", a=1))
                sp.wait_ge(s_w, (3 + 3 * NG + NG + 5) * 16)

            @block.scalar
            def _(a):
                a.wait_ge(s_v, 2)
                a.activation(lgt, lgt, ACT.Exp).then_inc(s_a, 1)
                a.wait_ge(s_v, 42)
                a.activation(rank, rank, ACT.Exp).then_inc(s_a, 1)

            @block.vector
            def _(v):
                link = Chain(v, s_v)
                link(v.tensor_reduce(mxg, lgt, AX.X, ALU.max))
                link(v.tensor_tensor(lgt, lgt, wide(mxg, NG), ALU.subtract))
                v.wait_ge(s_a, 1)
                link(v.tensor_reduce(sm, lgt, AX.X, ALU.add))
                link(v.reciprocal(sm, sm))
                link(v.tensor_tensor(lgt, lgt, wide(sm, NG), ALU.mult))
                for e in range(NG):
                    first = True
                    for j in range(NG):
                        if j == e:
                            continue
                        dst = rank[:, :, e] if first else t_a
                        link(v.tensor_tensor(dst, lgt[:, :, j], lgt[:, :, e], ALU.is_ge if j < e else ALU.is_gt))
                        if not first:
                            link(v.tensor_tensor(rank[:, :, e], rank[:, :, e], t_a, ALU.add))
                        first = False
                link(v.tensor_reduce(mxg, lgt, AX.X, ALU.max))
                for e in range(NG):
                    link(v.tensor_scalar(rank[:, :, e], rank[:, :, e], 2.0, None, ALU.is_lt))
                    link(v.tensor_tensor(lgt[:, :, e], lgt[:, :, e], mxg, ALU.subtract))
                for e in range(NG):
                    link(v.tensor_copy(gate[:, 200 + e * T:200 + (e + 1) * T] if e < 3 else newton[:, T:2 * T], rank[:, :, e]))
                for e in range(NG):
                    link(v.tensor_copy(rank[:, :, e], lgt[:, :, e]))
                v.wait_ge(s_a, 2)
                for e in range(NG):
                    sel = gate[:, 200 + e * T:200 + (e + 1) * T] if e < 3 else newton[:, T:2 * T]
                    link(v.tensor_tensor(rank[:, :, e], rank[:, :, e], sel, ALU.mult))
                link(v.tensor_reduce(sm, rank, AX.X, ALU.add))
                link(v.reciprocal(sm, sm))
                link(v.tensor_tensor(lgt, rank, wide(sm, NG), ALU.mult))

        wst = [small[:, 8 * b:8 * b + NG + 1] for b in range(2)]
        wT = [small[0:NG + 1, 64 + b * P:64 + (b + 1) * P] for b in range(2)]
        a1 = [rows[:, b * 768:(b + 1) * 768] for b in range(2)]
        a2 = [rows[:, 1536 + b * 384:1536 + (b + 1) * 384] for b in range(2)]
        with nc.Block() as block:
            l1, r1, l2, r2, l3, wc, wt, wtc, ad = steps("n_", "l1 r1 l2 r2 l3 wc wt wtc ad")
            s_o, s_c, s_one = sem("n_out"), sem("n_chain"), sem("n_one")

            @block.sync
            def _(sp):
                with sp.Fori(0, T - 1) as i:
                    sp.wait_ge(*ad.after(i))
                    sp.dma_start(out[bass.ds(i * P, P), :], R[:, bass.ds(i * D, D)]).then_inc(s_o, 16)
                sp.wait_ge(*ad.after(T - 1))
                sp.dma_start(out[(T - 1) * P:N, :], R[0:LAST, (T - 1) * D:T * D]).then_inc(s_o, 16)
                sp.wait_ge(s_o, T * 16)

            @block.scalar
            def _(a):
                start(a, r1, r2)

                def a_r1(t, b):
                    a.wait_ge(*l1.after(t))
                    a.wait_ge(*l2.room(t))
                    for k in range(6):
                        bias = sb1c[:, k:k + 1] if k < 2 else eb1c[:, k - 2:k - 1]
                        ins = a.activation(a1[b][:, k * P:(k + 1) * P], ps[k // 4][:, k % 4 * P:(k % 4 + 1) * P], ACT.Relu, bias=bias)
                    ins.then_inc(r1.sem, 1)

                def a_r2(t, b):
                    a.wait_ge(*l2.after(t))
                    a.wait_ge(*l3.room(t))
                    for k in range(3):
                        bias = sb2c if k < 1 else eb2c[:, k - 1:k]
                        ins = a.activation(a2[b][:, k * P:(k + 1) * P], ps[2][:, k * P:(k + 1) * P], ACT.Relu, bias=bias)
                    ins.then_inc(r2.sem, 1)
                tiles(a, (a_r1, 0), (a_r2, 1))

            @block.tensor
            def _(pe):
                start(pe, l1, l2, l3, wt)

                def p_l1(t, b):
                    pe.wait_ge(*r1.after(t - 1))
                    for k in range(6):
                        for c in range(2):
                            w = sw1[:, c, k * P:(k + 1) * P] if k < 2 else ew1[:, k - 2, c, :]
                            ins = pe.matmul(ps[k // 4][:, k % 4 * P:(k % 4 + 1) * P], w, XN[:, bass.ds(t * D + c * P, P)],
                                            start=c == 0, stop=c == 1)
                    ins.then_inc(l1.sem, 1)

                def p_l2(t, b):
                    pe.wait_ge(*r1.after(t))
                    pe.wait_ge(*r2.after(t - 1))
                    for c in range(2):
                        pe.matmul(ps[2][:, 0:P], sw2[:, c, :], a1[b][:, c * P:(c + 1) * P], start=c == 0, stop=c == 1)
                    for e in range(NG):
                        ins = pe.matmul(ps[2][:, (1 + e // 2) * P:(2 + e // 2) * P], ew2[:, e, :], a1[b][:, (2 + e) * P:(3 + e) * P],
                                        start=e % 2 == 0, stop=e % 2 == 1)
                    ins.then_inc(l2.sem, 1)
                    pe.wait_ge(*wc.after(t))
                    pe.wait_ge(*wtc.room(t))
                    pe.transpose(ps[6 + b][0:NG + 1, 0:P], wst[b], ident[:, :]).then_inc(wt.sem, 1)

                def p_l3(t, b):
                    pe.wait_ge(*r2.after(t))
                    pe.wait_ge(*ad.after(t - 1))
                    for e in range(NG):
                        q = slice(64 * (e % 2), 64 * (e % 2) + 64)
                        pe.matmul(ps[3 + e % 2][:, e // 2 * D:(e // 2 + 1) * D], a2[b][q, (1 + e // 2) * P:(2 + e // 2) * P], ew3[q, e // 2, :],
                                  start=True, stop=True)
                    pe.matmul(ps[5][:, 0:D], a2[b][:, 0:P], sw3, start=True, stop=False)
                    pe.wait_ge(*wtc.after(t))
                    pe.matmul(ps[5][:, 0:D], wT[b], bend, start=False, stop=True).then_inc(l3.sem, 1)
                tiles(pe, (p_l1, 0), (p_l2, 1), (p_l3, 2))

            @block.vector
            def _(v):
                start(v, wc, wtc, ad)
                chain = Chain(v, s_c, NG)
                for b in range(2):
                    v.memset(wst[b][:, NG:NG + 1], 1.0).then_inc(s_one, 1)

                def v_w(t, b):
                    v.wait_ge(*wt.room(t))
                    v.tensor_copy(wst[b][:, 0:NG], gate[:, bass.ds(t * NG, NG)]).then_inc(wc.sem, 1)

                def v_wt(t, b):
                    v.wait_ge(*wt.after(t))
                    v.wait_ge(*l3.room(t))
                    v.tensor_copy(wT[b], ps[6 + b][0:NG + 1, 0:P]).then_inc(wtc.sem, 1)

                def v_ad(t, b):
                    v.wait_ge(*l3.after(t))
                    chain.tile(t)
                    x = R[:, col(t)]
                    chain(v.tensor_tensor(x, x, ps[5][:, 0:D], ALU.add))
                    for e in range(NG):
                        ins = v.scalar_tensor_tensor(x, ps[3 + e % 2][:, e // 2 * D:(e // 2 + 1) * D], gate[:, bass.ds(t * NG + e, 1)], x,
                                                     ALU.mult, ALU.add)
                        if e < NG - 1:
                            chain(ins)
                        else:
                            ins.then_inc(ad.sem, 1)
                tiles(v, (v_w, 0), (v_wt, 1), (v_ad, 2))


_INPUTS = ["x", "src", "dst", "L0_gnn_W1", "L0_gnn_b1", "L0_gnn_W2", "L0_gnn_b2", "L0_mix_W_qkv", "L0_mix_W_out", "L0_mix_b_out",
           "L0_ffn_W1", "L0_ffn_b1", "L0_ffn_Wg", "L0_ffn_bg", "L0_ffn_Wd", "L0_ffn_bd", "L1_gnn_W_self", "L1_gnn_W_neigh", "L1_gnn_b",
           "L1_mix_w_qkv", "L1_mix_b_qkv", "L1_mix_norm_g", "L1_mix_norm_b", "L1_mix_w_fc1", "L1_mix_b_fc1", "L1_mix_w_fc2",
           "L1_mix_b_fc2", "L1_ffn_sW1", "L1_ffn_sb1", "L1_ffn_sW2", "L1_ffn_sb2", "L1_ffn_sW3", "L1_ffn_sb3", "L1_ffn_eW1",
           "L1_ffn_eb1", "L1_ffn_eW2", "L1_ffn_eb2", "L1_ffn_eW3", "L1_ffn_eb3", "L1_ffn_gW", "L1_ffn_gb"]


def kernel(**inputs):
    import numpy as np
    import concourse.bacc as bacc
    from concourse.bass_utils import run_bass_kernel_spmd

    nc = bacc.Bacc("TRN2", target_bir_lowering=False, num_devices=1)
    arrays, aps = {}, {}
    for name in _INPUTS:
        a = np.ascontiguousarray(inputs[name])
        arrays["in_" + name] = a
        aps[name] = nc.dram_tensor("in_" + name, a.shape, mybir.dt.from_np(a.dtype), kind="ExternalInput").ap()
    out = nc.dram_tensor("out_x", (N, D), F32, kind="ExternalOutput").ap()
    build(nc, aps, out)
    return run_bass_kernel_spmd(nc, [arrays], core_ids=[0]).results[0]["out_x"]
```
